# Optimizing a Trainium2 kernel written in Bass

```python
import numpy as np
import jax
import jax.numpy as jnp

def _softmax(x, axis=-1):
    return jax.nn.softmax(x, axis=axis)

def _gelu(x):
    return jax.nn.gelu(x, approximate=True)

def _silu(x):
    return jax.nn.silu(x)

def _sigmoid(x):
    return jax.nn.sigmoid(x)

def _layernorm(x, axis=-1, eps=1e-05):
    m = jnp.mean(x, axis=axis, keepdims=True)
    v = jnp.var(x, axis=axis, keepdims=True)
    return (x - m) / jnp.sqrt(v + eps)

def _scatter_add(tgt, idx, src, axis=0):
    return tgt.at[idx].add(src)

def _segment_sum(src, seg, n):
    return jax.ops.segment_sum(src, seg, n)
kernel_name = 'mk_decoder_preln_d1_seqx_r8_a366cb'

def setup_inputs(seed: int=0):
    np.random.seed(seed)
    _w = jnp.asarray

    def _rec_inputs():
        import jax
        import jax.numpy as jnp
        _rk = jax.random.key(seed)
        x = -0.0003929 + 0.9999 * jax.random.normal(jax.random.fold_in(_rk, 1), (32, 128, 128), jnp.float32)
        _lenS = 128 - jax.random.randint(jax.random.fold_in(_rk, 7), (32,), 0, max(1, 128 // 4) + 1, jnp.int32)
        _lenS2 = 128 - jax.random.randint(jax.random.fold_in(_rk, 8), (32,), 0, max(1, 128 // 4) + 1, jnp.int32)
        _ctx_1024P = jax.random.normal(jax.random.fold_in(_rk, 11), (32, 16, 128), jnp.float32)
        _ctx_1024c = jax.random.dirichlet(jax.random.fold_in(_rk, 511), 0.3 * jnp.ones((16,), jnp.float32), (32, 128))
        _ctx_1024t = jnp.einsum('bsk,bkd->bsd', _ctx_1024c, _ctx_1024P)
        _ctx_1024t = _ctx_1024t * jax.lax.rsqrt(jnp.mean(jnp.square(_ctx_1024t)) + 1e-12) * 0.953939
        ctx_1024 = 2.81802e-05 + 1.00001 * (_ctx_1024t + 0.3 * jax.random.normal(jax.random.fold_in(_rk, 611), (32, 128, 128), jnp.float32))
        return (x, ctx_1024)
    x, ctx_1024 = _rec_inputs()

    def _L0_attn_setup():
        import jax, jax.numpy as jnp
        import numpy as np
        import math
        B, S, E = (2, 256, 128)
        H, DK, DV = (16, 64, 64)

        def _rope(q, k):
            D = q.shape[-1]
            theta = 10000.0 ** (jnp.arange(0, D, 2, dtype=jnp.float32) / D)
            pos = jnp.arange(q.shape[-2], dtype=jnp.float32)
            freqs = pos[:, None] * (1.0 / theta)[None, :]
            emb = jnp.concatenate([freqs, freqs], axis=-1)
            cos = jnp.cos(emb)[None, None]
            sin = jnp.sin(emb)[None, None]

            def rotate(x):
                x1 = x[..., ::2]
                x2 = x[..., 1::2]
                return jnp.stack([-x2, x1], axis=-1).reshape(x.shape)
            return (q * cos + rotate(q) * sin, k * cos + rotate(k) * sin)
        key = jax.random.key(seed)
        ks = jax.random.split(key, 9)
        sE = 1.0 / math.sqrt(E)
        sV = 1.0 / math.sqrt(H * DV)
        return {'x': jax.random.normal(ks[0], (B, S, E), dtype=jnp.float32), 'wq': jax.random.uniform(ks[1], (H * DK, E), jnp.float32, -sE, sE), 'bq': jax.random.uniform(ks[2], (H * DK,), jnp.float32, -sE, sE), 'wk': jax.random.uniform(ks[3], (H * DK, E), jnp.float32, -sE, sE), 'bk': jax.random.uniform(ks[4], (H * DK,), jnp.float32, -sE, sE), 'wv': jax.random.uniform(ks[5], (H * DV, E), jnp.float32, -sE, sE), 'bv': jax.random.uniform(ks[6], (H * DV,), jnp.float32, -sE, sE), 'wo': jax.random.uniform(ks[7], (E, H * DV), jnp.float32, -sV, sV), 'bo': jax.random.uniform(ks[8], (E,), jnp.float32, -sV, sV)}
    _L0_attn_all = _L0_attn_setup()
    _L0_attn_in = {k: v for k, v in _L0_attn_all.items() if k in ('wq', 'bq', 'wk', 'bk', 'wv', 'bv', 'wo', 'bo')}
    del _L0_attn_all

    def _L0_xattn_setup():
        import jax, jax.numpy as jnp
        import numpy as np
        import math
        D_MODEL = 128
        N_HEADS = 16
        C = 1
        B, L = (8, 256)

        def _glorot(key, fan):
            lim = np.sqrt(6.0 / (fan + fan)).astype(np.float32)
            return jax.random.uniform(key, (fan, fan), jnp.float32, -lim, lim)
        key = jax.random.key(seed)
        ks = jax.random.split(key, 7)
        queries = jax.random.normal(ks[0], (B, L, D_MODEL), jnp.float32)
        keys = jax.random.normal(ks[1], (B, L, D_MODEL), jnp.float32)
        values = jax.random.normal(ks[2], (B, L, D_MODEL), jnp.float32)
        wq = _glorot(ks[3], D_MODEL)
        wk = _glorot(ks[4], D_MODEL)
        wv = _glorot(ks[5], D_MODEL)
        wo = _glorot(ks[6], D_MODEL)
        return {'queries': queries, 'keys': keys, 'values': values, 'wq': wq, 'wk': wk, 'wv': wv, 'wo': wo}
    _L0_xattn_all = _L0_xattn_setup()
    _L0_xattn_in = {k: v for k, v in _L0_xattn_all.items() if k in ('wq', 'wk', 'wv', 'wo')}
    del _L0_xattn_all

    def _L0_ffn_setup():
        import jax, jax.numpy as jnp
        import numpy as np
        D_MODEL = 128
        HIDDEN = 256
        E_ROUTED = 14
        E_SHARED = 2
        TOP_K = 2
        EPS = 1e-09
        RMS_EPS = 1.1920929e-07

        def _ffn(xn, rw, W1, W2):
            ms = jnp.mean(xn * xn, axis=-1, keepdims=True)
            h = xn * jax.lax.rsqrt(ms + RMS_EPS) * rw
            return jax.nn.silu(h @ W1) @ W2
        key = jax.random.key(seed)
        ks = jax.random.split(key, 9)
        B, T = (2, 128)
        x = jax.random.normal(ks[0], (B, T, D_MODEL), dtype=jnp.float32)
        router_w = jax.random.normal(ks[1], (D_MODEL, E_ROUTED), dtype=jnp.float32) * 0.006
        rms_w = jnp.ones((E_ROUTED, D_MODEL), dtype=jnp.float32)
        w1 = jax.random.normal(ks[2], (E_ROUTED, D_MODEL, HIDDEN), dtype=jnp.float32) * 0.02
        w2 = jax.random.normal(ks[3], (E_ROUTED, HIDDEN, D_MODEL), dtype=jnp.float32) * 0.02
        rms_w_s = jnp.ones((E_SHARED, D_MODEL), dtype=jnp.float32)
        w1_s = jax.random.normal(ks[4], (E_SHARED, D_MODEL, HIDDEN), dtype=jnp.float32) * 0.02
        w2_s = jax.random.normal(ks[5], (E_SHARED, HIDDEN, D_MODEL), dtype=jnp.float32) * 0.02
        return {'x': x, 'router_w': router_w, 'rms_w': rms_w, 'w1': w1, 'w2': w2, 'rms_w_s': rms_w_s, 'w1_s': w1_s, 'w2_s': w2_s}
    _L0_ffn_all = _L0_ffn_setup()
    _L0_ffn_in = {k: v for k, v in _L0_ffn_all.items() if k in ('router_w', 'rms_w', 'w1', 'w2', 'rms_w_s', 'w1_s', 'w2_s')}
    del _L0_ffn_all
    return {'x': x, 'ctx_1024': ctx_1024, 'L0_attn_wq': _L0_attn_in['wq'], 'L0_attn_bq': _L0_attn_in['bq'], 'L0_attn_wk': _L0_attn_in['wk'], 'L0_attn_bk': _L0_attn_in['bk'], 'L0_attn_wv': _L0_attn_in['wv'], 'L0_attn_bv': _L0_attn_in['bv'], 'L0_attn_wo': _L0_attn_in['wo'], 'L0_attn_bo': _L0_attn_in['bo'], 'L0_xattn_wq': _L0_xattn_in['wq'], 'L0_xattn_wk': _L0_xattn_in['wk'], 'L0_xattn_wv': _L0_xattn_in['wv'], 'L0_xattn_wo': _L0_xattn_in['wo'], 'L0_ffn_router_w': _L0_ffn_in['router_w'], 'L0_ffn_rms_w': _L0_ffn_in['rms_w'], 'L0_ffn_w1': _L0_ffn_in['w1'], 'L0_ffn_w2': _L0_ffn_in['w2'], 'L0_ffn_rms_w_s': _L0_ffn_in['rms_w_s'], 'L0_ffn_w1_s': _L0_ffn_in['w1_s'], 'L0_ffn_w2_s': _L0_ffn_in['w2_s']}

def reference(x, ctx_1024, L0_attn_wq, L0_attn_bq, L0_attn_wk, L0_attn_bk, L0_attn_wv, L0_attn_bv, L0_attn_wo, L0_attn_bo, L0_xattn_wq, L0_xattn_wk, L0_xattn_wv, L0_xattn_wo, L0_ffn_router_w, L0_ffn_rms_w, L0_ffn_w1, L0_ffn_w2, L0_ffn_rms_w_s, L0_ffn_w1_s, L0_ffn_w2_s):
    import jax
    import jax.numpy as jnp

    def _L0_attn_ref(x, wq, bq, wk, bk, wv, bv, wo, bo):
        import jax, jax.numpy as jnp
        import numpy as np
        import math
        B, S, E = (2, 256, 128)
        H, DK, DV = (16, 64, 64)

        def _rope(q, k):
            D = q.shape[-1]
            theta = 10000.0 ** (jnp.arange(0, D, 2, dtype=jnp.float32) / D)
            pos = jnp.arange(q.shape[-2], dtype=jnp.float32)
            freqs = pos[:, None] * (1.0 / theta)[None, :]
            emb = jnp.concatenate([freqs, freqs], axis=-1)
            cos = jnp.cos(emb)[None, None]
            sin = jnp.sin(emb)[None, None]

            def rotate(x):
                x1 = x[..., ::2]
                x2 = x[..., 1::2]
                return jnp.stack([-x2, x1], axis=-1).reshape(x.shape)
            return (q * cos + rotate(q) * sin, k * cos + rotate(k) * sin)
        Bx, Sx, Ex = x.shape
        q = (x @ wq.T + bq).reshape(Bx, Sx, H, DK).transpose(0, 2, 1, 3)
        k = (x @ wk.T + bk).reshape(Bx, Sx, H, DK).transpose(0, 2, 1, 3)
        v = (x @ wv.T + bv).reshape(Bx, Sx, H, DV).transpose(0, 2, 1, 3)
        q, k = _rope(q, k)
        scores = jnp.einsum('bhqd,bhkd->bhqk', q, k)
        causal = jnp.triu(jnp.ones((Sx, Sx), dtype=bool), k=1)
        scores = jnp.where(causal[None, None], -jnp.inf, scores)
        attn = jax.nn.softmax(scores / math.sqrt(DK), axis=-1)
        out = jnp.einsum('bhqk,bhkd->bhqd', attn, v)
        out = out.transpose(0, 2, 1, 3).reshape(Bx, Sx, H * DV)
        return out @ wo.T + bo

    def _L0_xattn_ref(queries, keys, values, wq, wk, wv, wo):
        import jax, jax.numpy as jnp
        import numpy as np
        import math
        D_MODEL = 128
        N_HEADS = 16
        C = 1
        B, L = (8, 256)

        def _glorot(key, fan):
            lim = np.sqrt(6.0 / (fan + fan)).astype(np.float32)
            return jax.random.uniform(key, (fan, fan), jnp.float32, -lim, lim)
        Bv, Lv, _ = queries.shape
        H = N_HEADS
        Dh = D_MODEL // N_HEADS
        Q = (queries @ wq).reshape(Bv, Lv, H, Dh).transpose(0, 2, 3, 1)
        K = (keys @ wk).reshape(Bv, Lv, H, Dh).transpose(0, 2, 3, 1)
        V = (values @ wv).reshape(Bv, Lv, H, Dh).transpose(0, 2, 3, 1)
        corr = jnp.fft.irfft(jnp.fft.rfft(Q, axis=-1) * jnp.conj(jnp.fft.rfft(K, axis=-1)), n=Lv, axis=-1)
        k_top = int(math.floor(C * math.log(Lv)))
        top_vals, top_idx = jax.lax.top_k(corr, k_top)
        w = jax.nn.softmax(top_vals, axis=-1)
        t = jnp.arange(Dh)
        out = jnp.zeros_like(V)
        for i in range(k_top):
            gather_idx = (t[None, None, :] - top_idx[..., i]) % Dh
            rolled = jnp.take_along_axis(V, gather_idx[..., None], axis=2)
            out = out + w[..., i, None] * rolled
        out = out.transpose(0, 2, 1, 3).reshape(Bv, Lv, D_MODEL)
        return out @ wo

    def _L0_ffn_ref(x, router_w, rms_w, w1, w2, rms_w_s, w1_s, w2_s):
        import jax, jax.numpy as jnp
        import numpy as np
        D_MODEL = 128
        HIDDEN = 256
        E_ROUTED = 14
        E_SHARED = 2
        TOP_K = 2
        EPS = 1e-09
        RMS_EPS = 1.1920929e-07

        def _ffn(xn, rw, W1, W2):
            ms = jnp.mean(xn * xn, axis=-1, keepdims=True)
            h = xn * jax.lax.rsqrt(ms + RMS_EPS) * rw
            return jax.nn.silu(h @ W1) @ W2
        B, T, D = x.shape
        N = B * T
        xf = x.reshape(N, D)
        gates = jax.nn.softmax(xf @ router_w, axis=-1)
        top_v, top_i = jax.lax.top_k(gates, TOP_K)
        masked = jnp.zeros_like(gates).at[jnp.arange(N)[:, None], top_i].set(top_v)
        masked = masked / (masked.sum(axis=-1, keepdims=True) + EPS)
        routed = jax.vmap(lambda rw_, W1_, W2_: _ffn(xf, rw_, W1_, W2_))(rms_w, w1, w2)
        routed_out = jnp.einsum('end,ne->nd', routed, masked)
        shared = jax.vmap(lambda rw_, W1_, W2_: _ffn(xf, rw_, W1_, W2_))(rms_w_s, w1_s, w2_s).sum(0)
        return (routed_out + shared).reshape(B, T, D)
    x = x + _L0_attn_ref(_layernorm(x, axis=-1), L0_attn_wq, L0_attn_bq, L0_attn_wk, L0_attn_bk, L0_attn_wv, L0_attn_bv, L0_attn_wo, L0_attn_bo)
    x = x + _L0_xattn_ref(_layernorm(x, axis=-1), ctx_1024, ctx_1024, L0_xattn_wq, L0_xattn_wk, L0_xattn_wv, L0_xattn_wo)
    x = x + _L0_ffn_ref(_layernorm(x, axis=-1), L0_ffn_router_w, L0_ffn_rms_w, L0_ffn_w1, L0_ffn_w2, L0_ffn_rms_w_s, L0_ffn_w1_s, L0_ffn_w2_s)
    return x

_drawn_inputs = setup_inputs


def setup_inputs(seed=0):
    import zlib

    import numpy as np

    out = dict(_drawn_inputs(seed))
    spreads = {'L0_ffn_rms_w': (1.0, 0.6), 'L0_ffn_rms_w_s': (1.0, 0.6)}
    factors = {'L0_attn_bq': 8.0,
     'L0_attn_bk': 8.0,
     'L0_attn_bo': 3.731,
     'L0_ffn_router_w': 2.95,
     'L0_ffn_w1': 2.752,
     'L0_ffn_w2': 2.736}
    for name, (base, spread) in spreads.items():
        noise = np.random.default_rng([zlib.crc32(name.encode()), seed]).standard_normal(out[name].shape)
        drawn = base * np.exp(spread * noise) if base else spread * noise
        out[name] = jnp.asarray(drawn.astype(out[name].dtype))
    for name, factor in factors.items():
        out[name] = (out[name] * factor).astype(out[name].dtype)
    return out
```

```python
from contextlib import ExitStack

import concourse.bass as bass
from concourse import mybir

ALU = mybir.AluOpType
ACT = mybir.ActivationFunctionType
AX_X = mybir.AxisListType.X
F32 = mybir.dt.float32
BF16 = mybir.dt.bfloat16
U32 = mybir.dt.uint32

P = 128
B = 32
T = 128
E = 128
H = 16
DK = 64
HPU = H // 2
FU = HPU * DK
CU = FU // P
UNITS = 2 * B
BANK = 512
LN_EPS = 1e-5
MASKED = -1e30
DH = E // H
TOP = 4
G = 4
GROUPS = B // G
GT = G * T
HID = 256
CH = HID // P
ROUTED, SHARED = 14, 2
EXPERTS = ROUTED + SHARED
RMS_EPS = 1.1920929e-07
GATE_EPS = 1e-9
RP = 16


class Slot:

    def __init__(self, base, i=None):
        self.base, self.i, self.parity = base, i, base % 2

    def count(self, d):
        return self.base + d if self.i is None else self.base + d + 2 * self.i

    def at_least(self, d):
        return self.base + d > 0

    def has(self, lag):
        return self.i is not None or 0 <= self.base - lag < UNITS

    def seq(self, lag):
        return (self.base - lag) // 2 + (0 if self.i is None else self.i)


def for_slots(engine, step):
    for s in range(4):
        step(Slot(s))
    with engine.Fori(0, (UNITS - 6) // 2) as i:
        step(Slot(4, i))
        step(Slot(5, i))
    for s in range(UNITS - 2, UNITS + 3):
        step(Slot(s))


class Group:

    def __init__(self, base, i=None):
        self.base, self.i = base, i

    def count(self, d):
        return self.base + d if self.i is None else self.base + d + self.i

    def at_least(self, d):
        return self.base + d > 0

    def has(self, lag):
        return self.i is not None or 0 <= self.base - lag < GROUPS

    def tokens(self, lag):
        return bass.ds(self.count(-lag) * G * E, G * E)


def for_groups(engine, step):
    for s in range(3):
        step(Group(s))
    with engine.Fori(0, GROUPS - 4) as i:
        step(Group(3, i))
    for s in range(GROUPS - 1, GROUPS + 2):
        step(Group(s))


def decoder_layer(nc, x, ctx_in, wqT, wkT, wvT, woT, bq, bk, bv, bo, xwq, xwk, xwv, xwo,
                  router, rms_w, w1, w2, consts, out):
    with ExitStack() as ctx:
        def sb(name, shape, dt=F32):
            return ctx.enter_context(nc.sbuf_tensor(name, shape, dt))

        def sem(name):
            return ctx.enter_context(nc.semaphore(name))

        banks = ctx.enter_context(nc.psum_tensor("banks", [P, 8 * BANK], F32))

        def bank(b, n=1, lo=0, hi=None):
            return banks[:, b * BANK + lo:(b + n - 1) * BANK + (BANK if hi is None else hi)]

        xs = sb("xs", [P, B * E])
        cst = sb("cst", [P, 4 * P])
        ident = cst[:, 0:128]
        mask_f = cst[:, 128:256]
        cos_c = cst[:, 256:384].rearrange("p (a d) -> p a d", a=2)
        sin_c = cst[:, 384:512].rearrange("p (a d) -> p a d", a=2)
        bn = sb("bn", [P, B, 6])
        mean = sb("mean", [P, B])
        rstd = sb("rstd", [P, B])
        tmp_m = sb("tmp_m", [P, B])
        tmp_v = sb("tmp_v", [P, B])

        wq_sb, wk_sb, wv_sb = sb("wq_sb", [P, H * DK]), sb("wk_sb", [P, H * DK]), sb("wv_sb", [P, H * DK])
        wo_sb = sb("wo_sb", [P, H * DK // P, E])
        bias3 = sb("bias3", [3, 2, H * DK], BF16)
        part_sel = sb("part_sel", [3, 3])
        ones3 = sb("ones3", [3, P], BF16)
        ident_h = sb("ident_h", [P, P], BF16)
        mask_h = sb("mask_h", [P, 4, P], BF16)
        cos_sb = sb("cos_sb", [P, 2, HPU, DK])
        sin_sb = sb("sin_sb", [P, 2, HPU, DK])
        bv_col = sb("bv_col", [P, H * DK // P])
        bv_rep = sb("bv_rep", [P, H * DK // P, P])
        out_bias = sb("out_bias", [P, E])
        xn = sb("xn", [P, E])
        xnT = sb("xnT", [P, T])
        rope_c = sb("rope_c", [P, 2 * FU])
        rope_s = sb("rope_s", [P, 2 * FU])
        qk = sb("qk", [P, 2 * FU])
        qkT = sb("qkT", [P, 2, CU, T])
        v = sb("v", [P, 2, FU])
        negmax = sb("negmax", [P, HPU])
        probs = sb("probs", [P, HPU, T])
        probsT = sb("probsT", [P, HPU, T])
        sums = sb("sums", [P, 2, HPU])
        rsums = sb("rsums", [P, HPU])
        o = sb("o", [P, FU])
        oT = sb("oT", [P, CU, T])

        dft = sb("dft", [P, 2 * P])
        dft_fwd, dft_inv = dft[:, 0:P], dft[:, P:2 * P]
        same_head = sb("same_head", [P, P])
        pos_c = sb("pos_c", [P, 1 + 2 * RP])
        head_pos, iota8, iota14 = pos_c[:, 0:1], pos_c[:, 1:1 + DH], pos_c[:, 1 + RP:1 + RP + ROUTED]
        xw = sb("xw", [P, 4, E])
        cs = sb("cs", [P, B * E])
        ctx_a, ctx_b = sb("ctx_a", [P, G * E]), sb("ctx_b", [P, G * E])
        xn4 = sb("xn4", [P, G * E])
        freq = sb("freq", [P, 2, GT])
        khat = sb("khat", [P, GT])
        spec = sb("spec", [P, GT])
        cross_a, cross_b = sb("cross_a", [P, G, DK - 1]), sb("cross_b", [P, G, DK - 1])
        specT = sb("specT", [P, GT])
        top_v, top_i = sb("top_v", [P, G, 8]), sb("top_i", [P, G, 8], U32)
        top_e, top_s, top_r = sb("top_e", [P, G, TOP]), sb("top_s", [P, G]), sb("top_r", [P, G])
        lag_n, lag_m = sb("lag_n", [P, G, TOP], U32), sb("lag_m", [P, G, TOP], U32)
        wait_pad = sb("wait_pad", [P, 1])
        onehot = sb("onehot", [P, G * TOP, DH])
        mix_row = sb("mix_row", [P, G, DH])
        mix = sb("mix", [P, G, DH, H])
        ctx_o = sb("ctx_o", [P, G * E])
        val_o = sb("val_o", [P, G * E])
        mixT = sb("mixT", [P, GT])

        w1_sb, w2_sb = sb("w1_sb", [P, EXPERTS, HID]), sb("w2_sb", [P, EXPERTS, CH, E])
        bias_f = w1_sb[0:3].rearrange("p n h -> p (n h)")[:, 0:2 * H * DK].rearrange("p (a f) -> p a f", a=2)
        bias_h = w2_sb[0:3].rearrange("p n c e -> p (n c e)").bitcast(BF16)[:, 0:6 * H * DK]\
            .rearrange("p (k a f) -> p k a f", k=3, a=2)
        rmsT = sb("rmsT", [P, EXPERTS])
        router_sb = sb("router_sb", [P, ROUTED])
        rms, scale3 = sb("rms", [P, B]), sb("scale3", [P, B])
        xr = sb("xr", [P, 2, E])
        xrT = cs
        gates = sb("gates", [P, B, ROUTED])
        pick = sb("pick", [P, B, ROUTED])
        best_v, best_i = sb("best_v", [P, B, 8]), sb("best_i", [P, B, 8], U32)
        best_n = sb("best_n", [P, B, 2])
        row_max, row_sum = sb("row_max", [P, B]), sb("row_sum", [P, B])
        hT = sb("hT", [P, 2, CH, GT])

        x_consts, ctx_loaded, e_loaded = sem("x_consts"), sem("ctx_loaded"), sem("e_loaded")
        ctx_a_ready, ctx_b_ready = sem("ctx_a_ready"), sem("ctx_b_ready")
        stats2, stats3 = sem("stats2"), sem("stats3")
        var2_ready, std2_ready, xn4_ready = sem("var2_ready"), sem("std2_ready"), sem("xn4_ready")
        freq_made, freq_ready = sem("freq_made"), sem("freq_ready")
        hats_made, khat_ready, spec_ready = sem("hats_made"), sem("khat_ready"), sem("spec_ready")
        spec_turned, specT_ready = sem("spec_turned"), sem("specT_ready")
        corr_made, shifted, top_exp = sem("corr_made"), sem("shifted"), sem("top_exp")
        mix_ready, ctx_o_made, ctx_o_ready = sem("mix_ready"), sem("ctx_o_made"), sem("ctx_o_ready")
        val_o_made, val_o_ready = sem("val_o_made"), sem("val_o_ready")
        mix_turned, mixT_ready = sem("mix_turned"), sem("mixT_ready")
        tops, mixed, spec_step = sem("tops"), sem("mixed"), sem("spec_step")
        crossed, residual2 = sem("crossed"), sem("residual2")
        var3_ready, std3_ready, ms_ready, rms_ready = sem("var3_ready"), sem("std3_ready"), sem("ms_ready"), sem("rms_ready")
        w1_ready, xr_ready, xr_turned, xrT_ready = sem("w1_ready"), sem("xr_ready"), sem("xr_turned"), sem("xrT_ready")
        routed, logits_shifted, gates_exp, gates_ready = sem("routed"), sem("logits_shifted"), sem("gates_exp"), sem("gates_ready")
        hidden_made, hidden_ready = sem("hidden_made"), sem("hidden_ready")
        expert_made, expert_added = sem("expert_made"), sem("expert_added")
        x_loaded, w_loaded, c_loaded = sem("x_loaded"), sem("w_loaded"), sem("c_loaded")
        tables_ready, bias_ready = sem("tables_ready"), sem("bias_ready")
        dve_step = sem("dve_step")
        var_ready, std_ready, rstd_ready = sem("var_ready"), sem("std_ready"), sem("rstd_ready")
        bv_product, out_bias_ready, x_biased = sem("bv_product"), sem("out_bias_ready"), sem("x_biased")
        bv_ready = sem("bv_ready")
        xn_ready, xn_turned, xnT_ready = sem("xn_ready"), sem("xn_turned"), sem("xnT_ready")
        qk_projected, rope_parts, rope_done = sem("qk_projected"), sem("rope_parts"), sem("rope_done")
        qk_turned, qkT_ready = sem("qk_turned"), sem("qkT_ready")
        scored, max_ready, exp_done = sem("scored"), sem("max_ready"), sem("exp_done")
        probs_turned, probsT_ready = sem("probs_turned"), sem("probsT_ready")
        v_projected, v_ready = sem("v_projected"), sem("v_ready")
        o_summed, rsum_ready, o_ready = sem("o_summed"), sem("rsum_ready"), sem("o_ready")
        o_turned, oT_ready = sem("o_turned"), sem("oT_ready")
        projected, residual = sem("projected"), sem("residual")
        stored = sem("stored")

        QK_BANK, T_BANK, S_BANK, V_BANK, O_BANK = 0, 2, 4, 6, 7
        X_PIECES = 4

        block = ctx.enter_context(nc.Block())

        @block.sync
        def _(sp):
            sp.dma_start(cst[:], consts[:, 0:4 * P]).then_inc(c_loaded, 16)
            for n in range(X_PIECES):
                k = B // X_PIECES
                sp.dma_start(xs[:, n * k * E:(n + 1) * k * E].rearrange("t (b e) -> t b e", b=k),
                             x[n * k:(n + 1) * k].rearrange("b t e -> t b e")).then_inc(x_loaded, 16)
            sp.dma_start(dft[:], consts[:, 5 * P:7 * P]).then_inc(x_consts, 16)
            sp.dma_start(same_head[:], consts[:, 7 * P:8 * P]).then_inc(x_consts, 16)
            sp.dma_start(pos_c[:], consts[:, 8 * P:8 * P + 1 + 2 * RP]).then_inc(x_consts, 16)
            for n, w in enumerate((xwq, xwk, xwv, xwo)):
                sp.dma_start(xw[:, n, :], w).then_inc(x_consts, 16)
            sp.dma_start(cs[:].rearrange("t (b e) -> t b e", b=B), ctx_in.rearrange("b t e -> t b e")).then_inc(ctx_loaded, 16)
            sp.wait_ge(bias_ready, 1)
            sp.dma_start(w1_sb[:], w1.rearrange("n e h -> e n h")).then_inc(e_loaded, 16)
            sp.dma_start(w2_sb[:], w2.rearrange("n (c p) e -> p n c e", p=P)).then_inc(e_loaded, 16)
            with nc.allow_non_contiguous_dma(reason="one weight per partition and expert"):
                sp.dma_start(rmsT[:], rms_w.rearrange("n e -> e n")).then_inc(e_loaded, 16)
            sp.dma_start(router_sb[:], router).then_inc(e_loaded, 16)
            for g in range(GROUPS):
                sp.wait_ge(expert_added, (g + 1) * (ROUTED + 1))
                sp.dma_start(out[g * G:(g + 1) * G].rearrange("b t e -> t b e"),
                             xs[:, g * G * E:(g + 1) * G * E].rearrange("t (b e) -> t b e", b=G)).then_inc(stored, 16)
            sp.wait_ge(stored, 16 * GROUPS)

        @block.gpsimd
        def _(pool):
            pool.wait_ge(c_loaded, 16)
            nc.gpsimd.tensor_copy(ident_h[:], ident).then_inc(tables_ready, 1)
            nc.gpsimd.tensor_copy(mask_h[:], mask_f.unsqueeze(1).broadcast_to([P, 4, P])).then_inc(tables_ready, 1)
            for a in range(2):
                nc.gpsimd.tensor_copy(cos_sb[:, a], cos_c[:, a].unsqueeze(1).broadcast_to([P, HPU, DK]))\
                    .then_inc(tables_ready, 1)
                nc.gpsimd.tensor_copy(sin_sb[:, a], sin_c[:, a].unsqueeze(1).broadcast_to([P, HPU, DK]))\
                    .then_inc(tables_ready, 1)

            def step(s):
                if s.has(0):
                    if s.parity == 0:
                        pool.wait_ge(xn_ready, s.seq(0) + 1)
                        if s.i is None and s.base == 0:
                            pool.wait_ge(out_bias_ready, 1)
                        xb = xs[:, bass.ds(s.seq(0) * E, E)]
                        nc.gpsimd.tensor_tensor(xb, xb, out_bias[:], ALU.add).then_inc(x_biased, 1)
                    pool.wait_ge(rope_parts, s.count(1))
                    nc.gpsimd.tensor_tensor(qk[:], rope_c[:], rope_s[:], ALU.add).then_inc(rope_done, 1)

            for_slots(pool, step)

            pool.wait_ge(ctx_loaded, 16)

            def copies(s):
                if s.has(0):
                    if s.at_least(0):
                        pool.wait_ge(freq_made, s.count(0))
                    nc.gpsimd.tensor_copy(ctx_a[:], cs[:, s.tokens(0)]).then_inc(ctx_a_ready, 1)
                if s.has(2):
                    if s.at_least(-2):
                        pool.wait_ge(ctx_o_made, s.count(-2))
                    nc.gpsimd.tensor_copy(ctx_b[:], cs[:, s.tokens(2)]).then_inc(ctx_b_ready, 1)

            for_groups(pool, copies)

        @block.scalar
        def _(act):
            for n, (dst, src) in enumerate((
                    (wq_sb[:], wqT), (wk_sb[:], wkT), (wv_sb[:], wvT),
                    (wo_sb[:], woT.rearrange("(c p) o -> p c o", p=P)))):
                act.dma_start(dst, src).then_inc(w_loaded, 16)
            act.dma_start(bias_f[:, 0, :], bq.unsqueeze(0).broadcast_to([3, H * DK])).then_inc(w_loaded, 16)
            act.dma_start(bias_f[:, 1, :], bk.unsqueeze(0).broadcast_to([3, H * DK])).then_inc(w_loaded, 16)
            act.dma_start(part_sel[:], consts[0:3, 4 * P:4 * P + 3]).then_inc(w_loaded, 16)
            act.dma_start(out_bias[:], bo.unsqueeze(0).broadcast_to([P, E])).then_inc(w_loaded, 16)
            with nc.allow_non_contiguous_dma(reason="one bias value per partition"):
                act.dma_start(bv_col[:], bv.rearrange("(c p) -> p c", p=P)).then_inc(w_loaded, 16)
            act.wait_ge(var_ready, 1)
            nc.scalar.activation(tmp_v[:], tmp_v[:], ACT.Sqrt).then_inc(std_ready, 1)

            def step(s):
                if s.has(1):
                    act.wait_ge(qk_turned, s.count(0))
                    nc.scalar.activation(qkT[:].rearrange("p a c t -> p (a c t)"), bank(T_BANK, 2), ACT.Copy)\
                        .then_inc(qkT_ready, 1)
                if s.has(3):
                    act.wait_ge(o_turned, s.count(-2))
                    nc.scalar.activation(oT[:].rearrange("p c t -> p (c t)"), bank(V_BANK), ACT.Copy)\
                        .then_inc(oT_ready, 1)
                if s.has(2):
                    act.wait_ge(probs_turned, s.count(-1))
                    nc.scalar.activation(probsT[:].rearrange("p h t -> p (h t)"), bank(T_BANK, 2), ACT.Copy)\
                        .then_inc(probsT_ready, 1)
                if s.has(1):
                    act.wait_ge(max_ready, s.count(0))
                    for h in range(HPU):
                        nc.scalar.activation(probs[:, h, :], bank(S_BANK, 2)[:, h * T:(h + 1) * T], ACT.Exp,
                                             bias=negmax[:, h:h + 1], accum_out=sums[:, 1 - s.parity, h:h + 1])\
                            .then_inc(exp_done, 1)

            for_slots(act, step)

            act.wait_ge(var2_ready, 1)
            nc.scalar.activation(tmp_v[:], tmp_v[:], ACT.Sqrt).then_inc(std2_ready, 1)

            def correlate(s):
                if s.has(0):
                    act.wait_ge(freq_made, s.count(1))
                    nc.scalar.activation(freq[:].rearrange("p a t -> p (a t)"), bank(0, 2), ACT.Copy).then_inc(freq_ready, 1)
                if s.has(1):
                    act.wait_ge(spec_turned, s.count(0))
                    nc.scalar.activation(specT[:], bank(4), ACT.Copy).then_inc(specT_ready, 1)
                if s.has(0):
                    act.wait_ge(hats_made, s.count(1))
                    nc.scalar.activation(khat[:], bank(3), ACT.Copy).then_inc(khat_ready, 1)
                if s.has(2):
                    act.wait_ge(ctx_o_made, s.count(-1))
                    nc.scalar.activation(ctx_o[:], bank(6), ACT.Copy).then_inc(ctx_o_ready, 1)
                    act.wait_ge(mix_turned, s.count(-1))
                    nc.scalar.activation(mixT[:], bank(4), ACT.Copy).then_inc(mixT_ready, 1)
                    act.wait_ge(val_o_made, s.count(-1))
                    nc.scalar.activation(val_o[:], bank(7), ACT.Copy).then_inc(val_o_ready, 1)
                if s.has(1):
                    act.wait_ge(shifted, s.count(0))
                    nc.scalar.activation(top_e[:], top_e[:], ACT.Exp).then_inc(top_exp, 1)

            for_groups(act, correlate)

            act.wait_ge(var3_ready, 1)
            nc.scalar.activation(tmp_v[:], tmp_v[:], ACT.Sqrt).then_inc(std3_ready, 1)
            act.wait_ge(ms_ready, 1)
            nc.scalar.activation(rms[:], rms[:], ACT.Sqrt).then_inc(rms_ready, 1)
            with act.Fori(0, B // 2) as i:
                act.wait_ge(xr_turned, 2 * i + 2)
                nc.scalar.activation(xrT[:, bass.ds(i * 2 * T, 2 * T)], bank(0)[:, 0:2 * T], ACT.Copy).then_inc(xrT_ready, 1)
            act.wait_ge(logits_shifted, 1)
            nc.scalar.activation(gates[:], gates[:], ACT.Exp).then_inc(gates_exp, 1)

            with act.Fori(0, GROUPS) as g:
                for n in range(EXPERTS):
                    for c in range(CH):
                        act.wait_ge(hidden_made, g * (EXPERTS * CH) + n * CH + c + 1)
                        nc.scalar.activation(hT[:, n % 2, c, :], bank(2 * (n % 2) + c), ACT.Silu).then_inc(hidden_ready, 1)

        @block.vector
        def _(dve):
            steps = [0]

            def then(ins):
                steps[0] += 1
                ins.then_inc(dve_step, 1)
                dve.wait_ge(dve_step, steps[0])

            def moments():
                even, odd = bn[:, :, 1], bn[:, :, 4]
                then(nc.vector.tensor_tensor(mean[:], even, odd, ALU.add))
                then(nc.vector.tensor_scalar(mean[:], mean[:], 0.5, None, ALU.mult))
                then(nc.vector.tensor_tensor(tmp_m[:], even, odd, ALU.subtract))
                then(nc.vector.tensor_tensor(tmp_m[:], tmp_m[:], tmp_m[:], ALU.mult))
                then(nc.vector.tensor_tensor(tmp_v[:], bn[:, :, 2], bn[:, :, 5], ALU.add))
                then(nc.vector.tensor_scalar(tmp_v[:], tmp_v[:], 1.0 / E, None, ALU.mult))
                then(nc.vector.scalar_tensor_tensor(tmp_v[:], tmp_m[:], 0.25, tmp_v[:], ALU.mult, ALU.add))

            dve.wait_ge(x_loaded, 16 * X_PIECES)
            with dve.Fori(0, B) as b:
                nc.vector.bn_stats(bn[:, bass.ds(b, 1), :].rearrange("p a s -> p (a s)"), xs[:, bass.ds(b * E, E)])\
                    .then_inc(dve_step, 1)
            steps[0] += B
            dve.wait_ge(dve_step, steps[0])
            moments()
            nc.vector.tensor_scalar(tmp_v[:], tmp_v[:], LN_EPS, None, ALU.add).then_inc(var_ready, 1)
            dve.wait_ge(w_loaded, 16 * 9)
            for n in range(3):
                then(nc.vector.tensor_copy(bias_h[:, n], bias_f))
                if n < 2:
                    then(nc.vector.tensor_tensor(bias_f, bias_f, bias_h[:, n], ALU.subtract))
            then(nc.vector.tensor_scalar(bias3[:], bias_h[:, 0], part_sel[:, 0:1], None, ALU.mult))
            then(nc.vector.scalar_tensor_tensor(bias3[:], bias_h[:, 1], part_sel[:, 1:2], bias3[:],
                                                ALU.mult, ALU.add))
            then(nc.vector.scalar_tensor_tensor(bias3[:], bias_h[:, 2], part_sel[:, 2:3], bias3[:],
                                                ALU.mult, ALU.add))
            nc.vector.memset(ones3[:], 1.0).then_inc(bias_ready, 1)
            dve.wait_ge(std_ready, 1)
            then(nc.vector.reciprocal(rstd[:], tmp_v[:]))

            def normalise(b, n):
                nc.vector.tensor_scalar(xn[:], xs[:, bass.ds(b * E, E)], mean[:, bass.ds(b, 1)],
                                        rstd[:, bass.ds(b, 1)], ALU.subtract, ALU.mult).then_inc(xn_ready, 1)

            normalise(0, 1)
            dve.wait_ge(xn_turned, 1)
            nc.vector.tensor_copy(xnT[:], bank(O_BANK)[:, 128:256]).then_inc(xnT_ready, 1)
            nc.vector.tensor_copy(bv_rep[:], bv_col[:].unsqueeze(2).broadcast_to([P, H * DK // P, P]))\
                .then_inc(bv_ready, 1)
            dve.wait_ge(bv_product, 1)
            nc.vector.tensor_tensor(out_bias[:], out_bias[:], bank(V_BANK)[:, 0:E], ALU.add).then_inc(out_bias_ready, 1)

            def step(s):
                if s.has(0):
                    dve.wait_ge(qk_projected, s.count(1))
                    if s.i is None and s.base == 0:
                        dve.wait_ge(tables_ready, 6)
                    raw = bank(QK_BANK, 2)
                    if s.at_least(0):
                        dve.wait_ge(rope_done, s.count(0))
                    nc.vector.tensor_tensor(rope_c[:], raw, cos_sb[:].rearrange("p a h d -> p (a h d)"), ALU.mult)
                    nc.vector.tensor_tensor(
                        rope_s[:].rearrange("p (f e) -> p f e", e=2), raw.rearrange("p (f e) -> p f e", e=2)[:, :, ::-1],
                        sin_sb[:].rearrange("p a h (f e) -> p (a h f) e", e=2), ALU.mult).then_inc(rope_parts, 1)
                if s.has(1):
                    dve.wait_ge(scored, s.count(0))
                    nc.vector.tensor_reduce(negmax[:], bank(S_BANK, 2).rearrange("p (h k) -> p h k", k=T), AX_X,
                                            ALU.max, negate=True).then_inc(max_ready, 1)
                if s.has(2):
                    dve.wait_ge(exp_done, (s.count(-1)) * HPU)
                    nc.vector.reciprocal(rsums[:], sums[:, s.parity, :]).then_inc(rsum_ready, 1)
                    dve.wait_ge(rsum_ready, s.count(-1))
                    dve.wait_ge(o_summed, s.count(-1))
                    nc.vector.tensor_tensor(
                        o[:].rearrange("p (a b d) -> p a b d", b=2, d=DK),
                        bank(O_BANK).rearrange("p (a b d) -> p a b d", b=2, d=DK),
                        rsums[:].rearrange("p (b a) -> p a b", b=2).unsqueeze(3).broadcast_to([P, HPU // 2, 2, DK]),
                        ALU.mult).then_inc(o_ready, 1)
                if s.has(0):
                    dve.wait_ge(v_projected, s.count(1))
                    nc.vector.tensor_copy(v[:, s.parity, :], bank(V_BANK)).then_inc(v_ready, 1)
                more = s.parity == 1 and (s.i is not None or s.base < UNITS - 1)
                if more:
                    normalise(s.seq(0) + 1, s)
                if s.has(3):
                    dve.wait_ge(x_biased, s.seq(3) + 1)
                    dve.wait_ge(projected, s.count(-2))
                    xb = xs[:, bass.ds(s.seq(3) * E, E)]
                    if s.at_least(-3):
                        dve.wait_ge(residual, s.count(-3))
                    nc.vector.tensor_tensor(xb, xb, bank(O_BANK)[:, 0:E], ALU.add).then_inc(residual, 1)
                    if s.parity == 0:
                        dve.wait_ge(residual, s.count(-2))
                        nc.vector.bn_stats(bn[:, bass.ds(s.seq(3), 1), :].rearrange("p a s -> p (a s)"), xb)\
                            .then_inc(stats2, 1)
                if more:
                    dve.wait_ge(xn_turned, s.seq(0) + 2)
                    nc.vector.tensor_copy(xnT[:], bank(O_BANK)[:, 128:256]).then_inc(xnT_ready, 1)

            for_slots(dve, step)

            dve.wait_ge(stats2, B)
            moments()
            nc.vector.tensor_scalar(tmp_v[:], tmp_v[:], LN_EPS, None, ALU.add).then_inc(var2_ready, 1)
            dve.wait_ge(std2_ready, 1)
            then(nc.vector.reciprocal(rstd[:], tmp_v[:]))

            def normalise4(s, lag):
                for n in range(G):
                    b = s.count(-lag) * G + n
                    nc.vector.tensor_scalar(xn4[:, n * E:(n + 1) * E], xs[:, bass.ds(b * E, E)], mean[:, bass.ds(b, 1)],
                                            rstd[:, bass.ds(b, 1)], ALU.subtract, ALU.mult).then_inc(xn4_ready, 1)

            dve.wait_ge(x_consts, 16 * 7)
            normalise4(Group(0), 0)
            N = DK

            def correlate(s):
                if s.has(1):
                    dve.wait_ge(corr_made, s.count(0))
                    nc.vector.memset(wait_pad[:], 0.0)
                    for n in range(G):
                        nc.vector.max(top_v[:, n, :], bank(5)[:, n * T:(n + 1) * T]).then_inc(tops, 1)
                    dve.wait_ge(tops, s.count(0) * (2 * G) - G)
                    nc.vector.memset(wait_pad[:], 0.0)
                    for n in range(G):
                        nc.vector.max_index(top_i[:, n, :], top_v[:, n, :], bank(5)[:, n * T:(n + 1) * T]).then_inc(tops, 1)
                    nc.vector.tensor_tensor(top_e[:], top_v[:, :, 0:TOP], top_v[:, :, 0:1].broadcast_to([P, G, TOP]),
                                            ALU.subtract).then_inc(shifted, 1)
                if s.has(0):
                    dve.wait_ge(hats_made, s.count(1))
                    dve.wait_ge(khat_ready, s.count(1))
                    if s.at_least(0):
                        dve.wait_ge(spec_turned, s.count(0))
                    q3 = bank(2).rearrange("p (g f) -> p g f", g=G)
                    k3 = khat[:].rearrange("p (g f) -> p g f", g=G)
                    s3 = spec[:].rearrange("p (g f) -> p g f", g=G)
                    re, im = slice(1, N), slice(N + 1, 2 * N)
                    nc.vector.tensor_tensor(spec[:], bank(2), khat[:], ALU.mult).then_inc(spec_step, 1)
                    nc.vector.tensor_tensor(cross_a[:], q3[:, :, im], k3[:, :, re], ALU.mult).then_inc(spec_step, 1)
                    nc.vector.tensor_tensor(cross_b[:], q3[:, :, re], k3[:, :, im], ALU.mult).then_inc(spec_step, 1)
                    dve.wait_ge(spec_step, s.count(0) * 4 + 3)
                    nc.vector.tensor_tensor(s3[:, :, re], s3[:, :, re], s3[:, :, im], ALU.add).then_inc(spec_step, 1)
                    dve.wait_ge(spec_step, s.count(1) * 4)
                    nc.vector.tensor_tensor(s3[:, :, im], cross_a[:], cross_b[:], ALU.subtract).then_inc(spec_ready, 1)
                if s.has(1):
                    k = 8
                    dve.wait_ge(tops, s.count(0) * (2 * G))
                    nc.vector.tensor_scalar(lag_n[:], top_i[:, :, 0:TOP], -1.0, head_pos, ALU.mult, ALU.add).then_inc(mixed, 1)
                    dve.wait_ge(mixed, s.count(-1) * k + 1)
                    nc.vector.tensor_scalar(lag_m[:], lag_n[:], DH - 1, None, ALU.bitwise_and).then_inc(mixed, 1)
                    dve.wait_ge(top_exp, s.count(0))
                    nc.vector.tensor_reduce(top_s[:], top_e[:], AX_X, ALU.add).then_inc(mixed, 1)
                    dve.wait_ge(mixed, s.count(-1) * k + 3)
                    nc.vector.reciprocal(top_r[:], top_s[:]).then_inc(mixed, 1)
                    nc.vector.tensor_tensor(
                        onehot[:], lag_m[:].rearrange("p g l -> p (g l)").unsqueeze(2).broadcast_to([P, G * TOP, DH]),
                        iota8.unsqueeze(1).broadcast_to([P, G * TOP, DH]), ALU.is_equal).then_inc(mixed, 1)
                    dve.wait_ge(mixed, s.count(-1) * k + 5)
                    nc.vector.tensor_tensor(top_e[:], top_e[:], top_r[:].unsqueeze(2).broadcast_to([P, G, TOP]), ALU.mult)\
                        .then_inc(mixed, 1)
                    dve.wait_ge(mixed, s.count(-1) * k + 6)
                    nc.vector.tensor_tensor(
                        onehot[:], onehot[:],
                        top_e[:].rearrange("p g l -> p (g l)").unsqueeze(2).broadcast_to([P, G * TOP, DH]), ALU.mult)\
                        .then_inc(mixed, 1)
                    dve.wait_ge(mixed, s.count(-1) * k + 7)
                    nc.vector.tensor_reduce(mix_row[:], onehot[:].rearrange("p (g l) d -> p g d l", g=G), AX_X, ALU.add)\
                        .then_inc(mixed, 1)
                    dve.wait_ge(mixed, s.count(0) * k)
                    if s.at_least(-1):
                        dve.wait_ge(mix_turned, s.count(-1))
                    nc.vector.tensor_tensor(
                        mix[:], mix_row[:].unsqueeze(3).broadcast_to([P, G, DH, H]),
                        same_head[:].rearrange("p (d h) -> p d h", h=H).unsqueeze(1).broadcast_to([P, G, DH, H]), ALU.mult)\
                        .then_inc(mix_ready, 1)
                if s.has(2):
                    dve.wait_ge(crossed, s.count(-1))
                    xg = xs[:, s.tokens(2)]
                    nc.vector.tensor_tensor(xg, xg, bank(6), ALU.add).then_inc(residual2, 1)
                    dve.wait_ge(residual2, s.count(-1))
                    for n in range(G):
                        b = s.count(-2) * G + n
                        nc.vector.bn_stats(bn[:, bass.ds(b, 1), :].rearrange("p a s -> p (a s)"), xs[:, bass.ds(b * E, E)])\
                            .then_inc(stats3, 1)
                if s.has(-1) and s.base != GROUPS - 1:
                    dve.wait_ge(freq_made, s.count(1))
                    normalise4(s, -1)

            for_groups(dve, correlate)

            dve.wait_ge(stats3, B)
            moments()
            then(nc.vector.tensor_scalar(rstd[:], tmp_v[:], LN_EPS, None, ALU.add))
            then(nc.vector.reciprocal(scale3[:], rstd[:]))
            then(nc.vector.tensor_tensor(rms[:], tmp_v[:], scale3[:], ALU.mult))
            nc.vector.tensor_scalar(rms[:], rms[:], RMS_EPS, None, ALU.add).then_inc(ms_ready, 1)
            nc.vector.tensor_copy(tmp_v[:], rstd[:]).then_inc(var3_ready, 1)
            dve.wait_ge(std3_ready, 1)
            dve.wait_ge(rms_ready, 1)
            then(nc.vector.tensor_tensor(tmp_v[:], tmp_v[:], rms[:], ALU.mult))
            then(nc.vector.reciprocal(scale3[:], tmp_v[:]))
            dve.wait_ge(e_loaded, 16 * 4)
            with dve.Fori(0, B // 2) as i:
                for n in range(2):
                    b = 2 * i + n
                    if n == 0:
                        pass
                    nc.vector.tensor_scalar(xr[:, n, :], xs[:, bass.ds(b * E, E)], mean[:, bass.ds(b, 1)],
                                            scale3[:, bass.ds(b, 1)], ALU.subtract, ALU.mult).then_inc(xr_ready, 1)
                    dve.wait_ge(xr_turned, b + 1)
            for n in range(EXPERTS):
                last = nc.vector.tensor_scalar(w1_sb[:, n, :], w1_sb[:, n, :], rmsT[:, n:n + 1], None, ALU.mult)
            last.then_inc(w1_ready, 1)
            dve.wait_ge(routed, B)
            then(nc.vector.tensor_tensor(gates[:], bank(6).rearrange("p (b n) -> p b n", n=RP)[:, :, 0:ROUTED],
                                         rms[:].unsqueeze(2).broadcast_to([P, B, ROUTED]), ALU.mult))
            then(nc.vector.tensor_reduce(row_max[:], gates[:], AX_X, ALU.max))
            nc.vector.tensor_tensor(gates[:], gates[:], row_max[:].unsqueeze(2).broadcast_to([P, B, ROUTED]),
                                    ALU.subtract).then_inc(logits_shifted, 1)
            dve.wait_ge(gates_exp, 1)
            then(nc.vector.tensor_reduce(row_sum[:], gates[:], AX_X, ALU.add))
            then(nc.vector.reciprocal(row_max[:], row_sum[:]))
            then(nc.vector.tensor_tensor(gates[:], gates[:], row_max[:].unsqueeze(2).broadcast_to([P, B, ROUTED]), ALU.mult))
            for b in range(B):
                last = nc.vector.max(best_v[:, b, :], gates[:, b, :])
            then(last)
            for b in range(B):
                last = nc.vector.max_index(best_i[:, b, :], best_v[:, b, :], gates[:, b, :])
            then(last)
            then(nc.vector.tensor_tensor(row_sum[:], best_v[:, :, 0], best_v[:, :, 1], ALU.add))
            then(nc.vector.tensor_scalar(row_sum[:], row_sum[:], GATE_EPS, None, ALU.add))
            then(nc.vector.reciprocal(row_max[:], row_sum[:]))
            then(nc.vector.tensor_tensor(best_n[:], best_v[:, :, 0:2], row_max[:].unsqueeze(2).broadcast_to([P, B, 2]), ALU.mult))
            for k in range(2):
                dst = gates if k == 0 else pick
                then(nc.vector.tensor_tensor(dst[:], best_i[:, :, k:k + 1].broadcast_to([P, B, ROUTED]),
                                             iota14.unsqueeze(1).broadcast_to([P, B, ROUTED]), ALU.is_equal))
                then(nc.vector.tensor_tensor(dst[:], dst[:], best_n[:, :, k:k + 1].broadcast_to([P, B, ROUTED]), ALU.mult))
            then(nc.vector.tensor_tensor(gates[:], gates[:], pick[:], ALU.add))

            with dve.Fori(0, GROUPS) as g:
                xg = xs[:, bass.ds(g * G * E, G * E)]
                for m in range(ROUTED + 1):
                    dve.wait_ge(expert_made, g * (ROUTED + 1) + m + 1)
                    if m == 0:
                        nc.vector.tensor_tensor(xg, xg, bank(4), ALU.add).then_inc(expert_added, 1)
                        dve.wait_ge(expert_added, g * (ROUTED + 1) + 1)
                        continue
                    for n in range(G):
                        b = g * G + n
                        xb = xs[:, bass.ds(b * E, E)]
                        last = nc.vector.scalar_tensor_tensor(
                            xb, bank(4 + m % 2)[:, n * E:(n + 1) * E],
                            gates[:].rearrange("p b n -> p (b n)")[:, bass.ds(b * ROUTED + m - 1, 1)], xb, ALU.mult, ALU.add)
                    last.then_inc(expert_added, 1)
                    dve.wait_ge(expert_added, g * (ROUTED + 1) + m + 1)

        @block.tensor
        def _(pe):
            def turn(b):
                pe.wait_ge(xn_ready, b + 1)
                nc.tensor.transpose(bank(O_BANK)[:, 128:256], xn[:], ident).then_inc(xn_turned, 1)

            pe.wait_ge(c_loaded, 16)
            turn(0)
            pe.wait_ge(bias_ready, 1)
            pe.wait_ge(w_loaded, 16 * 9)
            pe.wait_ge(tables_ready, 6)
            pe.wait_ge(bv_ready, 1)
            for c in range(H * DK // P):
                last = nc.tensor.matmul(bank(V_BANK)[:, 0:E], bv_rep[:, c, :], wo_sb[:, c, :],
                                        start=(c == 0), stop=(c == H * DK // P - 1))
            last.then_inc(bv_product, 1)
            pe.wait_ge(out_bias_ready, 1)

            def step(s):
                half = slice(s.parity * FU, (s.parity + 1) * FU)
                if s.has(1):
                    pe.wait_ge(rope_done, s.count(0))
                    for n in range(2 * CU):
                        last = nc.tensor.transpose(bank(T_BANK, 2)[:, n * T:(n + 1) * T], qk[:, n * P:(n + 1) * P], ident)
                    last.then_inc(qk_turned, 1)
                if s.has(3):
                    pe.wait_ge(o_ready, s.count(-2))
                    if s.has(1):
                        pe.wait_ge(v_ready, s.count(0))
                    for c in range(CU):
                        last = nc.tensor.transpose(bank(V_BANK)[:, c * T:(c + 1) * T], o[:, c * P:(c + 1) * P], ident)
                    last.then_inc(o_turned, 1)
                if s.has(0):
                    pe.wait_ge(xnT_ready, s.seq(0) + 1)
                    if s.at_least(0):
                        pe.wait_ge(rope_parts, s.count(0))
                    for a, w in enumerate((wq_sb, wk_sb)):
                        nc.tensor.matmul(bank(QK_BANK + a), xnT[:], w[:, half], start=True, stop=False)
                        last = nc.tensor.matmul(bank(QK_BANK + a), ones3[:], bias3[:, a, half], start=False, stop=True)
                    last.then_inc(qk_projected, 1)
                if s.has(2):
                    pe.wait_ge(exp_done, s.count(-1) * HPU)
                    if s.has(1):
                        pe.wait_ge(qkT_ready, s.count(0))
                    for h in range(HPU):
                        last = nc.tensor.transpose(bank(T_BANK, 2)[:, h * T:(h + 1) * T], probs[:, h, :], ident)
                    last.then_inc(probs_turned, 1)
                if s.has(1):
                    pe.wait_ge(qkT_ready, s.count(0))
                    for a in range(2):
                        nc.tensor.matmul(bank(S_BANK + a), ident_h[:], mask_h[:].rearrange("p a k -> p (a k)"),
                                         start=True, stop=True)
                    for c in range(CU):
                        for a in range(2):
                            rows = slice(a * DK, (a + 1) * DK)
                            last = nc.tensor.matmul(bank(S_BANK + a)[:, c * T:(c + 1) * T], qkT[rows, 0, c, :],
                                                    qkT[rows, 1, c, :], start=False, stop=True,
                                                    skip_group_check=True)
                    last.then_inc(scored, 1)
                if s.has(2):
                    pe.wait_ge(probsT_ready, s.count(-1))
                    pe.wait_ge(v_ready, s.count(-1))
                    if s.at_least(-3):
                        pe.wait_ge(residual, s.count(-3))
                    for n in range(HPU):
                        h = 2 * (n % CU) + n // CU
                        last = nc.tensor.matmul(bank(O_BANK)[:, h * DK:(h + 1) * DK], probsT[:, n, :],
                                                v[:, s.parity, h * DK:(h + 1) * DK], start=True, stop=True)
                    last.then_inc(o_summed, 1)
                if s.has(0):
                    if s.at_least(0):
                        pe.wait_ge(v_ready, s.count(0))
                    if s.has(3):
                        pe.wait_ge(oT_ready, s.count(-2))
                    nc.tensor.matmul(bank(V_BANK), xnT[:], wv_sb[:, half], start=True, stop=True)\
                        .then_inc(v_projected, 1)
                if s.parity == 1 and (s.i is not None or s.base < UNITS - 1):
                    pe.wait_ge(o_ready, s.count(-1)) if s.has(2) else None
                    turn(s.seq(0) + 1)
                if s.has(3):
                    pe.wait_ge(oT_ready, s.count(-2))
                    if s.has(2):
                        pe.wait_ge(o_ready, s.count(-1))
                    elif s.at_least(-3):
                        pe.wait_ge(residual, s.count(-3))
                    for c in range(CU):
                        last = nc.tensor.matmul(bank(O_BANK)[:, 0:E], oT[:, c, :], wo_sb[:, (1 - s.parity) * CU + c, :],
                                                start=(c == 0), stop=(c == CU - 1))
                    last.then_inc(projected, 1)

            for_slots(pe, step)

            pe.wait_ge(x_consts, 16 * 7)
            pe.wait_ge(residual, UNITS)

            def correlate(s):
                if s.has(0):
                    pe.wait_ge(ctx_a_ready, s.count(1))
                    pe.wait_ge(xn4_ready, s.count(1) * G)
                    if s.at_least(0):
                        pe.wait_ge(freq_ready, s.count(0))
                    for a, src in enumerate((xn4, ctx_a)):
                        for n in range(G):
                            last = nc.tensor.matmul(bank(a)[:, n * T:(n + 1) * T], src[:, n * E:(n + 1) * E], dft_fwd,
                                                    start=True, stop=True)
                    last.then_inc(freq_made, 1)
                if s.has(1):
                    pe.wait_ge(spec_ready, s.count(0))
                    if s.has(3):
                        pe.wait_ge(mixT_ready, s.count(-2))
                    for n in range(G):
                        last = nc.tensor.transpose(bank(4)[:, n * T:(n + 1) * T], spec[:, n * T:(n + 1) * T], ident)
                    last.then_inc(spec_turned, 1)
                if s.has(0):
                    pe.wait_ge(freq_ready, s.count(1))
                    if s.at_least(0):
                        pe.wait_ge(spec_ready, s.count(0))
                    for a in range(2):
                        last = nc.tensor.matmul(bank(2 + a), xw[:, a, :], freq[:, a, :], start=True, stop=True)
                    last.then_inc(hats_made, 1)
                if s.has(1):
                    pe.wait_ge(specT_ready, s.count(0))
                    if s.at_least(-1):
                        pe.wait_ge(tops, s.count(-1) * (2 * G))
                    for n in range(G):
                        last = nc.tensor.matmul(bank(5)[:, n * T:(n + 1) * T], specT[:, n * T:(n + 1) * T], dft_inv,
                                                start=True, stop=True)
                    last.then_inc(corr_made, 1)
                if s.has(2):
                    pe.wait_ge(ctx_b_ready, s.count(-1))
                    if s.at_least(-2):
                        pe.wait_ge(residual2, s.count(-2))
                    for n in range(G):
                        last = nc.tensor.matmul(bank(6)[:, n * E:(n + 1) * E], ctx_b[:, n * E:(n + 1) * E],
                                                xw[:, 3, :], start=True, stop=True)
                    last.then_inc(ctx_o_made, 1)
                    pe.wait_ge(mix_ready, s.count(-1))
                    pe.wait_ge(specT_ready, s.count(0) if s.has(1) else GROUPS)
                    for n in range(G):
                        last = nc.tensor.transpose(bank(4)[:, n * T:(n + 1) * T],
                                                   mix[:, n].rearrange("p d h -> p (d h)"), ident)
                    last.then_inc(mix_turned, 1)
                    pe.wait_ge(ctx_o_ready, s.count(-1))
                    if s.at_least(-2):
                        pe.wait_ge(val_o_ready, s.count(-2))
                    nc.tensor.matmul(bank(7), xw[:, 2, :], ctx_o[:], start=True, stop=True).then_inc(val_o_made, 1)
                    pe.wait_ge(val_o_ready, s.count(-1))
                    pe.wait_ge(mixT_ready, s.count(-1))
                    for n in range(G):
                        last = nc.tensor.matmul(bank(6)[:, n * E:(n + 1) * E], mixT[:, n * T:(n + 1) * T],
                                                val_o[:, n * E:(n + 1) * E], start=True, stop=True)
                    last.then_inc(crossed, 1)

            for_groups(pe, correlate)

            pe.wait_ge(e_loaded, 16 * 4)
            pe.wait_ge(residual2, GROUPS)
            def turn_xr(i, first):
                for n in range(2):
                    pe.wait_ge(xr_ready, 2 * i + n + 1)
                    if n == 0 and not first:
                        pe.wait_ge(xrT_ready, i)
                    nc.tensor.transpose(bank(0)[:, n * T:(n + 1) * T], xr[:, n, :], ident).then_inc(xr_turned, 1)

            turn_xr(0, True)
            with pe.Fori(1, B // 2) as i:
                turn_xr(i, False)

            pe.wait_ge(xrT_ready, B // 2)
            for b in range(B):
                nc.tensor.matmul(bank(6)[:, b * RP:b * RP + ROUTED], xrT[:, b * T:(b + 1) * T], router_sb[:],
                                 start=True, stop=True).then_inc(routed, 1)
            pe.wait_ge(w1_ready, 1)

            order = list(range(ROUTED, EXPERTS)) + list(range(ROUTED))

            def hidden(g, m):
                n = order[m]
                for c in range(CH):
                    nc.tensor.matmul(bank(2 * (m % 2) + c), w1_sb[:, n, c * P:(c + 1) * P], xrT[:, bass.ds(g * GT, GT)],
                                     start=True, stop=True).then_inc(hidden_made, 1)

            def expert(g, m):
                n = order[m]
                slot = max(m - 1, 0)
                for c in range(CH):
                    pe.wait_ge(hidden_ready, g * (EXPERTS * CH) + m * CH + c + 1)
                for t in range(G):
                    for c in range(CH):
                        last = nc.tensor.matmul(bank(4 + slot % 2)[:, t * E:(t + 1) * E], hT[:, m % 2, c, t * T:(t + 1) * T],
                                                w2_sb[:, n, c, :], start=(c == 0 and (m > 1 or (m == 0 and t == 0))), stop=(c == CH - 1),
                                                skip_group_check=True)
                if m >= 1:
                    last.then_inc(expert_made, 1)

            with pe.Fori(0, GROUPS) as g:
                for m in range(EXPERTS + 1):
                    if m < EXPERTS:
                        hidden(g, m)
                    if m >= 1:
                        k = m - 1
                        if k >= 3:
                            pe.wait_ge(expert_added, g * (ROUTED + 1) + k - 2)
                        expert(g, k)
                pe.wait_ge(expert_added, (g + 1) * (ROUTED + 1))


def _tables(np):
    f = np.float32
    ident = np.eye(P, dtype=f)
    mask = np.triu(np.full((P, P), MASKED, dtype=f), k=1)
    theta = (f(10000.0) ** (np.arange(0, DK, 2, dtype=f) / f(DK))).astype(f)
    freqs = np.arange(T, dtype=f)[:, None] * (f(1.0) / theta)[None, :]
    emb = np.concatenate([freqs, freqs], axis=-1)
    cos, sin = np.cos(emb).astype(f), np.sin(emb).astype(f)
    sin[:, 0::2] = -sin[:, 0::2]
    q_scale = f(DK ** -0.5)
    sel = np.zeros((P, P), dtype=f)
    sel[0:3, 0:3] = np.eye(3)
    t = np.arange(T)
    k_re, k_im = np.arange(T // 2 + 1), np.arange(1, T // 2)
    turn = 2.0 * np.pi / T
    fwd = np.concatenate([np.cos(turn * np.outer(t, k_re) % (2 * np.pi)), -np.sin(turn * (np.outer(t, k_im) % T))], axis=1)
    fwd[:, :T // 2 + 1] = np.cos(turn * (np.outer(t, k_re) % T))
    weight = np.full(T, 2.0 / T)
    weight[0] = weight[T // 2] = 1.0 / T
    inv = fwd.T * weight[:, None]
    row = np.arange(P)
    same = (row[:, None] % H == row[None, :] % H)
    pos = np.zeros((P, P))
    pos[:, 0] = row // H + T
    pos[:, 1:1 + DH] = np.arange(DH)
    pos[:, 1 + RP:1 + RP + ROUTED] = np.arange(ROUTED)
    return np.concatenate([ident, mask, cos * q_scale, cos, sin * q_scale, sin, sel, fwd, inv, same, pos],
                          axis=1).astype(f)


def kernel(**inputs):
    import numpy as np
    import concourse.bacc as bacc
    from concourse.bass_utils import run_bass_kernel_spmd

    layout = {k: np.ascontiguousarray(v) for k, v in inputs.items()}
    for k in ("L0_attn_wq", "L0_attn_wk", "L0_attn_wv", "L0_attn_wo"):
        layout[k] = np.ascontiguousarray(layout[k].T)
    for k in ("L0_xattn_wq", "L0_xattn_wk", "L0_xattn_wv"):
        layout[k] = np.ascontiguousarray(layout[k].reshape(E, H, DH).transpose(0, 2, 1).reshape(E, E))
    layout["consts"] = _tables(np)
    for name, routed, shared in (("rms", "L0_ffn_rms_w", "L0_ffn_rms_w_s"), ("w1", "L0_ffn_w1", "L0_ffn_w1_s"),
                                 ("w2", "L0_ffn_w2", "L0_ffn_w2_s")):
        layout[name] = np.concatenate([layout[routed], layout[shared]], axis=0)
    nc = bacc.Bacc("TRN2", target_bir_lowering=False, num_devices=1)
    names = ["x", "ctx_1024", "L0_attn_wq", "L0_attn_wk", "L0_attn_wv", "L0_attn_wo",
             "L0_attn_bq", "L0_attn_bk", "L0_attn_bv", "L0_attn_bo", "L0_xattn_wq", "L0_xattn_wk", "L0_xattn_wv", "L0_xattn_wo",
             "L0_ffn_router_w", "rms", "w1", "w2", "consts"]
    arrays, args = {}, []
    for name in names:
        a = layout[name]
        arrays[f"in_{name}"] = a
        args.append(nc.dram_tensor(f"in_{name}", a.shape, mybir.dt.from_np(a.dtype), kind="ExternalInput").ap())
    out = nc.dram_tensor("out_x", (B, T, E), F32, kind="ExternalOutput").ap()
    decoder_layer(nc, *args, out)
    r = run_bass_kernel_spmd(nc, [arrays], core_ids=[0])
    return r.results[0]["out_x"]
```

```python
from contextlib import ExitStack

import concourse.bass as bass
from concourse import mybir

ALU = mybir.AluOpType
ACT = mybir.ActivationFunctionType
AX_X = mybir.AxisListType.X
F32 = mybir.dt.float32
BF16 = mybir.dt.bfloat16
F32R = mybir.dt.float32r
U32 = mybir.dt.uint32

P = 128
B = 32
T = 128
E = 128
H = 16
DK = 64
HPU = H // 2
FU = HPU * DK
CU = FU // P
UNITS = 2 * B
BANK = 512
LN_EPS = 1e-5
MASKED = -1e30
DH = E // H
TOP = 4
G = 4
GROUPS = B // G
GT = G * T
HID = 256
CH = HID // P
ROUTED, SHARED = 14, 2
EXPERTS = ROUTED + SHARED
RMS_EPS = 1.1920929e-07
GATE_EPS = 1e-9
RP = 16
TOP_K = 2
HALF = B // 2
TILES = (HALF * T * TOP_K + ROUTED * (P - 1)) // P
BATCH = 3
RING = 3
TURN = BATCH * RING
TURNS = TILES // TURN
assert TILES == TURNS * TURN
ALL_TILES = 2 * TILES
LAG = 4
FIRST_B = TURNS
CHUNKS = HALF // G


class Slot:

    def __init__(self, base, i=None):
        self.base, self.i, self.parity = base, i, base % 2

    def count(self, d):
        return self.base + d if self.i is None else self.base + d + 2 * self.i

    def at_least(self, d):
        return self.base + d > 0

    def has(self, lag):
        return self.i is not None or 0 <= self.base - lag < UNITS

    def seq(self, lag):
        return (self.base - lag) // 2 + (0 if self.i is None else self.i)


def for_slots(engine, step):
    for s in range(4):
        step(Slot(s))
    with engine.Fori(0, (UNITS - 6) // 2) as i:
        step(Slot(4, i))
        step(Slot(5, i))
    for s in range(UNITS - 2, UNITS + 2):
        step(Slot(s))


class Group:

    def __init__(self, base, i=None):
        self.base, self.i = base, i

    def count(self, d):
        return self.base + d if self.i is None else self.base + d + self.i

    def at_least(self, d):
        return self.base + d > 0

    def has(self, lag):
        return self.i is not None or 0 <= self.base - lag < GROUPS

    def tokens(self, lag):
        return bass.ds(self.count(-lag) * G * E, G * E)


def for_groups(engine, step):
    for s in range(3):
        step(Group(s))
    with engine.Fori(0, GROUPS - 4) as i:
        step(Group(3, i))
    for s in range(GROUPS - 1, GROUPS + 3):
        step(Group(s))


class Tile:

    def __init__(self, k, turn):
        self.k, self.turn, self.static = k, turn, isinstance(turn, int)

    def count(self, d):
        return self.k + d + TURN * self.turn

    def at_least(self, d):
        return not self.static or self.count(d) > 0

    def has(self, lag):
        return not self.static or 0 <= self.count(-lag) < ALL_TILES


def decoder_layer(nc, x, ctx_in, wqT, wkT, wv, woT, bq, bk, bv, bo, xwq, xwk, xwv, xwo,
                  router, rms_w, w1, w2, consts, out):
    with ExitStack() as ctx:
        def sb(name, shape, dt=F32):
            return ctx.enter_context(nc.sbuf_tensor(name, shape, dt))

        def sem(name):
            return ctx.enter_context(nc.semaphore(name))

        banks = ctx.enter_context(nc.psum_tensor("banks", [P, 8 * BANK], F32))

        def bank(b, n=1, lo=0, hi=None):
            return banks[:, b * BANK + lo:(b + n - 1) * BANK + (BANK if hi is None else hi)]

        xs = sb("xs", [P, B * E])
        cst = sb("cst", [P, 4 * P])
        ident = cst[:, 0:128]
        mask_f = cst[:, 128:256]
        cos_c = cst[:, 256:384].rearrange("p (a d) -> p a d", a=2)
        sin_c = cst[:, 384:512].rearrange("p (a d) -> p a d", a=2)
        bn = sb("bn", [P, B, 6])
        mean = sb("mean", [P, B])
        rstd = sb("rstd", [P, B])
        tmp_m = sb("tmp_m", [P, B])
        tmp_v = sb("tmp_v", [P, B])
        shift = sb("shift", [P, B])

        wqk_hi, wqk_lo = sb("wqk_hi", [P, 2, H * DK], F32R), sb("wqk_lo", [P, 2, H * DK], F32R)
        wvo_hi, wvo_lo = sb("wvo_hi", [P, H * E], F32R), sb("wvo_lo", [P, H * E], F32R)
        bias_row = sb("bias_row", [1, 2, H * DK])
        bv_col = sb("bv_col", [P, H * DK // P])
        last_row = sb("last_row", [1, P])
        fold = sb("fold", [P, P])
        cos_sb = sb("cos_sb", [P, 2, HPU, DK])
        sin_sb = sb("sin_sb", [P, 2, HPU, DK])
        out_bias = sb("out_bias", [P, E])
        xn = sb("xn", [P, E])
        xnT_hi, xnT_lo = sb("xnT_hi", [P, T], F32R), sb("xnT_lo", [P, T], F32R)
        rope_c = sb("rope_c", [P, 2 * FU])
        rope_s = sb("rope_s", [P, 2 * FU])
        qk = sb("qk", [P, 2 * FU])
        qkT = sb("qkT", [P, 2, CU, T])
        negmax = sb("negmax", [P, HPU])
        heads_sb = sb("heads_sb", [P, 4 * HPU * T])
        v = heads_sb[:, 0:2 * HPU * E].rearrange("p (a f) -> p a f", a=2)
        probs = heads_sb[:, 2 * HPU * T:3 * HPU * T].rearrange("p (h t) -> p h t", h=HPU)
        probsT = heads_sb[:, 3 * HPU * T:4 * HPU * T].rearrange("p (h t) -> p h t", h=HPU)
        sums = sb("sums", [P, HPU])
        rsums = sb("rsums", [P, HPU])

        dft = sb("dft", [P, 2 * P])
        dft_fwd, dft_inv = dft[:, 0:P], dft[:, P:2 * P]
        same_head = sb("same_head", [P, P])
        pos_c = sb("pos_c", [P, 1 + 2 * RP])
        head_pos, iota8, iota14 = pos_c[:, 0:1], pos_c[:, 1:1 + DH], pos_c[:, 1 + RP:1 + RP + ROUTED]
        xw = sb("xw", [P, 4, E])
        cs = sb("cs", [P, B * E])
        corr_sb = sb("corr_sb", [P, 9 * GT])
        ctx_a, ctx_b, xn4, khat, spec, specT, ctx_o, val_o, mixT = (corr_sb[:, n * GT:(n + 1) * GT] for n in range(9))
        freq = sb("freq", [P, 2, GT])
        cross_a, cross_b = sb("cross_a", [P, G, DK - 1]), sb("cross_b", [P, G, DK - 1])
        top_v, top_i = sb("top_v", [P, G, 8]), sb("top_i", [P, G, 8], U32)
        top_e, top_s, top_r = sb("top_e", [P, G, TOP]), sb("top_s", [P, G]), sb("top_r", [P, G])
        lag_n, lag_m = sb("lag_n", [P, G, TOP], U32), sb("lag_m", [P, G, TOP], U32)
        wait_pad = sb("wait_pad", [P, 1])
        onehot = sb("onehot", [P, G * TOP, DH])
        mix_row = sb("mix_row", [P, G, DH])
        mix = sb("mix", [P, G, DH, H])

        w1_sb, w2_sb = sb("w1_sb", [P, EXPERTS, HID]), sb("w2_sb", [P, EXPERTS, CH, E])
        stage = w1_sb[:].rearrange("p n h -> p (n h)").rearrange("p (k f) -> p k f", k=4)
        wq_raw, wk_raw = stage[:, 0], stage[:, 1]
        wv_raw = stage[:, 2].rearrange("p (c e) -> p c e", e=E)
        wo_raw = stage[:, 3].rearrange("p (c o) -> p c o", o=E)
        rmsT = sb("rmsT", [P, EXPERTS])
        router_sb = sb("router_sb", [P, ROUTED])
        rms, scale3 = sb("rms", [P, B]), sb("scale3", [P, B])
        xr = heads_sb
        back = heads_sb
        xrT = cs
        gates = sb("gates", [P, B, ROUTED])
        plan_c = sb("plan_c", [P, 2 * P])
        before_e = plan_c[:, 0:ROUTED * ROUTED].rearrange("p (e a) -> p e a", a=ROUTED)
        tile_start = plan_c[:, ROUTED * ROUTED:ROUTED * ROUTED + TILES]
        zeros = sb("zeros", [P, E])
        before_h, ones_h = sb("before_h", [P, P], BF16), sb("ones_h", [P, P], BF16)
        chosen = sb("chosen", [P, B, ROUTED], BF16)
        spare = [rope_c, rope_s]
        picks = [t[:, 0:B * ROUTED].rearrange("p (b n) -> p b n", n=ROUTED) for t in spare]
        place = qk[:, 0:B * ROUTED].rearrange("p (b n) -> p b n", n=ROUTED)
        spread = qk[:, BANK:BANK + B * ROUTED].rearrange("p (b n) -> p b n", n=ROUTED)
        spread_e = qk[:, BANK:BANK + 2 * ROUTED * ROUTED].rearrange("p (h e a) -> p h e a", h=2, a=ROUTED)
        past = cos_sb[:].rearrange("p a h d -> p (a h d)")
        past_b = sin_sb[:].rearrange("p a h d -> p (a h d)")
        count_n, count_m = sb("count_n", [P, 2, ROUTED], U32), sb("count_m", [P, 2, ROUTED], U32)
        begin, end = sb("begin", [P, 2, ROUTED]), sb("end", [P, 2, ROUTED])
        dest_f, dest = sb("dest_f", [P, TOP_K, B]), sb("dest", [P, TOP_K, B], U32)
        tile_e = sb("tile_e", [1, ALL_TILES])
        w_offset = sb("w_offset", [1, LAG + ALL_TILES + LAG], U32)
        x_tile = corr_sb[:, 0:TURN * E].rearrange("p (n e) -> p n e", e=E)
        y_tile = corr_sb[:, TURN * E:2 * TURN * E].rearrange("p (n e) -> p n e", e=E)
        tile_sb = corr_sb[:, 2 * TURN * E:2 * TURN * E + 3 * (P + 2 * HID)]
        x_tileT = tile_sb[:, 0:3 * P].rearrange("p (r t) -> p r t", r=3)
        h_tile = tile_sb[:, 3 * P:3 * (P + HID)].rearrange("p (r f) -> p r f", r=3)
        h_tileT = tile_sb[:, 3 * (P + HID):].rearrange("p (r f) -> p r f", r=3)
        x_rows = [nc.dram_tensor(f"x_rows_{h}", (TILES * P, E), F32, kind="Internal").ap() for h in range(2)]
        y_rows = [nc.dram_tensor(f"y_rows_{h}", (TILES * P, E), F32, kind="Internal").ap() for h in range(2)]
        best_v, best_i = sb("best_v", [P, B, 8]), sb("best_i", [P, B, 8], U32)
        best_n = sb("best_n", [P, B, 2])
        row_max, row_sum = sb("row_max", [P, B]), sb("row_sum", [P, B])
        hT = sb("hT", [P, 2, CH, GT])

        x_consts, ctx_loaded, e_loaded = sem("x_consts"), sem("ctx_loaded"), sem("e_loaded")
        ctx_a_ready, ctx_b_ready = sem("ctx_a_ready"), sem("ctx_b_ready")
        stats2, stats3 = sem("stats2"), sem("stats3")
        var2_ready, std2_ready, xn4_ready = sem("var2_ready"), sem("std2_ready"), sem("xn4_ready")
        freq_made, freq_ready = sem("freq_made"), sem("freq_ready")
        hats_made, khat_ready, spec_ready = sem("hats_made"), sem("khat_ready"), sem("spec_ready")
        spec_turned, specT_ready = sem("spec_turned"), sem("specT_ready")
        corr_made, shifted, top_exp = sem("corr_made"), sem("shifted"), sem("top_exp")
        mix_ready, ctx_o_made, ctx_o_ready = sem("mix_ready"), sem("ctx_o_made"), sem("ctx_o_ready")
        val_o_made, val_o_ready = sem("val_o_made"), sem("val_o_ready")
        mix_turned, mixT_ready = sem("mix_turned"), sem("mixT_ready")
        shift_ready = sem("shift_ready")
        tops, mixed, spec_step = sem("tops"), sem("mixed"), sem("spec_step")
        crossed, residual2 = sem("crossed"), sem("residual2")
        var3_ready, std3_ready, ms_ready, rms_ready = sem("var3_ready"), sem("std3_ready"), sem("ms_ready"), sem("rms_ready")
        w1_ready, xr_ready, xr_turned, xrT_ready = sem("w1_ready"), sem("xr_ready"), sem("xr_turned"), sem("xrT_ready")
        routed, logits_shifted, gates_exp, gates_ready = sem("routed"), sem("logits_shifted"), sem("gates_exp"), sem("gates_ready")
        hidden_made, hidden_ready = sem("hidden_made"), sem("hidden_ready")
        shared_made, shared_added = sem("shared_made"), sem("shared_added")
        zeros_set, rows_cleared = sem("zeros_set"), sem("rows_cleared")
        chosen_ready, ranked, dest_ready, plan_ready = sem("chosen_ready"), sem("ranked"), sem("dest_ready"), sem("plan_ready")
        scattered = [sem(f"scattered_{h}") for h in range(2)]
        tile_loaded = [sem(f"tile_loaded_{r}") for r in range(RING)]
        tile_stored = [sem(f"tile_stored_{r}") for r in range(RING)]
        tile_turned, tile_copied = sem("tile_turned"), sem("tile_copied")
        tile_multiplied, tile_activated = sem("tile_multiplied"), sem("tile_activated")
        gathered_a = sem("gathered_a")
        gathered_b = [sem(f"gathered_b_{c}") for c in range(CHUNKS)]
        combined, offsets_set = sem("combined"), sem("offsets_set")
        X_PIECES = 4
        x_loaded = [sem(f"x_loaded_{n}") for n in range(X_PIECES)]
        bias_loaded, c_loaded, tables_ready = sem("bias_loaded"), sem("c_loaded"), sem("tables_ready")
        qk_loaded, vo_loaded, b_loaded = sem("qk_loaded"), sem("vo_loaded"), sem("b_loaded")
        dve_step = sem("dve_step")
        var_ready, std_ready = sem("var_ready"), sem("std_ready")
        qk_folded, wv_ready, vo_folded = sem("qk_folded"), sem("wv_ready"), sem("vo_folded")
        hi_ready, lo_ready = sem("hi_ready"), sem("lo_ready")
        x_biased, ones_set = sem("x_biased"), sem("ones_set")
        xn_ready, xn_turned, xnT_ready = sem("xn_ready"), sem("xn_turned"), sem("xnT_ready")
        xnT_step = sem("xnT_step")
        qk_projected, rope_parts, rope_done = sem("qk_projected"), sem("rope_parts"), sem("rope_done")
        qk_turned, qkT_ready = sem("qk_turned"), sem("qkT_ready")
        masked = sem("masked")
        scored, max_ready, exp_done = sem("scored"), sem("max_ready"), sem("exp_done")
        rsum_ready, probs_ready = sem("rsum_ready"), sem("probs_ready")
        probs_turned, probsT_ready = sem("probs_turned"), sem("probsT_ready")
        v_projected, v_ready = sem("v_projected"), sem("v_ready")
        projected, residual = sem("projected"), sem("residual")
        stored = sem("stored")

        QK_BANK, T_BANK, S_BANK, V_BANK = 0, 2, 4, 6
        O_BANK, XN_BANK = QK_BANK, QK_BANK + 1
        HB = HPU // 2
        XB = B // X_PIECES

        block = ctx.enter_context(nc.Block())

        @block.sync
        def _(sp):
            sp.dma_start(cst[:], consts[:, 0:4 * P]).then_inc(c_loaded, 16)
            sp.dma_start(fold[:], consts[:, 4 * P:5 * P]).then_inc(c_loaded, 16)
            sp.dma_start(last_row[:], consts[E - 1:E, 0:P]).then_inc(bias_loaded, 16)
            sp.dma_start(wv_raw, wv.rearrange("(c p) e -> p c e", p=P)).then_inc(vo_loaded, 16)
            sp.dma_start(wo_raw, woT.rearrange("(c p) o -> p c o", p=P)).then_inc(vo_loaded, 16)
            for n in range(X_PIECES):
                sp.dma_start(xs[:, n * XB * E:(n + 1) * XB * E].rearrange("t (b e) -> t b e", b=XB),
                             x[n * XB:(n + 1) * XB].rearrange("b t e -> t b e")).then_inc(x_loaded[n], 16)
            sp.dma_start(dft[:], consts[:, 5 * P:7 * P]).then_inc(x_consts, 16)
            sp.dma_start(same_head[:], consts[:, 7 * P:8 * P]).then_inc(x_consts, 16)
            sp.dma_start(pos_c[:], consts[:, 8 * P:8 * P + 1 + 2 * RP]).then_inc(x_consts, 16)
            sp.dma_start(plan_c[:], consts[:, 9 * P:11 * P]).then_inc(x_consts, 16)
            for n, w in enumerate((xwq, xwk, xwv, xwo)):
                sp.dma_start(xw[:, n, :], w).then_inc(x_consts, 16)
            sp.dma_start(cs[:].rearrange("t (b e) -> t b e", b=B), ctx_in.rearrange("b t e -> t b e")).then_inc(ctx_loaded, 16)
            sp.wait_ge(vo_folded, 1)
            sp.dma_start(w1_sb[:], w1.rearrange("n e h -> e n h")).then_inc(e_loaded, 16)
            sp.dma_start(w2_sb[:], w2.rearrange("n (c p) e -> p n c e", p=P)).then_inc(e_loaded, 16)
            with nc.allow_non_contiguous_dma(reason="one weight per partition and expert"):
                sp.dma_start(rmsT[:], rms_w.rearrange("n e -> e n")).then_inc(e_loaded, 16)
            sp.dma_start(router_sb[:], router).then_inc(e_loaded, 16)
            sp.wait_ge(zeros_set, 1)
            for rows in x_rows:
                sp.dma_start(rows.rearrange("(n p) e -> p n e", p=P),
                             zeros[:].unsqueeze(1).broadcast_to([P, TILES, E])).then_inc(rows_cleared, 16)

            def load(half, local, r):
                sp.dma_start(x_tile[:, r * BATCH:(r + 1) * BATCH, :],
                             x_rows[half][bass.ds((local * TURN + r * BATCH) * P, BATCH * P), :]
                             .rearrange("(n p) e -> p n e", p=P)).then_inc(tile_loaded[r], 16)

            def store(half, local, r):
                sp.dma_start(y_rows[half][bass.ds((local * TURN + r * BATCH) * P, BATCH * P), :]
                             .rearrange("(n p) e -> p n e", p=P),
                             y_tile[:, r * BATCH:(r + 1) * BATCH, :]).then_inc(tile_stored[r], 16)

            for half in range(2):
                first = half * FIRST_B
                sp.wait_ge(scattered[half], 16 * TOP_K * HALF)
                for r in range(RING):
                    if half == 1:
                        sp.wait_ge(tile_turned, (first - 1) * TURN + (r + 1) * BATCH)
                    load(half, 0, r)
                    if half == 1:
                        sp.wait_ge(tile_activated, (first - 1) * TURN + (r + 1) * BATCH + LAG - 1)
                        store(0, TURNS - 1, r)
                with sp.Fori(1, TURNS) as i:
                    for r in range(RING):
                        sp.wait_ge(tile_turned, (i + first - 1) * TURN + (r + 1) * BATCH)
                        load(half, i, r)
                        sp.wait_ge(tile_activated, (i + first - 1) * TURN + (r + 1) * BATCH + LAG - 1)
                        store(half, i - 1, r)
            for r in range(RING):
                sp.wait_ge(tile_activated, (2 * TURNS - 1) * TURN + (r + 1) * BATCH + LAG - 1)
                store(1, TURNS - 1, r)
            for g in range(GROUPS):
                sp.wait_ge(combined, (g + 1) * TOP_K * G)
                sp.dma_start(out[g * G:(g + 1) * G].rearrange("b t e -> t b e"),
                             xs[:, g * G * E:(g + 1) * G * E].rearrange("t (b e) -> t b e", b=G)).then_inc(stored, 16)
            sp.wait_ge(stored, 16 * GROUPS)

        @block.gpsimd
        def _(pool):
            nc.gpsimd.memset(zeros[:], 0.0).then_inc(zeros_set, 1)
            pool.wait_ge(c_loaded, 16 * 2)
            for a in range(2):
                nc.gpsimd.tensor_copy(cos_sb[:, a], cos_c[:, a].unsqueeze(1).broadcast_to([P, HPU, DK]))\
                    .then_inc(tables_ready, 1)
                nc.gpsimd.tensor_copy(sin_sb[:, a], sin_c[:, a].unsqueeze(1).broadcast_to([P, HPU, DK]))\
                    .then_inc(tables_ready, 1)

            def step(s):
                if s.has(0):
                    if s.parity == 0:
                        pool.wait_ge(xn_ready, s.seq(0) + 1)
                        if s.i is None and s.base == 0:
                            pool.wait_ge(b_loaded, 16 * 2)
                        xb = xs[:, bass.ds(s.seq(0) * E, E)]
                        nc.gpsimd.tensor_tensor(xb, xb, out_bias[:], ALU.add).then_inc(x_biased, 1)
                    pool.wait_ge(rope_parts, s.count(1))
                    nc.gpsimd.tensor_tensor(qk[:], rope_c[:], rope_s[:], ALU.add).then_inc(rope_done, 1)

            for_slots(pool, step)

            pool.wait_ge(ctx_loaded, 16)

            def copies(s):
                if s.has(0):
                    if s.at_least(0):
                        pool.wait_ge(freq_made, s.count(0))
                    nc.gpsimd.tensor_copy(ctx_a[:], cs[:, s.tokens(0)]).then_inc(ctx_a_ready, 1)
                    if s.i is None and s.base < 2:
                        if s.base == 0:
                            pool.wait_ge(e_loaded, 16 * 4)
                        n = slice(s.base * EXPERTS // 2, (s.base + 1) * EXPERTS // 2)
                        nc.gpsimd.tensor_tensor(w1_sb[:, n, :], w1_sb[:, n, :],
                                                rmsT[:, n].unsqueeze(2).broadcast_to([P, EXPERTS // 2, HID]), ALU.mult)\
                            .then_inc(w1_ready, 1)
                if s.has(2):
                    if s.at_least(-2):
                        pool.wait_ge(ctx_o_made, s.count(-2))
                    nc.gpsimd.tensor_copy(ctx_b[:], cs[:, s.tokens(2)]).then_inc(ctx_b_ready, 1)

            for_groups(pool, copies)

            pool.wait_ge(rows_cleared, 16 * 2)
            pool.wait_ge(dest_ready, 1)
            for half in range(2):
                for b in range(half * HALF, (half + 1) * HALF):
                    for k in range(TOP_K):
                        nc.gpsimd.indirect_dma_start(
                            out=x_rows[half], out_offset=bass.IndirectOffsetOnAxis(ap=dest[:, k, b:b + 1], axis=0),
                            in_=xr[:, b * E:(b + 1) * E], in_offset=None).then_inc(scattered[half], 16)
            pool.wait_ge(scattered[0], 16 * TOP_K * HALF)
            pool.wait_ge(scattered[1], 16 * TOP_K * HALF)
            for half in range(2):
                for r in range(RING):
                    pool.wait_ge(tile_stored[r], 16 * TURNS * (half + 1))
                for c in range(CHUNKS):
                    if half == 1:
                        pool.wait_ge(combined, (c + 1) * TOP_K * G)
                    for k in range(TOP_K):
                        for n in range(G):
                            b = half * HALF + c * G + n
                            m = (c * TOP_K + k) * G + n
                            nc.gpsimd.indirect_dma_start(
                                out=back[:, m * E:(m + 1) * E], out_offset=None, in_=y_rows[half],
                                in_offset=bass.IndirectOffsetOnAxis(ap=dest[:, k, b:b + 1], axis=0))\
                                .then_inc(gathered_b[c] if half == 1 else gathered_a, 16)
                    if half == 0:
                        pool.wait_ge(gathered_a, 16 * TOP_K * G * (c + 1))

        @block.scalar
        def _(act):
            act.dma_start(wq_raw, wqT).then_inc(qk_loaded, 16)
            act.dma_start(wk_raw, wkT).then_inc(qk_loaded, 16)
            act.dma_start(bias_row[:, 0, :], bq.unsqueeze(0)).then_inc(bias_loaded, 16)
            act.dma_start(bias_row[:, 1, :], bk.unsqueeze(0)).then_inc(bias_loaded, 16)
            act.dma_start(out_bias[:], bo.unsqueeze(0).broadcast_to([P, E])).then_inc(b_loaded, 16)
            with nc.allow_non_contiguous_dma(reason="one bias value per partition"):
                act.dma_start(bv_col[:], bv.rearrange("(c p) -> p c", p=P)).then_inc(b_loaded, 16)
            act.wait_ge(var_ready, 1)
            nc.scalar.activation(tmp_v[:], tmp_v[:], ACT.Sqrt).then_inc(std_ready, 1)
            act.wait_ge(qk_folded, 1)
            nc.scalar.activation(wqk_hi[:].rearrange("p a f -> p (a f)"), bank(0, 4), ACT.Copy).then_inc(hi_ready, 1)
            act.wait_ge(vo_folded, 1)
            nc.scalar.activation(wvo_hi[:], bank(4, 4), ACT.Copy).then_inc(hi_ready, 1)

            def step(s):
                if s.has(1):
                    act.wait_ge(qk_turned, s.count(0))
                    nc.scalar.activation(qkT[:].rearrange("p a c t -> p (a c t)"), bank(T_BANK, 2), ACT.Copy)\
                        .then_inc(qkT_ready, 1)
                    act.wait_ge(v_projected, s.count(0))
                    nc.scalar.activation(v[:, 1 - s.parity, :], bank(V_BANK, 2), ACT.Copy).then_inc(v_ready, 1)
                if s.has(2):
                    act.wait_ge(probs_turned, s.count(-1))
                    nc.scalar.activation(probsT.rearrange("p h t -> p (h t)"), bank(T_BANK, 2), ACT.Copy)\
                        .then_inc(probsT_ready, 1)
                if s.has(1):
                    for h in range(HPU):
                        if h % HB == 0:
                            act.wait_ge(max_ready, s.count(-1) * 2 + h // HB + 1)
                        nc.scalar.activation(probs[:, h, :], bank(S_BANK, 2)[:, h * T:(h + 1) * T], ACT.Exp,
                                             bias=negmax[:, h:h + 1], accum_out=sums[:, h:h + 1])\
                            .then_inc(exp_done, 1)

            for_slots(act, step)

            act.wait_ge(var2_ready, 1)
            nc.scalar.activation(tmp_v[:], tmp_v[:], ACT.Sqrt).then_inc(std2_ready, 1)

            def normalise4(s, lag):
                for n in range(G):
                    b = s.count(-lag) * G + n
                    nc.scalar.activation(xn4[:, n * E:(n + 1) * E], xs[:, bass.ds(b * E, E)], ACT.Identity,
                                         bias=shift[:, bass.ds(b, 1)], scale=rstd[:, bass.ds(b, 1)]).then_inc(xn4_ready, 1)

            act.wait_ge(shift_ready, 1)
            normalise4(Group(0), 0)

            def correlate(s):
                if s.has(0):
                    act.wait_ge(freq_made, s.count(1))
                    nc.scalar.activation(freq[:].rearrange("p a t -> p (a t)"), bank(0, 2), ACT.Copy).then_inc(freq_ready, 1)
                if s.has(1):
                    act.wait_ge(spec_turned, s.count(0))
                    nc.scalar.activation(specT[:], bank(4), ACT.Copy).then_inc(specT_ready, 1)
                if s.has(2):
                    act.wait_ge(ctx_o_made, s.count(-1))
                    nc.scalar.activation(ctx_o[:], bank(6), ACT.Copy).then_inc(ctx_o_ready, 1)
                if s.has(-1) and s.base != GROUPS - 1:
                    normalise4(s, -1)
                if s.has(0):
                    act.wait_ge(hats_made, s.count(1))
                    nc.scalar.activation(khat[:], bank(3), ACT.Copy).then_inc(khat_ready, 1)
                if s.has(2):
                    act.wait_ge(val_o_made, s.count(-1))
                    nc.scalar.activation(val_o[:], bank(7), ACT.Copy).then_inc(val_o_ready, 1)
                    act.wait_ge(mix_turned, s.count(-1))
                    nc.scalar.activation(mixT[:], bank(4), ACT.Copy).then_inc(mixT_ready, 1)
                if s.has(1):
                    act.wait_ge(shifted, s.count(0))
                    nc.scalar.activation(top_e[:], top_e[:], ACT.Exp).then_inc(top_exp, 1)

            for_groups(act, correlate)

            act.wait_ge(var3_ready, 1)
            nc.scalar.activation(tmp_v[:], tmp_v[:], ACT.Sqrt).then_inc(std3_ready, 1)
            act.wait_ge(ms_ready, 1)
            nc.scalar.activation(rms[:], rms[:], ACT.Sqrt).then_inc(rms_ready, 1)
            for g in range(GROUPS):
                act.wait_ge(xr_turned, g + 1)
                nc.scalar.activation(xrT[:, g * GT:(g + 1) * GT], bank(g % 2), ACT.Copy).then_inc(xrT_ready, 1)
            act.wait_ge(logits_shifted, 1)
            nc.scalar.activation(gates[:], gates[:], ACT.Exp).then_inc(gates_exp, 1)

            with act.Fori(0, GROUPS) as g:
                for m in range(SHARED):
                    for c in range(CH):
                        act.wait_ge(hidden_made, g * (SHARED * CH) + m * CH + c + 1)
                        nc.scalar.activation(hT[:, m, c, :], bank(2 * m + c), ACT.Silu).then_inc(hidden_ready, 1)

            def tile_slot(s):
                if s.at_least(0):
                    act.wait_ge(tile_multiplied, s.count(0))
                    src = bank(3 + s.k % 3)
                    if s.has(1):
                        last = nc.scalar.activation(h_tile[:, (s.k - 1) % 3, :], src[:, 0:HID], ACT.Silu)
                    if s.has(LAG):
                        k = (s.k - LAG) % TURN
                        turn = s.turn if s.k >= LAG else s.turn - 1
                        if k % BATCH == 0 and not (s.static and turn < 1):
                            act.wait_ge(tile_stored[k // BATCH], 16 * turn)
                        last = nc.scalar.activation(y_tile[:, k, :], src[:, HID:HID + E], ACT.Copy)
                    last.then_inc(tile_activated, 1)

            for k in range(TURN):
                tile_slot(Tile(k, 0))
            tile_slot_first = [Tile(k, 1) for k in range(LAG)]
            for t in tile_slot_first:
                tile_slot(t)
            for k in range(LAG, TURN):
                tile_slot(Tile(k, 1))
            with act.Fori(2, 2 * TURNS) as i:
                for k in range(TURN):
                    tile_slot(Tile(k, i))
            for k in range(LAG):
                tile_slot(Tile(k, 2 * TURNS))

        @block.vector
        def _(dve):
            steps = [0]

            def then(ins):
                steps[0] += 1
                ins.then_inc(dve_step, 1)
                dve.wait_ge(dve_step, steps[0])

            def moments():
                even, odd = bn[:, :, 1], bn[:, :, 4]
                then(nc.vector.tensor_tensor(mean[:], even, odd, ALU.add))
                then(nc.vector.tensor_scalar(mean[:], mean[:], 0.5, None, ALU.mult))
                then(nc.vector.tensor_tensor(tmp_m[:], even, odd, ALU.subtract))
                then(nc.vector.tensor_tensor(tmp_m[:], tmp_m[:], tmp_m[:], ALU.mult))
                then(nc.vector.tensor_tensor(tmp_v[:], bn[:, :, 2], bn[:, :, 5], ALU.add))
                then(nc.vector.tensor_scalar(tmp_v[:], tmp_v[:], 1.0 / E, None, ALU.mult))
                then(nc.vector.scalar_tensor_tensor(tmp_v[:], tmp_m[:], 0.25, tmp_v[:], ALU.mult, ALU.add))

            nc.vector.memset(xnT_hi[:].bitcast(F32), 1.0).then_inc(ones_set, 1)
            nc.vector.memset(xnT_lo[:].bitcast(F32), 0.0).then_inc(ones_set, 1)
            dve.wait_ge(b_loaded, 16 * 2)
            dve.wait_ge(vo_loaded, 16 * 2)
            last = wv_raw[:, :, E - 1:E]
            then(nc.vector.tensor_tensor(wv_raw[:, :, 0:E - 1], wv_raw[:, :, 0:E - 1],
                                         last.broadcast_to([P, H * DK // P, E - 1]), ALU.subtract))
            nc.vector.tensor_copy(wv_raw[:, :, E - 1], bv_col[:]).then_inc(wv_ready, 1)
            for b in range(B):
                if b % XB == 0:
                    dve.wait_ge(x_loaded[b // XB], 16)
                last = nc.vector.bn_stats(bn[:, b, :], xs[:, b * E:(b + 1) * E])
            then(last)
            moments()
            nc.vector.tensor_scalar(tmp_v[:], tmp_v[:], LN_EPS, None, ALU.add).then_inc(var_ready, 1)
            dve.wait_ge(std_ready, 1)
            then(nc.vector.reciprocal(rstd[:], tmp_v[:]))

            def normalise(b):
                nc.vector.tensor_scalar(xn[:], xs[:, bass.ds(b * E, E)], mean[:, bass.ds(b, 1)],
                                        rstd[:, bass.ds(b, 1)], ALU.subtract, ALU.mult).then_inc(xn_ready, 1)

            def split_xnT(b):
                dve.wait_ge(xn_turned, b + 1)
                rows = slice(0, E - 1)
                nc.vector.tensor_copy(xnT_hi[rows, :], bank(XN_BANK)[rows, 0:T]).then_inc(xnT_step, 1)
                dve.wait_ge(xnT_step, b + 1)
                nc.vector.tensor_tensor(xnT_lo[rows, :], bank(XN_BANK)[rows, 0:T], xnT_hi[rows, :].bitcast(F32),
                                        ALU.subtract).then_inc(xnT_ready, 1)

            normalise(0)
            dve.wait_ge(hi_ready, 1)
            nc.vector.tensor_tensor(wqk_lo[:].rearrange("p a f -> p (a f)"), bank(0, 4),
                                    wqk_hi[:].rearrange("p a f -> p (a f)").bitcast(F32), ALU.subtract).then_inc(lo_ready, 1)
            dve.wait_ge(ones_set, 2)
            split_xnT(0)
            dve.wait_ge(hi_ready, 2)
            nc.vector.tensor_tensor(wvo_lo[:], bank(4, 4), wvo_hi[:].bitcast(F32), ALU.subtract).then_inc(lo_ready, 1)

            def normalise_probs(s, lag, a):
                dve.wait_ge(exp_done, s.count(-lag) * HPU + (a + 1) * HB)
                heads = slice(a * HB, (a + 1) * HB)
                nc.vector.reciprocal(rsums[:, heads], sums[:, heads]).then_inc(rsum_ready, 1)
                dve.wait_ge(rsum_ready, s.count(-lag) * 2 + a + 1)
                nc.vector.tensor_tensor(probs[:, heads, :], probs[:, heads, :],
                                        rsums[:, heads].unsqueeze(2).broadcast_to([P, HB, T]), ALU.mult)\
                    .then_inc(probs_ready, 1)

            def sequence_stats(b):
                nc.vector.bn_stats(bn[:, bass.ds(b, 1), :].rearrange("p a s -> p (a s)"), xs[:, bass.ds(b * E, E)])\
                    .then_inc(stats2, 1)

            def step(s):
                if s.has(2):
                    normalise_probs(s, 2, 1)
                if s.has(0):
                    dve.wait_ge(qk_projected, s.count(1))
                    if s.i is None and s.base == 0:
                        dve.wait_ge(tables_ready, 4)
                    raw = bank(QK_BANK, 2)
                    if s.at_least(0):
                        dve.wait_ge(rope_done, s.count(0))
                    nc.vector.tensor_tensor(rope_c[:], raw, cos_sb[:].rearrange("p a h d -> p (a h d)"), ALU.mult)
                    nc.vector.tensor_tensor(
                        rope_s[:].rearrange("p (f e) -> p f e", e=2), raw.rearrange("p (f e) -> p f e", e=2)[:, :, ::-1],
                        sin_sb[:].rearrange("p a h (f e) -> p (a h f) e", e=2), ALU.mult).then_inc(rope_parts, 1)
                more = s.parity == 1 and (s.i is not None or s.base < UNITS - 1)
                if more:
                    normalise(s.seq(0) + 1)
                if s.has(1):
                    dve.wait_ge(scored, s.count(0))
                    for a in range(2):
                        sc = bank(S_BANK + a).rearrange("p (h k) -> p h k", k=T)
                        nc.vector.tensor_tensor(sc, sc, mask_f.unsqueeze(1).broadcast_to([P, HB, T]), ALU.add)\
                            .then_inc(masked, 1)
                        dve.wait_ge(masked, s.count(-1) * 2 + a + 1)
                        nc.vector.tensor_reduce(negmax[:, a * HB:(a + 1) * HB],
                                                bank(S_BANK + a).rearrange("p (h k) -> p h k", k=T), AX_X,
                                                ALU.max, negate=True).then_inc(max_ready, 1)
                if s.parity == 0 and s.has(3):
                    dve.wait_ge(residual, s.count(-2))
                    sequence_stats(s.seq(3))
                if more:
                    dve.wait_ge(v_projected, s.count(1))
                    split_xnT(s.seq(0) + 1)
                if s.has(1):
                    normalise_probs(s, 1, 0)
                if s.has(2):
                    dve.wait_ge(x_biased, s.seq(2) + 1)
                    dve.wait_ge(projected, s.count(-1))
                    xb = xs[:, bass.ds(s.seq(2) * E, E)]
                    if s.at_least(-2):
                        dve.wait_ge(residual, s.count(-2))
                    nc.vector.tensor_tensor(xb, xb, bank(O_BANK)[:, 0:E], ALU.add).then_inc(residual, 1)

            for_slots(dve, step)
            dve.wait_ge(residual, UNITS)
            sequence_stats(B - 1)

            dve.wait_ge(stats2, B)
            moments()
            nc.vector.tensor_scalar(tmp_v[:], tmp_v[:], LN_EPS, None, ALU.add).then_inc(var2_ready, 1)
            dve.wait_ge(std2_ready, 1)
            then(nc.vector.reciprocal(rstd[:], tmp_v[:]))

            nc.vector.scalar_tensor_tensor(shift[:], mean[:], -1.0, rstd[:], ALU.mult, ALU.mult).then_inc(shift_ready, 1)
            dve.wait_ge(x_consts, 16 * 8)
            N = DK

            def correlate(s):
                if s.has(3):
                    dve.wait_ge(crossed, s.count(-2))
                    xg = xs[:, s.tokens(3)]
                    nc.vector.tensor_tensor(xg, xg, bank(7), ALU.add).then_inc(residual2, 1)
                    dve.wait_ge(residual2, s.count(-2))
                    for n in range(G):
                        b = s.count(-3) * G + n
                        nc.vector.bn_stats(bn[:, bass.ds(b, 1), :].rearrange("p a s -> p (a s)"), xs[:, bass.ds(b * E, E)])\
                            .then_inc(stats3, 1)
                if s.has(0):
                    dve.wait_ge(hats_made, s.count(1))
                    dve.wait_ge(khat_ready, s.count(1))
                    if s.at_least(0):
                        dve.wait_ge(spec_turned, s.count(0))
                    q3 = bank(2).rearrange("p (g f) -> p g f", g=G)
                    k3 = khat[:].rearrange("p (g f) -> p g f", g=G)
                    s3 = spec[:].rearrange("p (g f) -> p g f", g=G)
                    re, im = slice(1, N), slice(N + 1, 2 * N)
                    nc.vector.tensor_tensor(spec[:], bank(2), khat[:], ALU.mult).then_inc(spec_step, 1)
                    nc.vector.tensor_tensor(cross_a[:], q3[:, :, im], k3[:, :, re], ALU.mult).then_inc(spec_step, 1)
                    nc.vector.tensor_tensor(cross_b[:], q3[:, :, re], k3[:, :, im], ALU.mult).then_inc(spec_step, 1)
                    dve.wait_ge(spec_step, s.count(0) * 4 + 3)
                    nc.vector.tensor_tensor(s3[:, :, re], s3[:, :, re], s3[:, :, im], ALU.add).then_inc(spec_step, 1)
                    dve.wait_ge(spec_step, s.count(1) * 4)
                    nc.vector.tensor_tensor(s3[:, :, im], cross_a[:], cross_b[:], ALU.subtract).then_inc(spec_ready, 1)
                if s.has(1):
                    dve.wait_ge(corr_made, s.count(0))
                    nc.vector.memset(wait_pad[:], 0.0)
                    for n in range(G):
                        nc.vector.max(top_v[:, n, :], bank(5)[:, n * T:(n + 1) * T]).then_inc(tops, 1)
                    dve.wait_ge(tops, s.count(0) * (2 * G) - G)
                    nc.vector.memset(wait_pad[:], 0.0)
                    for n in range(G):
                        nc.vector.max_index(top_i[:, n, :], top_v[:, n, :], bank(5)[:, n * T:(n + 1) * T]).then_inc(tops, 1)
                    nc.vector.tensor_tensor(top_e[:], top_v[:, :, 0:TOP], top_v[:, :, 0:1].broadcast_to([P, G, TOP]),
                                            ALU.subtract).then_inc(shifted, 1)
                if s.has(1):
                    k = 8
                    dve.wait_ge(tops, s.count(0) * (2 * G))
                    nc.vector.tensor_scalar(lag_n[:], top_i[:, :, 0:TOP], -1.0, head_pos, ALU.mult, ALU.add).then_inc(mixed, 1)
                    dve.wait_ge(mixed, s.count(-1) * k + 1)
                    nc.vector.tensor_scalar(lag_m[:], lag_n[:], DH - 1, None, ALU.bitwise_and).then_inc(mixed, 1)
                    dve.wait_ge(top_exp, s.count(0))
                    nc.vector.tensor_reduce(top_s[:], top_e[:], AX_X, ALU.add).then_inc(mixed, 1)
                    dve.wait_ge(mixed, s.count(-1) * k + 3)
                    nc.vector.reciprocal(top_r[:], top_s[:]).then_inc(mixed, 1)
                    nc.vector.tensor_tensor(
                        onehot[:], lag_m[:].rearrange("p g l -> p (g l)").unsqueeze(2).broadcast_to([P, G * TOP, DH]),
                        iota8.unsqueeze(1).broadcast_to([P, G * TOP, DH]), ALU.is_equal).then_inc(mixed, 1)
                    dve.wait_ge(mixed, s.count(-1) * k + 5)
                    nc.vector.tensor_tensor(top_e[:], top_e[:], top_r[:].unsqueeze(2).broadcast_to([P, G, TOP]), ALU.mult)\
                        .then_inc(mixed, 1)
                    dve.wait_ge(mixed, s.count(-1) * k + 6)
                    nc.vector.tensor_tensor(
                        onehot[:], onehot[:],
                        top_e[:].rearrange("p g l -> p (g l)").unsqueeze(2).broadcast_to([P, G * TOP, DH]), ALU.mult)\
                        .then_inc(mixed, 1)
                    dve.wait_ge(mixed, s.count(-1) * k + 7)
                    nc.vector.tensor_reduce(mix_row[:], onehot[:].rearrange("p (g l) d -> p g d l", g=G), AX_X, ALU.add)\
                        .then_inc(mixed, 1)
                    dve.wait_ge(mixed, s.count(0) * k)
                    if s.at_least(-1):
                        dve.wait_ge(mix_turned, s.count(-1))
                    nc.vector.tensor_tensor(
                        mix[:], mix_row[:].unsqueeze(3).broadcast_to([P, G, DH, H]),
                        same_head[:].rearrange("p (d h) -> p d h", h=H).unsqueeze(1).broadcast_to([P, G, DH, H]), ALU.mult)\
                        .then_inc(mix_ready, 1)

            for_groups(dve, correlate)

            dve.wait_ge(stats3, B)
            moments()
            then(nc.vector.tensor_scalar(rstd[:], tmp_v[:], LN_EPS, None, ALU.add))
            then(nc.vector.reciprocal(scale3[:], rstd[:]))
            then(nc.vector.tensor_tensor(rms[:], tmp_v[:], scale3[:], ALU.mult))
            nc.vector.tensor_scalar(rms[:], rms[:], RMS_EPS, None, ALU.add).then_inc(ms_ready, 1)
            nc.vector.tensor_copy(tmp_v[:], rstd[:]).then_inc(var3_ready, 1)
            dve.wait_ge(std3_ready, 1)
            dve.wait_ge(rms_ready, 1)
            then(nc.vector.tensor_tensor(tmp_v[:], tmp_v[:], rms[:], ALU.mult))
            then(nc.vector.reciprocal(scale3[:], tmp_v[:]))
            for b in range(B):
                nc.vector.tensor_scalar(xr[:, b * E:(b + 1) * E], xs[:, b * E:(b + 1) * E], mean[:, b:b + 1],
                                        scale3[:, b:b + 1], ALU.subtract, ALU.mult).then_inc(xr_ready, 1)
            nc.vector.tensor_scalar(before_h[:], mask_f, 0.0, None, ALU.is_lt)
            nc.vector.memset(ones_h[:], 1.0)
            nc.vector.memset(w_offset[:], 0).then_inc(offsets_set, 1)
            dve.wait_ge(routed, B)
            then(nc.vector.tensor_tensor(gates[:], bank(6).rearrange("p (b n) -> p b n", n=RP)[:, :, 0:ROUTED],
                                         rms[:].unsqueeze(2).broadcast_to([P, B, ROUTED]), ALU.mult))
            then(nc.vector.tensor_reduce(row_max[:], gates[:], AX_X, ALU.max))
            nc.vector.tensor_tensor(gates[:], gates[:], row_max[:].unsqueeze(2).broadcast_to([P, B, ROUTED]),
                                    ALU.subtract).then_inc(logits_shifted, 1)
            dve.wait_ge(gates_exp, 1)
            then(nc.vector.tensor_reduce(row_sum[:], gates[:], AX_X, ALU.add))
            then(nc.vector.reciprocal(row_max[:], row_sum[:]))
            then(nc.vector.tensor_tensor(gates[:], gates[:], row_max[:].unsqueeze(2).broadcast_to([P, B, ROUTED]), ALU.mult))
            for b in range(B):
                last = nc.vector.max(best_v[:, b, :], gates[:, b, :])
            then(last)
            for b in range(B):
                last = nc.vector.max_index(best_i[:, b, :], best_v[:, b, :], gates[:, b, :])
            then(last)
            then(nc.vector.tensor_tensor(row_sum[:], best_v[:, :, 0], best_v[:, :, 1], ALU.add))
            then(nc.vector.tensor_scalar(row_sum[:], row_sum[:], GATE_EPS, None, ALU.add))
            then(nc.vector.reciprocal(row_max[:], row_sum[:]))
            then(nc.vector.tensor_tensor(best_n[:], best_v[:, :, 0:2], row_max[:].unsqueeze(2).broadcast_to([P, B, 2]), ALU.mult))
            for k in range(TOP_K):
                then(nc.vector.tensor_tensor(picks[k], best_i[:, :, k:k + 1].broadcast_to([P, B, ROUTED]),
                                             iota14.unsqueeze(1).broadcast_to([P, B, ROUTED]), ALU.is_equal))
            nc.vector.tensor_tensor(chosen[:], picks[0], picks[1], ALU.add).then_inc(chosen_ready, 1)

            def add_shared(g, b):
                xg = xs[:, bass.ds(g * G * E, G * E)]
                dve.wait_ge(shared_made, g + 1)
                nc.vector.tensor_tensor(xg, xg, bank(b), ALU.add).then_inc(shared_added, 1)

            add_shared(0, 5)
            add_shared(1, 4)
            dve.wait_ge(ranked, 2)
            counts = bank(6)[:, 0:2 * ROUTED].rearrange("p (h e) -> p h e", h=2)
            then(nc.vector.tensor_scalar(count_n[:], counts, float(P - 1), None, ALU.add))
            then(nc.vector.tensor_scalar(count_m[:], count_n[:], 0xFFFF - (P - 1), None, ALU.bitwise_and))
            then(nc.vector.tensor_tensor(spread_e, count_m[:].unsqueeze(2).broadcast_to([P, 2, ROUTED, ROUTED]),
                                         before_e.unsqueeze(1).broadcast_to([P, 2, ROUTED, ROUTED]), ALU.mult))
            then(nc.vector.tensor_reduce(begin[:], spread_e, AX_X, ALU.add))
            then(nc.vector.tensor_tensor(
                place.rearrange("p (h b) e -> p h b e", h=2),
                bank(7)[:, 0:B * ROUTED].rearrange("p (h b e) -> p h b e", h=2, e=ROUTED),
                begin[:].unsqueeze(2).broadcast_to([P, 2, HALF, ROUTED]), ALU.add))
            for k in range(TOP_K):
                then(nc.vector.tensor_tensor(picks[k], picks[k], place, ALU.mult))
                then(nc.vector.tensor_reduce(dest_f[:, k, :], picks[k], AX_X, ALU.add))
            nc.vector.tensor_copy(dest[:], dest_f[:]).then_inc(dest_ready, 1)
            then(nc.vector.tensor_tensor(end[:], begin[:], count_m[:], ALU.add))
            for half, mem in enumerate((past, past_b)):
                behind = mem[0:1, 0:TILES * ROUTED].rearrange("p (j e) -> p j e", e=ROUTED)
                then(nc.vector.tensor_tensor(behind, end[0:1, half].unsqueeze(1).broadcast_to([1, TILES, ROUTED]),
                                             tile_start[0:1].unsqueeze(2).broadcast_to([1, TILES, ROUTED]), ALU.is_le))
                then(nc.vector.tensor_reduce(tile_e[:, half * TILES:(half + 1) * TILES], behind, AX_X, ALU.add))
            then(nc.vector.tensor_scalar(tile_e[:], tile_e[:], float(ROUTED - 1), float(HID), ALU.min, ALU.mult))
            dve.wait_ge(offsets_set, 1)
            nc.vector.tensor_copy(w_offset[:, LAG:LAG + ALL_TILES], tile_e[:]).then_inc(plan_ready, 1)

            with dve.Fori(1, GROUPS // 2) as i:
                add_shared(2 * i, 5)
                add_shared(2 * i + 1, 4)

            def tile_slot(s):
                dve.wait_ge(tile_turned, s.count(1))
                src = bank(s.k % 3)
                if s.at_least(-2):
                    dve.wait_ge(tile_multiplied, s.count(-2))
                if s.has(0):
                    last = nc.vector.tensor_copy(x_tileT[:, s.k % 3, :], src[:, 0:P])
                if s.has(3):
                    last = nc.vector.tensor_copy(h_tileT[:, s.k % 3, :], src[:, P:P + HID])
                last.then_inc(tile_copied, 1)

            def combine(c, n, k, b, m):
                xb = xs[:, bass.ds(b * E, E)]
                if k == 1:
                    dve.wait_ge(combined, c - G + 1)
                nc.vector.scalar_tensor_tensor(xb, back[:, bass.ds(m * E, E)],
                                               best_n[:].rearrange("p b k -> p (b k)")[:, bass.ds(b * TOP_K + k, 1)],
                                               xb, ALU.mult, ALU.add).then_inc(combined, 1)

            dve.wait_ge(shared_added, GROUPS)
            for k in range(TURN):
                tile_slot(Tile(k, 0))
            with dve.Fori(1, FIRST_B + 2) as i:
                for k in range(TURN):
                    tile_slot(Tile(k, i))
            with dve.Fori(FIRST_B + 2, 2 * TURNS) as i:
                c = i - (FIRST_B + 2)
                for k in range(TURN):
                    tile_slot(Tile(k, i))
                    if k < TOP_K * G:
                        if k == 0:
                            dve.wait_ge(gathered_a, 16 * TOP_K * G * (c + 1))
                        combine(c * TOP_K * G + k, k % G, k // G, c * G + k % G, c * TOP_K * G + k)
            for k in range(LAG - 1):
                tile_slot(Tile(k, 2 * TURNS))
            c = CHUNKS - 1
            dve.wait_ge(gathered_a, 16 * TOP_K * HALF)
            for k in range(TOP_K * G):
                combine(c * TOP_K * G + k, k % G, k // G, c * G + k % G, c * TOP_K * G + k)
            for c in range(CHUNKS):
                dve.wait_ge(gathered_b[c], 16 * TOP_K * G)
                for k in range(TOP_K * G):
                    combine((CHUNKS + c) * TOP_K * G + k, k % G, k // G, HALF + c * G + k % G, c * TOP_K * G + k)

        @block.tensor
        def _(pe):
            def turn(b):
                pe.wait_ge(xn_ready, b + 1)
                nc.tensor.transpose(bank(XN_BANK)[:, 0:T], xn[:], ident).then_inc(xn_turned, 1)

            pe.wait_ge(c_loaded, 16 * 2)
            pe.wait_ge(qk_loaded, 16 * 2)
            pe.wait_ge(bias_loaded, 16 * 3)
            for a, w in enumerate((wq_raw, wk_raw)):
                for u in range(2):
                    cols = slice(u * FU, (u + 1) * FU)
                    nc.tensor.matmul(bank(2 * a + u), fold[:], w[:, cols], start=True, stop=False)
                    last = nc.tensor.matmul(bank(2 * a + u), last_row[:], bias_row[:, a, cols], start=False, stop=True)
            last.then_inc(qk_folded, 1)
            pe.wait_ge(wv_ready, 1)
            for u in range(2):
                for n in range(CU):
                    for a in range(2):
                        rows, c = slice(a * DK, (a + 1) * DK), u * CU + n
                        last = nc.tensor.matmul(bank(4 + 2 * u + a)[:, n * E:(n + 1) * E], wv_raw[rows, c, :],
                                                wo_raw[rows, c, :], start=True, stop=True)
            last.then_inc(vo_folded, 1)
            pe.wait_ge(lo_ready, 1)
            turn(0)
            pe.wait_ge(tables_ready, 4)

            def project(n, cols, hi, lo):
                nc.tensor.matmul(bank(n), xnT_hi[:], hi[:, cols], start=True, stop=False)
                nc.tensor.matmul(bank(n), xnT_hi[:], lo[:, cols], start=False, stop=False)
                return nc.tensor.matmul(bank(n), xnT_lo[:], hi[:, cols], start=False, stop=True)

            def step(s):
                if s.has(1):
                    pe.wait_ge(rope_done, s.count(0))
                    for n in range(2 * CU):
                        last = nc.tensor.transpose(bank(T_BANK, 2)[:, n * T:(n + 1) * T], qk[:, n * P:(n + 1) * P], ident)
                    last.then_inc(qk_turned, 1)
                if s.has(0):
                    pe.wait_ge(xnT_ready, s.seq(0) + 1)
                    if s.at_least(-2):
                        pe.wait_ge(residual, s.count(-2))
                    for a in range(2):
                        last = project(QK_BANK + a, slice(s.parity * FU, (s.parity + 1) * FU),
                                       wqk_hi[:, a], wqk_lo[:, a])
                    last.then_inc(qk_projected, 1)
                if s.has(1):
                    pe.wait_ge(qkT_ready, s.count(0))
                    if s.at_least(-1):
                        pe.wait_ge(exp_done, s.count(-1) * HPU)
                    for c in range(CU):
                        for a in range(2):
                            rows = slice(a * DK, (a + 1) * DK)
                            last = nc.tensor.matmul(bank(S_BANK + a)[:, c * T:(c + 1) * T], qkT[rows, 0, c, :],
                                                    qkT[rows, 1, c, :], start=True, stop=True)
                    last.then_inc(scored, 1)
                if s.has(2):
                    if s.has(1):
                        pe.wait_ge(qkT_ready, s.count(0))
                    for h in range(HPU):
                        if h % HB == 0:
                            pe.wait_ge(probs_ready, s.count(-2) * 2 + h // HB + 1)
                        last = nc.tensor.transpose(bank(T_BANK, 2)[:, h * T:(h + 1) * T], probs[:, h, :], ident)
                    last.then_inc(probs_turned, 1)
                if s.parity == 1 and (s.i is not None or s.base < UNITS - 1):
                    pe.wait_ge(rope_parts, s.count(1))
                    turn(s.seq(0) + 1)
                if s.has(0):
                    if s.at_least(0):
                        pe.wait_ge(v_ready, s.count(0))
                    else:
                        pe.wait_ge(lo_ready, 2)
                    for a in range(2):
                        last = project(V_BANK + a, slice((2 * s.parity + a) * BANK, (2 * s.parity + a + 1) * BANK),
                                       wvo_hi, wvo_lo)
                    last.then_inc(v_projected, 1)
                if s.has(2):
                    pe.wait_ge(probsT_ready, s.count(-1))
                    pe.wait_ge(v_ready, s.count(-1))
                    if s.has(0):
                        pe.wait_ge(rope_parts, s.count(1))
                    elif s.at_least(-2):
                        pe.wait_ge(residual, s.count(-2))
                    for n in range(HPU):
                        last = nc.tensor.matmul(bank(O_BANK)[:, 0:E], probsT[:, n, :], v[:, s.parity, n * E:(n + 1) * E],
                                                start=(n == 0), stop=(n == HPU - 1))
                    last.then_inc(projected, 1)

            for_slots(pe, step)

            pe.wait_ge(x_consts, 16 * 8)
            pe.wait_ge(residual, UNITS)

            def correlate(s):
                if s.has(0):
                    pe.wait_ge(ctx_a_ready, s.count(1))
                    pe.wait_ge(xn4_ready, s.count(1) * G)
                    if s.at_least(0):
                        pe.wait_ge(freq_ready, s.count(0))
                    for a, src in enumerate((xn4, ctx_a)):
                        for n in range(G):
                            last = nc.tensor.matmul(bank(a)[:, n * T:(n + 1) * T], src[:, n * E:(n + 1) * E], dft_fwd,
                                                    start=True, stop=True)
                    last.then_inc(freq_made, 1)
                if s.has(3):
                    pe.wait_ge(val_o_ready, s.count(-2))
                    pe.wait_ge(mixT_ready, s.count(-2))
                    for n in range(G):
                        last = nc.tensor.matmul(bank(7)[:, n * E:(n + 1) * E], mixT[:, n * T:(n + 1) * T],
                                                val_o[:, n * E:(n + 1) * E], start=True, stop=True)
                    last.then_inc(crossed, 1)
                if s.has(1):
                    pe.wait_ge(spec_ready, s.count(0))
                    if s.has(3):
                        pe.wait_ge(mixT_ready, s.count(-2))
                    for n in range(G):
                        last = nc.tensor.transpose(bank(4)[:, n * T:(n + 1) * T], spec[:, n * T:(n + 1) * T], ident)
                    last.then_inc(spec_turned, 1)
                if s.has(2):
                    pe.wait_ge(ctx_b_ready, s.count(-1))
                    if s.at_least(-2):
                        pe.wait_ge(ctx_o_ready, s.count(-2))
                    for n in range(G):
                        last = nc.tensor.matmul(bank(6)[:, n * E:(n + 1) * E], ctx_b[:, n * E:(n + 1) * E],
                                                xw[:, 3, :], start=True, stop=True)
                    last.then_inc(ctx_o_made, 1)
                if s.has(0):
                    pe.wait_ge(freq_ready, s.count(1))
                    if s.at_least(0):
                        pe.wait_ge(spec_ready, s.count(0))
                    for a in range(2):
                        last = nc.tensor.matmul(bank(2 + a), xw[:, a, :], freq[:, a, :], start=True, stop=True)
                    last.then_inc(hats_made, 1)
                if s.has(2):
                    pe.wait_ge(ctx_o_ready, s.count(-1))
                    if s.at_least(-2):
                        pe.wait_ge(residual2, s.count(-2))
                    nc.tensor.matmul(bank(7), xw[:, 2, :], ctx_o[:], start=True, stop=True).then_inc(val_o_made, 1)
                if s.has(1):
                    pe.wait_ge(specT_ready, s.count(0))
                    if s.at_least(-1):
                        pe.wait_ge(tops, s.count(-1) * (2 * G))
                    for n in range(G):
                        last = nc.tensor.matmul(bank(5)[:, n * T:(n + 1) * T], specT[:, n * T:(n + 1) * T], dft_inv,
                                                start=True, stop=True)
                    last.then_inc(corr_made, 1)
                if s.has(2):
                    pe.wait_ge(mix_ready, s.count(-1))
                    pe.wait_ge(specT_ready, s.count(0) if s.has(1) else GROUPS)
                    for n in range(G):
                        last = nc.tensor.transpose(bank(4)[:, n * T:(n + 1) * T],
                                                   mix[:, n].rearrange("p d h -> p (d h)"), ident)
                    last.then_inc(mix_turned, 1)

            for_groups(pe, correlate)

            pe.wait_ge(e_loaded, 16 * 4)
            pe.wait_ge(residual2, GROUPS)
            for g in range(GROUPS + 1):
                if g < GROUPS:
                    pe.wait_ge(xr_ready, (g + 1) * G)
                    if g >= 2:
                        pe.wait_ge(xrT_ready, g - 1)
                    for n in range(G):
                        b = g * G + n
                        last = nc.tensor.transpose(bank(g % 2)[:, n * T:(n + 1) * T], xr[:, b * E:(b + 1) * E], ident)
                    last.then_inc(xr_turned, 1)
                if g >= 1:
                    pe.wait_ge(xrT_ready, g)
                    for b in range((g - 1) * G, g * G):
                        nc.tensor.matmul(bank(6)[:, b * RP:b * RP + ROUTED], xrT[:, b * T:(b + 1) * T], router_sb[:],
                                         start=True, stop=True).then_inc(routed, 1)
            pe.wait_ge(w1_ready, 2)

            def shared(g, b):
                for m in range(SHARED):
                    for c in range(CH):
                        nc.tensor.matmul(bank(2 * m + c), w1_sb[:, ROUTED + m, c * P:(c + 1) * P],
                                         xrT[:, bass.ds(g * GT, GT)], start=True, stop=True).then_inc(hidden_made, 1)
                for m in range(SHARED):
                    for c in range(CH):
                        pe.wait_ge(hidden_ready, g * (SHARED * CH) + m * CH + c + 1)
                    for t in range(G):
                        for c in range(CH):
                            last = nc.tensor.matmul(bank(b)[:, t * E:(t + 1) * E], hT[:, m, c, t * T:(t + 1) * T],
                                                    w2_sb[:, ROUTED + m, c, :], start=(m == 0 and t == 0 and c == 0),
                                                    stop=(c == CH - 1), skip_group_check=True)
                last.then_inc(shared_made, 1)

            shared(0, 5)
            shared(1, 4)
            pe.wait_ge(chosen_ready, 1)
            rows = bank(7)[:, 0:B * ROUTED]
            rows_h = rows.rearrange("p (h f) -> p h f", h=2)
            chosen_h = chosen[:].rearrange("p (h b) n -> p h (b n)", h=2)
            nc.tensor.matmul(rows, before_h[:], chosen[:].rearrange("p b n -> p (b n)"), start=True, stop=True)
            for d in range(1, HALF):
                last = nc.tensor.matmul(rows_h[:, :, d * ROUTED:], ones_h[:], chosen_h[:, :, 0:(HALF - d) * ROUTED],
                                        start=False, stop=True, skip_group_check=True)
            last.then_inc(ranked, 1)
            for b in range(HALF):
                last = nc.tensor.matmul(bank(6)[:, 0:2 * ROUTED].rearrange("p (h e) -> p h e", h=2), ones_h[:],
                                        chosen_h[:, :, b * ROUTED:(b + 1) * ROUTED], start=(b == 0), stop=(b == HALF - 1))
            last.then_inc(ranked, 1)
            with pe.Fori(1, GROUPS // 2) as i:
                pe.wait_ge(shared_added, 2 * i - 1)
                shared(2 * i, 5)
                pe.wait_ge(shared_added, 2 * i)
                shared(2 * i + 1, 4)

            w1_flat = w1_sb[:].rearrange("p n f -> p (n f)")
            w2_flat = w2_sb[:].rearrange("p n c e -> p (n c e)")
            registers = [pe.alloc_register(f"w_offset_{k}") for k in range(LAG + TURN - 1)]

            def experts_of(first, count):
                pe.reg_load(registers[0:count], w_offset[0:1, bass.ds(first, count)])
                return [pe.snap(r, min_val=0, max_val=(ROUTED - 1) * HID) for r in registers[0:count]]

            def tile_slot(s, offsets):
                if s.has(0) or s.has(3):
                    if s.at_least(-2):
                        pe.wait_ge(tile_copied, s.count(-2))
                    if s.has(0):
                        if s.k % BATCH == 0:
                            pe.wait_ge(tile_loaded[s.k // BATCH], 16 * (s.turn + 1))
                        last = nc.tensor.transpose(bank(s.k % 3)[:, 0:P], x_tile[:, s.k, :], ident)
                    if s.has(3):
                        pe.wait_ge(tile_activated, s.count(-2))
                        for c in range(CH):
                            last = nc.tensor.transpose(bank(s.k % 3)[:, P + c * P:P + (c + 1) * P],
                                                       h_tile[:, s.k % 3, c * P:(c + 1) * P], ident)
                    last.then_inc(tile_turned, 1)
                if s.at_least(0):
                    pe.wait_ge(tile_copied, s.count(0) if s.has(0) or s.has(1) or s.has(2) or s.has(3) else ALL_TILES + 3)
                    if s.at_least(-3):
                        pe.wait_ge(tile_activated, s.count(-3))
                    if s.has(1):
                        last = nc.tensor.matmul(bank(3 + s.k % 3)[:, 0:HID], x_tileT[:, (s.k - 1) % 3, :],
                                                w1_flat[:, bass.ds(offsets[s.k + LAG - 1], HID)], start=True, stop=True)
                    if s.has(LAG):
                        for c in range(CH):
                            last = nc.tensor.matmul(bank(3 + s.k % 3)[:, HID:HID + E],
                                                    h_tileT[:, (s.k - LAG) % 3, c * P:(c + 1) * P],
                                                    w2_flat[:, bass.ds(offsets[s.k] + c * E, E)],
                                                    start=(c == 0), stop=(c == CH - 1), skip_group_check=True)
                    last.then_inc(tile_multiplied, 1)

            pe.wait_ge(plan_ready, 1)
            pe.wait_ge(shared_added, GROUPS)
            offsets = experts_of(0, LAG + TURN - 1)
            for k in range(TURN):
                tile_slot(Tile(k, 0), offsets)
            with pe.Fori(1, 2 * TURNS) as i:
                offsets = experts_of(i * TURN, LAG + TURN - 1)
                for k in range(TURN):
                    tile_slot(Tile(k, i), offsets)
            offsets = experts_of(ALL_TILES, LAG)
            for k in range(LAG):
                tile_slot(Tile(k, 2 * TURNS), offsets)


def _tables(np):
    f = np.float32
    ident = np.eye(P, dtype=f)
    mask = np.triu(np.full((P, P), MASKED, dtype=f), k=1)
    theta = (f(10000.0) ** (np.arange(0, DK, 2, dtype=f) / f(DK))).astype(f)
    freqs = np.arange(T, dtype=f)[:, None] * (f(1.0) / theta)[None, :]
    emb = np.concatenate([freqs, freqs], axis=-1)
    cos, sin = np.cos(emb).astype(f), np.sin(emb).astype(f)
    sin[:, 0::2] = -sin[:, 0::2]
    q_scale = f(DK ** -0.5)
    fold = np.eye(P, dtype=f)
    fold[E - 1, :] -= 1
    t = np.arange(T)
    k_re, k_im = np.arange(T // 2 + 1), np.arange(1, T // 2)
    turn = 2.0 * np.pi / T
    fwd = np.concatenate([np.cos(turn * np.outer(t, k_re) % (2 * np.pi)), -np.sin(turn * (np.outer(t, k_im) % T))], axis=1)
    fwd[:, :T // 2 + 1] = np.cos(turn * (np.outer(t, k_re) % T))
    weight = np.full(T, 2.0 / T)
    weight[0] = weight[T // 2] = 1.0 / T
    inv = fwd.T * weight[:, None]
    row = np.arange(P)
    same = (row[:, None] % H == row[None, :] % H)
    pos = np.zeros((P, P))
    pos[:, 0] = row // H + T
    pos[:, 1:1 + DH] = np.arange(DH)
    pos[:, 1 + RP:1 + RP + ROUTED] = np.arange(ROUTED)
    plan = np.zeros((P, 2 * P))
    plan[:, 0:ROUTED * ROUTED] = np.tril(np.ones((ROUTED, ROUTED)), k=-1).reshape(-1)
    plan[:, ROUTED * ROUTED:ROUTED * ROUTED + TILES] = np.arange(TILES) * P
    return np.concatenate([ident, mask, cos * q_scale, cos, sin * q_scale, sin, fold, fwd, inv, same, pos, plan],
                          axis=1).astype(f)


def kernel(**inputs):
    import numpy as np
    import concourse.bacc as bacc
    from concourse.bass_utils import run_bass_kernel_spmd

    layout = {k: np.ascontiguousarray(v) for k, v in inputs.items()}
    for k in ("L0_attn_wq", "L0_attn_wk", "L0_attn_wo"):
        layout[k] = np.ascontiguousarray(layout[k].T)
    for k in ("L0_xattn_wq", "L0_xattn_wk", "L0_xattn_wv"):
        layout[k] = np.ascontiguousarray(layout[k].reshape(E, H, DH).transpose(0, 2, 1).reshape(E, E))
    layout["consts"] = _tables(np)
    for name, routed, shared in (("rms", "L0_ffn_rms_w", "L0_ffn_rms_w_s"), ("w1", "L0_ffn_w1", "L0_ffn_w1_s"),
                                 ("w2", "L0_ffn_w2", "L0_ffn_w2_s")):
        layout[name] = np.concatenate([layout[routed], layout[shared]], axis=0)
    nc = bacc.Bacc("TRN2", target_bir_lowering=False, num_devices=1)
    names = ["x", "ctx_1024", "L0_attn_wq", "L0_attn_wk", "L0_attn_wv", "L0_attn_wo",
             "L0_attn_bq", "L0_attn_bk", "L0_attn_bv", "L0_attn_bo", "L0_xattn_wq", "L0_xattn_wk", "L0_xattn_wv", "L0_xattn_wo",
             "L0_ffn_router_w", "rms", "w1", "w2", "consts"]
    arrays, args = {}, []
    for name in names:
        a = layout[name]
        arrays[f"in_{name}"] = a
        args.append(nc.dram_tensor(f"in_{name}", a.shape, mybir.dt.from_np(a.dtype), kind="ExternalInput").ap())
    out = nc.dram_tensor("out_x", (B, T, E), F32, kind="ExternalOutput").ap()
    decoder_layer(nc, *args, out)
    r = run_bass_kernel_spmd(nc, [arrays], core_ids=[0])
    return r.results[0]["out_x"]
```

```python
from contextlib import ExitStack

import concourse.bass as bass
from concourse import mybir

ALU = mybir.AluOpType
ACT = mybir.ActivationFunctionType
AX_X = mybir.AxisListType.X
F32 = mybir.dt.float32
BF16 = mybir.dt.bfloat16
F32R = mybir.dt.float32r
U32 = mybir.dt.uint32

P = 128
B = 32
T = 128
E = 128
H = 16
DK = 64
HPU = H // 2
FU = HPU * DK
CU = FU // P
UNITS = 2 * B
BANK = 512
LN_EPS = 1e-5
MASKED = -1e30
DH = E // H
TOP = 4
G = 4
GROUPS = B // G
GT = G * T
HID = 256
CH = HID // P
ROUTED, SHARED = 14, 2
EXPERTS = ROUTED + SHARED
RMS_EPS = 1.1920929e-07
GATE_EPS = 1e-9
RP = 16
TOP_K = 2
HALF = B // 2
TILES = (HALF * T * TOP_K + ROUTED * (P - 1)) // P
BATCH = 3
RING = 3
TURN = BATCH * RING
TURNS = TILES // TURN
assert TILES == TURNS * TURN
ALL_TILES = 2 * TILES
LAG = 4
HALF_GROUPS = HALF // G
EARLY = HALF_GROUPS
FIRST_B = TURNS
CHUNKS = HALF // G


class Slot:

    def __init__(self, base, i=None):
        self.base, self.i, self.parity = base, i, base % 2

    def count(self, d):
        return self.base + d if self.i is None else self.base + d + 2 * self.i

    def at_least(self, d):
        return self.base + d > 0

    def has(self, lag):
        return self.i is not None or 0 <= self.base - lag < UNITS

    def seq(self, lag):
        return (self.base - lag) // 2 + (0 if self.i is None else self.i)


def for_slots(engine, step):
    for s in range(4):
        step(Slot(s))
    with engine.Fori(0, (UNITS - 6) // 2) as i:
        step(Slot(4, i))
        step(Slot(5, i))
    for s in range(UNITS - 2, UNITS + 2):
        step(Slot(s))


class Group:

    def __init__(self, base, i=None):
        self.base, self.i = base, i

    def count(self, d):
        return self.base + d if self.i is None else self.base + d + self.i

    def at_least(self, d):
        return self.base + d > 0

    def has(self, lag):
        return self.i is not None or 0 <= self.base - lag < GROUPS

    def tokens(self, lag):
        return bass.ds(self.count(-lag) * G * E, G * E)


def for_groups(engine, step, after={}):
    for s in range(3):
        step(Group(s))
    with engine.Fori(0, GROUPS - 4) as i:
        step(Group(3, i))
    for s in range(GROUPS - 1, GROUPS + 3):
        step(Group(s))
        if s in after:
            after[s]()


class Tile:

    def __init__(self, k, turn):
        self.k, self.turn, self.static = k, turn, isinstance(turn, int)

    def count(self, d):
        return self.k + d + TURN * self.turn

    def at_least(self, d):
        return not self.static or self.count(d) > 0

    def has(self, lag):
        return not self.static or 0 <= self.count(-lag) < ALL_TILES


def decoder_layer(nc, x, ctx_in, wqT, wkT, wv, woT, bq, bk, bv, bo, xwq, xwk, xwv, xwo,
                  router, rms_w, w1, w2, consts, out):
    with ExitStack() as ctx:
        def sb(name, shape, dt=F32):
            return ctx.enter_context(nc.sbuf_tensor(name, shape, dt))

        def sem(name):
            return ctx.enter_context(nc.semaphore(name))

        banks = ctx.enter_context(nc.psum_tensor("banks", [P, 8 * BANK], F32))

        def bank(b, n=1, lo=0, hi=None):
            return banks[:, b * BANK + lo:(b + n - 1) * BANK + (BANK if hi is None else hi)]

        xs = sb("xs", [P, B * E])
        cst = sb("cst", [P, 4 * P])
        ident = cst[:, 0:128]
        mask_f = cst[:, 128:256]
        cos_c = cst[:, 256:384].rearrange("p (a d) -> p a d", a=2)
        sin_c = cst[:, 384:512].rearrange("p (a d) -> p a d", a=2)
        bn = sb("bn", [P, B, 6])
        mean = sb("mean", [P, B])
        rstd = sb("rstd", [P, B])
        tmp_m = sb("tmp_m", [P, B])
        tmp_v = sb("tmp_v", [P, B])
        shift = sb("shift", [P, B])

        wqk, wvo = sb("wqk", [P, 2, 2, H * DK], F32R), sb("wvo", [P, 2, H * E], F32R)
        wqk_hi, wqk_lo, wvo_hi, wvo_lo = wqk[:, 0], wqk[:, 1], wvo[:, 0], wvo[:, 1]
        bv_col = sb("bv_col", [P, H * DK // P])
        cos_sb = sb("cos_sb", [P, 2, HPU, DK])
        sin_sb = sb("sin_sb", [P, 2, HPU, DK])
        out_bias = sb("out_bias", [P, E])
        xn = sb("xn", [P, E])
        xnT_hi, xnT_lo = sb("xnT_hi", [P, T], F32R), sb("xnT_lo", [P, T], F32R)
        rope_c = sb("rope_c", [P, 2 * FU])
        rope_s = sb("rope_s", [P, 2 * FU])
        qk = sb("qk", [P, 2 * FU])
        qkT = sb("qkT", [P, 2, CU, T])
        negmax = sb("negmax", [P, HPU])
        heads_sb = sb("heads_sb", [P, 4 * HPU * T])
        v = heads_sb[:, 0:2 * HPU * E].rearrange("p (a f) -> p a f", a=2)
        last_w = heads_sb[:, 0:2 * H * DK].rearrange("p (a f) -> p a f", a=2)
        probs = heads_sb[:, 2 * HPU * T:3 * HPU * T].rearrange("p (h t) -> p h t", h=HPU)
        probsT = heads_sb[:, 3 * HPU * T:4 * HPU * T].rearrange("p (h t) -> p h t", h=HPU)
        sums = sb("sums", [P, HPU])
        rsums = sb("rsums", [P, HPU])

        dft = sb("dft", [P, 2 * P])
        dft_fwd, dft_inv = dft[:, 0:P], dft[:, P:2 * P]
        same_head = sb("same_head", [P, P])
        pos_c = sb("pos_c", [P, 1 + 2 * RP])
        head_pos, iota8, iota14 = pos_c[:, 0:1], pos_c[:, 1:1 + DH], pos_c[:, 1 + RP:1 + RP + ROUTED]
        xw = sb("xw", [P, 4, E])
        cs = sb("cs", [P, B * E])
        corr_sb = sb("corr_sb", [P, 9 * GT])
        ctx_a, ctx_b, xn4, khat, spec, specT, ctx_o, val_o, mixT = (corr_sb[:, n * GT:(n + 1) * GT] for n in range(9))
        freq = sb("freq", [P, 2, GT])
        cross_a, cross_b = sb("cross_a", [P, G, DK - 1]), sb("cross_b", [P, G, DK - 1])
        top_v, top_i = sb("top_v", [P, G, 8]), sb("top_i", [P, G, 8], U32)
        top_e, top_s, top_r = sb("top_e", [P, G, TOP]), sb("top_s", [P, G]), sb("top_r", [P, G])
        lag_n, lag_m = sb("lag_n", [P, G, TOP], U32), sb("lag_m", [P, G, TOP], U32)
        wait_pad = sb("wait_pad", [P, 1])
        onehot = sb("onehot", [P, G * TOP, DH])
        mix_row = sb("mix_row", [P, G, DH])
        mix = sb("mix", [P, G, DH, H])

        w1_sb, w2_sb = sb("w1_sb", [P, EXPERTS, HID]), sb("w2_sb", [P, EXPERTS, CH, E])
        stage = w1_sb[:].rearrange("p n h -> p (n h)").rearrange("p (k f) -> p k f", k=4)
        wq_raw, wk_raw, qk_raw = stage[:, 0], stage[:, 1], stage[:, 0:2].rearrange("p a f -> p (a f)")
        wv_raw = stage[:, 2].rearrange("p (c e) -> p c e", e=E)
        wo_raw = stage[:, 3].rearrange("p (c o) -> p c o", o=E)
        rmsT = sb("rmsT", [P, EXPERTS])
        router_sb = sb("router_sb", [P, ROUTED])
        rms, scale3 = sb("rms", [P, B]), sb("scale3", [P, B])
        xr = heads_sb
        back = heads_sb
        xrT = cs
        gates = sb("gates", [P, B, ROUTED])
        plan_c = sb("plan_c", [P, 2 * P])
        before_e = plan_c[:, 0:ROUTED * ROUTED].rearrange("p (e a) -> p e a", a=ROUTED)
        tile_start = plan_c[:, ROUTED * ROUTED:ROUTED * ROUTED + TILES]
        zeros = sb("zeros", [P, E])
        before_h, ones_h = sb("before_h", [P, P], BF16), sb("ones_h", [P, P], BF16)
        chosen = sb("chosen", [P, B, ROUTED], BF16)
        spare = [rope_c, rope_s]
        picks = [t[:, 0:B * ROUTED].rearrange("p (b n) -> p b n", n=ROUTED) for t in spare]
        place = qk[:, 0:B * ROUTED].rearrange("p (b n) -> p b n", n=ROUTED)
        spread_e = qk[:, BANK:BANK + ROUTED * ROUTED].rearrange("p (e a) -> p e a", a=ROUTED)
        past = cos_sb[:].rearrange("p a h d -> p (a h d)")
        count_n, count_m = sb("count_n", [P, ROUTED], U32), sb("count_m", [P, ROUTED], U32)
        begin, end = sb("begin", [P, ROUTED]), sb("end", [P, ROUTED])
        var_e, shift3 = sb("var_e", [P, B]), sb("shift3", [P, B])
        dest_f, dest = sb("dest_f", [P, TOP_K, B]), sb("dest", [P, TOP_K, B], U32)
        tile_e = sb("tile_e", [1, ALL_TILES])
        w_offset = sb("w_offset", [1, LAG + ALL_TILES + LAG], U32)
        x_tile = corr_sb[:, 0:TURN * E].rearrange("p (n e) -> p n e", e=E)
        y_tile = corr_sb[:, TURN * E:2 * TURN * E].rearrange("p (n e) -> p n e", e=E)
        tile_sb = corr_sb[:, 2 * TURN * E:2 * TURN * E + 3 * (P + 2 * HID)]
        x_tile_hi, x_tile_lo = sb("x_tile_hi", [P, 3, P], F32R), sb("x_tile_lo", [P, 3, P], F32R)
        W1_COLS = ROUTED * HID
        w1_hi = wqk[:].rearrange("p n a f -> p (n a f)")[:, 0:W1_COLS]
        w1_lo = wvo[:].rearrange("p n f -> p (n f)")[:, 0:W1_COLS]
        h_tile = tile_sb[:, 3 * P:3 * (P + HID)].rearrange("p (r f) -> p r f", r=3)
        h_tileT = tile_sb[:, 3 * (P + HID):].rearrange("p (r f) -> p r f", r=3)
        x_rows = [nc.dram_tensor(f"x_rows_{h}", (TILES * P, E), F32, kind="Internal").ap() for h in range(2)]
        y_rows = [nc.dram_tensor(f"y_rows_{h}", (TILES * P, E), F32, kind="Internal").ap() for h in range(2)]
        best_v, best_i = sb("best_v", [P, B, 8]), sb("best_i", [P, B, 8], U32)
        best_n = sb("best_n", [P, B, 2])
        row_max, row_sum = sb("row_max", [P, B]), sb("row_sum", [P, B])
        hT = sb("hT", [P, 2, CH, GT])

        x_consts, ctx_loaded, e_loaded = sem("x_consts"), sem("ctx_loaded"), sem("e_loaded")
        ctx_a_ready, ctx_b_ready = sem("ctx_a_ready"), sem("ctx_b_ready")
        stats2, stats3 = sem("stats2"), sem("stats3")
        var2_ready, std2_ready, xn4_ready = sem("var2_ready"), sem("std2_ready"), sem("xn4_ready")
        freq_made, freq_ready = sem("freq_made"), sem("freq_ready")
        hats_made, khat_ready, spec_ready = sem("hats_made"), sem("khat_ready"), sem("spec_ready")
        spec_turned, specT_ready = sem("spec_turned"), sem("specT_ready")
        corr_made, shifted, top_exp = sem("corr_made"), sem("shifted"), sem("top_exp")
        mix_ready, ctx_o_made, ctx_o_ready = sem("mix_ready"), sem("ctx_o_made"), sem("ctx_o_ready")
        val_o_made, val_o_ready = sem("val_o_made"), sem("val_o_ready")
        mix_turned, mixT_ready = sem("mix_turned"), sem("mixT_ready")
        shift_ready, shift3_ready = sem("shift_ready"), sem("shift3_ready")
        xr_even_ready, xr_odd_ready = sem("xr_even_ready"), sem("xr_odd_ready")
        tops, mixed, spec_step = sem("tops"), sem("mixed"), sem("spec_step")
        crossed, residual2 = sem("crossed"), sem("residual2")
        var3_ready, std3_ready, ms_ready, rms_ready = sem("var3_ready"), sem("std3_ready"), sem("ms_ready"), sem("rms_ready")
        w1_ready, xr_turned, xrT_ready = sem("w1_ready"), sem("xr_turned"), sem("xrT_ready")
        routed, logits_shifted, gates_exp = sem("routed"), sem("logits_shifted"), sem("gates_exp")
        hidden_made, hidden_ready = sem("hidden_made"), sem("hidden_ready")
        shared_made, shared_added = sem("shared_made"), sem("shared_added")
        zeros_set, rows_cleared = sem("zeros_set"), sem("rows_cleared")
        chosen_ready, ranked, dest_ready, plan_ready = sem("chosen_ready"), sem("ranked"), sem("dest_ready"), sem("plan_ready")
        scattered = [sem(f"scattered_{h}") for h in range(2)]
        tile_loaded = [sem(f"tile_loaded_{r}") for r in range(RING)]
        tile_stored = [sem(f"tile_stored_{r}") for r in range(RING)]
        tile_turned, tile_copied = sem("tile_turned"), sem("tile_copied")
        tile_multiplied, tile_activated = sem("tile_multiplied"), sem("tile_activated")
        gathered_a = sem("gathered_a")
        gathered_b = [sem(f"gathered_b_{c}") for c in range(CHUNKS)]
        combined, w1_split, tile_hi = sem("combined"), sem("w1_split"), sem("tile_hi")
        X_PIECES = 4
        x_loaded = [sem(f"x_loaded_{n}") for n in range(X_PIECES)]
        c_loaded, tables_ready = sem("c_loaded"), sem("tables_ready")
        qk_loaded, vo_loaded, b_loaded = sem("qk_loaded"), sem("vo_loaded"), sem("b_loaded")
        dve_step = sem("dve_step")
        var_ready, std_ready = sem("var_ready"), sem("std_ready")
        qk_folded, wv_ready, vo_folded = sem("qk_folded"), sem("wv_ready"), sem("vo_folded")
        hi_ready, lo_ready = sem("hi_ready"), sem("lo_ready")
        x_biased, ones_set = sem("x_biased"), sem("ones_set")
        xn_ready, xn_turned, xnT_ready = sem("xn_ready"), sem("xn_turned"), sem("xnT_ready")
        xnT_step = sem("xnT_step")
        qk_projected, rope_parts, rope_done = sem("qk_projected"), sem("rope_parts"), sem("rope_done")
        qk_turned, qkT_ready = sem("qk_turned"), sem("qkT_ready")
        masked = sem("masked")
        scored, max_ready, exp_done = sem("scored"), sem("max_ready"), sem("exp_done")
        rsum_ready, probs_ready = sem("rsum_ready"), sem("probs_ready")
        probs_turned, probsT_ready = sem("probs_turned"), sem("probsT_ready")
        v_projected, v_ready = sem("v_projected"), sem("v_ready")
        projected, residual = sem("projected"), sem("residual")
        stored = sem("stored")

        QK_BANK, T_BANK, S_BANK, V_BANK = 0, 2, 4, 6
        O_BANK, XN_BANK = QK_BANK, QK_BANK + 1
        T_BANKS, L_BANKS = ((0, 1), (6,)), (5, 7)
        HB = HPU // 2
        XB = B // X_PIECES

        block = ctx.enter_context(nc.Block())

        @block.sync
        def _(sp):
            sp.dma_start(cst[:], consts[:, 0:4 * P]).then_inc(c_loaded, 16)
            for a, (w, bias) in enumerate(((wqT, bq), (wkT, bk))):
                sp.dma_start(last_w[0:E - 1, a, :], w[E - 1:E, :].broadcast_to([E - 1, H * DK])).then_inc(qk_loaded, 16)
                sp.dma_start(stage[E - 1:E, a, :], bias.unsqueeze(0)).then_inc(qk_loaded, 16)
            for n in range(X_PIECES):
                if n == 1:
                    sp.dma_start(wv_raw, wv.rearrange("(c p) e -> p c e", p=P)).then_inc(vo_loaded, 16)
                    sp.dma_start(wo_raw, woT.rearrange("(c p) o -> p c o", p=P)).then_inc(vo_loaded, 16)
                sp.dma_start(xs[:, n * XB * E:(n + 1) * XB * E].rearrange("t (b e) -> t b e", b=XB),
                             x[n * XB:(n + 1) * XB].rearrange("b t e -> t b e")).then_inc(x_loaded[n], 16)
            sp.dma_start(dft[:], consts[:, 4 * P:6 * P]).then_inc(x_consts, 16)
            sp.dma_start(same_head[:], consts[:, 6 * P:7 * P]).then_inc(x_consts, 16)
            sp.dma_start(pos_c[:], consts[:, 7 * P:7 * P + 1 + 2 * RP]).then_inc(x_consts, 16)
            sp.dma_start(plan_c[:], consts[:, 8 * P:10 * P]).then_inc(x_consts, 16)
            for n, w in enumerate((xwq, xwk, xwv, xwo)):
                sp.dma_start(xw[:, n, :], w).then_inc(x_consts, 16)
            sp.dma_start(cs[:].rearrange("t (b e) -> t b e", b=B), ctx_in.rearrange("b t e -> t b e")).then_inc(ctx_loaded, 16)
            sp.wait_ge(vo_folded, 1)
            sp.wait_ge(lo_ready, 1)
            sp.dma_start(w1_sb[:], w1.rearrange("n e h -> e n h")).then_inc(e_loaded, 16)
            sp.dma_start(w2_sb[:], w2.rearrange("n (c p) e -> p n c e", p=P)).then_inc(e_loaded, 16)
            with nc.allow_non_contiguous_dma(reason="one weight per partition and expert"):
                sp.dma_start(rmsT[:], rms_w.rearrange("n e -> e n")).then_inc(e_loaded, 16)
            sp.dma_start(router_sb[:], router).then_inc(e_loaded, 16)
            sp.wait_ge(zeros_set, 1)
            for rows in x_rows:
                sp.dma_start(rows.rearrange("(n p) e -> p n e", p=P),
                             zeros[:].unsqueeze(1).broadcast_to([P, TILES, E])).then_inc(rows_cleared, 16)

            def load(half, local, r):
                sp.dma_start(x_tile[:, r * BATCH:(r + 1) * BATCH, :],
                             x_rows[half][bass.ds((local * TURN + r * BATCH) * P, BATCH * P), :]
                             .rearrange("(n p) e -> p n e", p=P)).then_inc(tile_loaded[r], 16)

            def store(half, local, r):
                sp.dma_start(y_rows[half][bass.ds((local * TURN + r * BATCH) * P, BATCH * P), :]
                             .rearrange("(n p) e -> p n e", p=P),
                             y_tile[:, r * BATCH:(r + 1) * BATCH, :]).then_inc(tile_stored[r], 16)

            for half in range(2):
                first = half * FIRST_B
                sp.wait_ge(scattered[half], 16 * TOP_K * HALF)
                for r in range(RING):
                    if half == 1:
                        sp.wait_ge(tile_turned, (first - 1) * TURN + (r + 1) * BATCH)
                    load(half, 0, r)
                    if half == 1:
                        sp.wait_ge(tile_activated, (first - 1) * TURN + (r + 1) * BATCH + LAG - 1)
                        store(0, TURNS - 1, r)
                with sp.Fori(1, TURNS) as i:
                    for r in range(RING):
                        sp.wait_ge(tile_turned, (i + first - 1) * TURN + (r + 1) * BATCH)
                        load(half, i, r)
                        sp.wait_ge(tile_activated, (i + first - 1) * TURN + (r + 1) * BATCH + LAG - 1)
                        store(half, i - 1, r)
            for r in range(RING):
                sp.wait_ge(tile_activated, (2 * TURNS - 1) * TURN + (r + 1) * BATCH + LAG - 1)
                store(1, TURNS - 1, r)
            for g in range(GROUPS):
                sp.wait_ge(shared_added, g + 1)
                sp.wait_ge(combined, (g + 1) * TOP_K * G)
                sp.dma_start(out[g * G:(g + 1) * G].rearrange("b t e -> t b e"),
                             xs[:, g * G * E:(g + 1) * G * E].rearrange("t (b e) -> t b e", b=G)).then_inc(stored, 16)
            sp.wait_ge(stored, 16 * GROUPS)

        @block.gpsimd
        def _(pool):
            nc.gpsimd.memset(zeros[:], 0.0).then_inc(zeros_set, 1)
            pool.wait_ge(c_loaded, 16)
            for a in range(2):
                nc.gpsimd.tensor_copy(cos_sb[:, a], cos_c[:, a].unsqueeze(1).broadcast_to([P, HPU, DK]))\
                    .then_inc(tables_ready, 1)
                nc.gpsimd.tensor_copy(sin_sb[:, a], sin_c[:, a].unsqueeze(1).broadcast_to([P, HPU, DK]))\
                    .then_inc(tables_ready, 1)

            def step(s):
                if s.has(0):
                    if s.parity == 0:
                        pool.wait_ge(xn_ready, s.seq(0) + 1)
                        if s.i is None and s.base == 0:
                            pool.wait_ge(b_loaded, 16 * 2)
                        xb = xs[:, bass.ds(s.seq(0) * E, E)]
                        nc.gpsimd.tensor_tensor(xb, xb, out_bias[:], ALU.add).then_inc(x_biased, 1)
                    pool.wait_ge(rope_parts, s.count(1))
                    nc.gpsimd.tensor_tensor(qk[:], rope_c[:], rope_s[:], ALU.add).then_inc(rope_done, 1)

            for_slots(pool, step)

            pool.wait_ge(ctx_loaded, 16)

            def copies(s):
                if s.has(0):
                    if s.at_least(0):
                        pool.wait_ge(freq_made, s.count(0))
                    nc.gpsimd.tensor_copy(ctx_a[:], cs[:, s.tokens(0)]).then_inc(ctx_a_ready, 1)
                    if s.i is None and s.base < 2:
                        if s.base == 0:
                            pool.wait_ge(e_loaded, 16 * 4)
                        n = slice(s.base * EXPERTS // 2, (s.base + 1) * EXPERTS // 2)
                        nc.gpsimd.tensor_tensor(w1_sb[:, n, :], w1_sb[:, n, :],
                                                rmsT[:, n].unsqueeze(2).broadcast_to([P, EXPERTS // 2, HID]), ALU.mult)\
                            .then_inc(w1_ready, 1)
                if s.has(2):
                    if s.at_least(-2):
                        pool.wait_ge(ctx_o_made, s.count(-2))
                    nc.gpsimd.tensor_copy(ctx_b[:], cs[:, s.tokens(2)]).then_inc(ctx_b_ready, 1)

            for_groups(pool, copies)

            w1_flat = w1_sb[:].rearrange("p n f -> p (n f)")[:, 0:W1_COLS]
            pool.wait_ge(w1_ready, 2)
            nc.gpsimd.tensor_copy(w1_hi, w1_flat).then_inc(w1_split, 1)
            pool.wait_ge(w1_split, 1)
            nc.gpsimd.tensor_tensor(w1_lo, w1_flat, w1_hi.bitcast(F32), ALU.subtract).then_inc(w1_split, 1)

            pool.wait_ge(rows_cleared, 16 * 2)
            for half in range(2):
                pool.wait_ge(dest_ready, half + 1)
                for b in range(half * HALF, (half + 1) * HALF):
                    for k in range(TOP_K):
                        nc.gpsimd.indirect_dma_start(
                            out=x_rows[half], out_offset=bass.IndirectOffsetOnAxis(ap=dest[:, k, b:b + 1], axis=0),
                            in_=xr[:, b * E:(b + 1) * E], in_offset=None).then_inc(scattered[half], 16)
            pool.wait_ge(scattered[0], 16 * TOP_K * HALF)
            pool.wait_ge(scattered[1], 16 * TOP_K * HALF)
            for half in range(2):
                for r in range(RING):
                    pool.wait_ge(tile_stored[r], 16 * TURNS * (half + 1))
                for c in range(CHUNKS):
                    if half == 1:
                        pool.wait_ge(combined, (c + 1) * TOP_K * G)
                    for k in range(TOP_K):
                        for n in range(G):
                            b = half * HALF + c * G + n
                            m = (c * TOP_K + k) * G + n
                            nc.gpsimd.indirect_dma_start(
                                out=back[:, m * E:(m + 1) * E], out_offset=None, in_=y_rows[half],
                                in_offset=bass.IndirectOffsetOnAxis(ap=dest[:, k, b:b + 1], axis=0))\
                                .then_inc(gathered_b[c] if half == 1 else gathered_a, 16)
                    if half == 0:
                        pool.wait_ge(gathered_a, 16 * TOP_K * G * (c + 1))

        @block.scalar
        def _(act):
            act.dma_start(wq_raw[0:E - 1, :], wqT[0:E - 1, :]).then_inc(qk_loaded, 16)
            act.dma_start(wk_raw[0:E - 1, :], wkT[0:E - 1, :]).then_inc(qk_loaded, 16)
            act.dma_start(out_bias[:], bo.unsqueeze(0).broadcast_to([P, E])).then_inc(b_loaded, 16)
            with nc.allow_non_contiguous_dma(reason="one bias value per partition"):
                act.dma_start(bv_col[:], bv.rearrange("(c p) -> p c", p=P)).then_inc(b_loaded, 16)
            act.wait_ge(qk_folded, 1)
            nc.scalar.activation(wqk_hi.rearrange("p a f -> p (a f)"), qk_raw, ACT.Copy).then_inc(hi_ready, 1)
            act.wait_ge(var_ready, 1)
            nc.scalar.activation(tmp_v[:, 0:XB], tmp_v[:, 0:XB], ACT.Sqrt).then_inc(std_ready, 1)
            act.wait_ge(vo_folded, 1)
            nc.scalar.activation(wvo_hi, bank(4, 4), ACT.Copy).then_inc(hi_ready, 1)

            def step(s):
                if s.i is None and s.base == 2:
                    act.wait_ge(var_ready, 2)
                    nc.scalar.activation(tmp_v[:, XB:], tmp_v[:, XB:], ACT.Sqrt).then_inc(std_ready, 1)
                if s.has(1):
                    act.wait_ge(qk_turned, s.count(0))
                    nc.scalar.activation(qkT[:].rearrange("p a c t -> p (a c t)"), bank(T_BANK, 2), ACT.Copy)\
                        .then_inc(qkT_ready, 1)
                    act.wait_ge(v_projected, s.count(0))
                    nc.scalar.activation(v[:, 1 - s.parity, :], bank(V_BANK, 2), ACT.Copy).then_inc(v_ready, 1)
                if s.has(2):
                    act.wait_ge(probs_turned, s.count(-1))
                    nc.scalar.activation(probsT.rearrange("p h t -> p (h t)"), bank(T_BANK, 2), ACT.Copy)\
                        .then_inc(probsT_ready, 1)
                if s.has(1):
                    for h in range(HPU):
                        if h % HB == 0:
                            act.wait_ge(max_ready, s.count(-1) * 2 + h // HB + 1)
                        nc.scalar.activation(probs[:, h, :], bank(S_BANK, 2)[:, h * T:(h + 1) * T], ACT.Exp,
                                             bias=negmax[:, h:h + 1], accum_out=sums[:, h:h + 1])\
                            .then_inc(exp_done, 1)

            for_slots(act, step)

            act.wait_ge(var2_ready, 1)
            nc.scalar.activation(tmp_v[:, 0:B - G], tmp_v[:, 0:B - G], ACT.Sqrt).then_inc(std2_ready, 1)

            def normalise4(s, lag):
                for n in range(G):
                    b = s.count(-lag) * G + n
                    nc.scalar.activation(xn4[:, n * E:(n + 1) * E], xs[:, bass.ds(b * E, E)], ACT.Identity,
                                         bias=shift[:, bass.ds(b, 1)], scale=rstd[:, bass.ds(b, 1)]).then_inc(xn4_ready, 1)

            act.wait_ge(shift_ready, 1)
            normalise4(Group(0), 0)
            act.wait_ge(var2_ready, 2)
            nc.scalar.activation(tmp_v[:, B - G:B], tmp_v[:, B - G:B], ACT.Sqrt).then_inc(std2_ready, 1)
            act.wait_ge(shift_ready, 2)

            def correlate(s):
                if s.has(0):
                    act.wait_ge(freq_made, s.count(1))
                    nc.scalar.activation(freq[:].rearrange("p a t -> p (a t)"), bank(0, 2), ACT.Copy).then_inc(freq_ready, 1)
                if s.has(1):
                    act.wait_ge(spec_turned, s.count(0))
                    nc.scalar.activation(specT[:], bank(4), ACT.Copy).then_inc(specT_ready, 1)
                if s.has(2):
                    act.wait_ge(ctx_o_made, s.count(-1))
                    nc.scalar.activation(ctx_o[:], bank(6), ACT.Copy).then_inc(ctx_o_ready, 1)
                if s.has(-1) and s.base != GROUPS - 1:
                    normalise4(s, -1)
                if s.has(0):
                    act.wait_ge(hats_made, s.count(1))
                    nc.scalar.activation(khat[:], bank(3), ACT.Copy).then_inc(khat_ready, 1)
                if s.has(2):
                    act.wait_ge(val_o_made, s.count(-1))
                    nc.scalar.activation(val_o[:], bank(7), ACT.Copy).then_inc(val_o_ready, 1)
                    act.wait_ge(mix_turned, s.count(-1))
                    nc.scalar.activation(mixT[:], bank(4), ACT.Copy).then_inc(mixT_ready, 1)
                if s.has(1):
                    act.wait_ge(shifted, s.count(0))
                    nc.scalar.activation(top_e[:], top_e[:], ACT.Exp).then_inc(top_exp, 1)

            def deviations(h):
                b = slice(h * HALF, (h + 1) * HALF)
                act.wait_ge(var3_ready, h + 1)
                nc.scalar.activation(tmp_v[:, b], tmp_v[:, b], ACT.Sqrt).then_inc(std3_ready, 1)
                act.wait_ge(ms_ready, h + 1)
                nc.scalar.activation(rms[:, b], rms[:, b], ACT.Sqrt).then_inc(rms_ready, 1)

            def scale_odd(h):
                act.wait_ge(shift3_ready, h + 1)
                for g in range(h * HALF_GROUPS + 1, (h + 1) * HALF_GROUPS, 2):
                    for n in range(g * G, (g + 1) * G):
                        nc.scalar.activation(xr[:, n * E:(n + 1) * E], xs[:, n * E:(n + 1) * E], ACT.Identity,
                                             bias=shift3[:, n:n + 1], scale=scale3[:, n:n + 1]).then_inc(xr_odd_ready, 1)

            def copy_turned(h):
                act.wait_ge(ctx_b_ready, (h + 1) * HALF_GROUPS)
                for g in range(h * HALF_GROUPS, (h + 1) * HALF_GROUPS):
                    act.wait_ge(xr_turned, g + 1)
                    nc.scalar.activation(xrT[:, g * GT:(g + 1) * GT], bank(T_BANKS[h][g % len(T_BANKS[h])]), ACT.Copy)\
                        .then_inc(xrT_ready, 1)

            def exp_logits(h):
                b = slice(h * HALF, (h + 1) * HALF)
                act.wait_ge(logits_shifted, h + 1)
                nc.scalar.activation(gates[:, b], gates[:, b], ACT.Exp).then_inc(gates_exp, 1)

            def shared_silu(g):
                for m in range(SHARED):
                    for c in range(CH):
                        act.wait_ge(hidden_made, g * (SHARED * CH) + m * CH + c + 1)
                        nc.scalar.activation(hT[:, m, c, :], bank(2 * m + c), ACT.Silu).then_inc(hidden_ready, 1)

            for_groups(act, correlate, {GROUPS: lambda: deviations(0), GROUPS + 1: lambda: scale_odd(0)})
            copy_turned(0)
            exp_logits(0)
            shared_silu(0)
            deviations(1)
            shared_silu(1)
            scale_odd(1)
            copy_turned(1)
            exp_logits(1)
            shared_silu(2)
            shared_silu(3)

            def tile_slot(s):
                if s.at_least(0):
                    act.wait_ge(tile_multiplied, s.count(0))
                    src = bank(3 + s.k % 3)
                    if s.has(1):
                        last = nc.scalar.activation(h_tile[:, (s.k - 1) % 3, :], src[:, 0:HID], ACT.Silu)
                    if s.has(LAG):
                        k = (s.k - LAG) % TURN
                        turn = s.turn if s.k >= LAG else s.turn - 1
                        if k % BATCH == 0 and not (s.static and turn < 1):
                            act.wait_ge(tile_stored[k // BATCH], 16 * turn)
                        last = nc.scalar.activation(y_tile[:, k, :], src[:, HID:HID + E], ACT.Copy)
                    last.then_inc(tile_activated, 1)

            for k in range(TURN):
                tile_slot(Tile(k, 0))
            for k in range(TURN):
                tile_slot(Tile(k, 1))
            with act.Fori(2, 2 * TURNS) as i:
                for k in range(TURN):
                    tile_slot(Tile(k, i))
            for k in range(LAG):
                tile_slot(Tile(k, 2 * TURNS))
            with act.Fori(EARLY, GROUPS) as g:
                shared_silu(g)

        @block.vector
        def _(dve):
            steps = [0]

            def then(ins):
                steps[0] += 1
                ins.then_inc(dve_step, 1)
                dve.wait_ge(dve_step, steps[0])

            def moments(b=slice(0, B)):
                even, odd = bn[:, b, 1], bn[:, b, 4]
                m, v = tmp_m[:, b], tmp_v[:, b]
                then(nc.vector.tensor_tensor(mean[:, b], even, odd, ALU.add))
                then(nc.vector.tensor_scalar(mean[:, b], mean[:, b], 0.5, None, ALU.mult))
                then(nc.vector.tensor_tensor(m, even, odd, ALU.subtract))
                then(nc.vector.tensor_tensor(m, m, m, ALU.mult))
                then(nc.vector.tensor_tensor(v, bn[:, b, 2], bn[:, b, 5], ALU.add))
                then(nc.vector.tensor_scalar(v, v, 1.0 / E, None, ALU.mult))
                then(nc.vector.scalar_tensor_tensor(v, m, 0.25, v, ALU.mult, ALU.add))

            nc.vector.memset(xnT_hi[:].bitcast(F32), 1.0).then_inc(ones_set, 1)
            nc.vector.memset(xnT_lo[:].bitcast(F32), 0.0).then_inc(ones_set, 1)
            dve.wait_ge(qk_loaded, 16 * 6)
            rows = slice(0, E - 1)
            nc.vector.tensor_tensor(stage[rows, 0:2], stage[rows, 0:2], last_w[rows], ALU.subtract).then_inc(qk_folded, 1)

            def sequences_stats(b):
                for n in range(b.start, b.stop):
                    if n % XB == 0:
                        dve.wait_ge(x_loaded[n // XB], 16)
                    last = nc.vector.bn_stats(bn[:, n, :], xs[:, n * E:(n + 1) * E])
                then(last)

            def variances(b):
                moments(b)
                nc.vector.tensor_scalar(tmp_v[:, b], tmp_v[:, b], LN_EPS, None, ALU.add).then_inc(var_ready, 1)

            first, rest = slice(0, XB), slice(XB, B)
            sequences_stats(first)
            variances(first)
            dve.wait_ge(hi_ready, 1)
            nc.vector.tensor_tensor(wqk_lo.rearrange("p a f -> p (a f)"), qk_raw,
                                    wqk_hi.rearrange("p a f -> p (a f)").bitcast(F32), ALU.subtract).then_inc(lo_ready, 1)
            dve.wait_ge(std_ready, 1)
            then(nc.vector.reciprocal(rstd[:, first], tmp_v[:, first]))

            def normalise(b):
                nc.vector.tensor_scalar(xn[:], xs[:, bass.ds(b * E, E)], mean[:, bass.ds(b, 1)],
                                        rstd[:, bass.ds(b, 1)], ALU.subtract, ALU.mult).then_inc(xn_ready, 1)

            def split_xnT(b):
                dve.wait_ge(xn_turned, b + 1)
                rows = slice(0, E - 1)
                nc.vector.tensor_copy(xnT_hi[rows, :], bank(XN_BANK)[rows, 0:T]).then_inc(xnT_step, 1)
                dve.wait_ge(xnT_step, b + 1)
                nc.vector.tensor_tensor(xnT_lo[rows, :], bank(XN_BANK)[rows, 0:T], xnT_hi[rows, :].bitcast(F32),
                                        ALU.subtract).then_inc(xnT_ready, 1)

            normalise(0)
            dve.wait_ge(b_loaded, 16 * 2)
            dve.wait_ge(vo_loaded, 16 * 2)
            last = wv_raw[:, :, E - 1:E]
            then(nc.vector.tensor_tensor(wv_raw[:, :, 0:E - 1], wv_raw[:, :, 0:E - 1],
                                         last.broadcast_to([P, H * DK // P, E - 1]), ALU.subtract))
            nc.vector.tensor_copy(wv_raw[:, :, E - 1], bv_col[:]).then_inc(wv_ready, 1)
            dve.wait_ge(ones_set, 2)
            split_xnT(0)

            def normalise_probs(s, lag, a):
                dve.wait_ge(exp_done, s.count(-lag) * HPU + (a + 1) * HB)
                heads = slice(a * HB, (a + 1) * HB)
                nc.vector.reciprocal(rsums[:, heads], sums[:, heads]).then_inc(rsum_ready, 1)
                dve.wait_ge(rsum_ready, s.count(-lag) * 2 + a + 1)
                nc.vector.tensor_tensor(probs[:, heads, :], probs[:, heads, :],
                                        rsums[:, heads].unsqueeze(2).broadcast_to([P, HB, T]), ALU.mult)\
                    .then_inc(probs_ready, 1)

            def layer_norm2(b, n):
                dve.wait_ge(stats2, b.stop if b.stop < B else B)
                moments(b)
                nc.vector.tensor_scalar(tmp_v[:, b], tmp_v[:, b], LN_EPS, None, ALU.add).then_inc(var2_ready, 1)
                dve.wait_ge(std2_ready, n)
                then(nc.vector.reciprocal(rstd[:, b], tmp_v[:, b]))
                nc.vector.scalar_tensor_tensor(shift[:, b], mean[:, b], -1.0, rstd[:, b], ALU.mult, ALU.mult)\
                    .then_inc(shift_ready, 1)

            def sequence_stats(b):
                nc.vector.bn_stats(bn[:, bass.ds(b, 1), :].rearrange("p a s -> p (a s)"), xs[:, bass.ds(b * E, E)])\
                    .then_inc(stats2, 1)

            def step(s):
                if s.i is None and s.base == 2:
                    dve.wait_ge(std_ready, 2)
                    then(nc.vector.reciprocal(rstd[:, rest], tmp_v[:, rest]))
                if s.has(2):
                    normalise_probs(s, 2, 1)
                more = s.parity == 1 and (s.i is not None or s.base < UNITS - 1)
                if more:
                    normalise(s.seq(0) + 1)
                if s.has(0):
                    dve.wait_ge(qk_projected, s.count(1))
                    if s.i is None and s.base == 0:
                        dve.wait_ge(tables_ready, 4)
                    raw = bank(QK_BANK, 2)
                    if s.at_least(0):
                        dve.wait_ge(rope_done, s.count(0))
                    nc.vector.tensor_tensor(rope_c[:], raw, cos_sb[:].rearrange("p a h d -> p (a h d)"), ALU.mult)
                    nc.vector.tensor_tensor(
                        rope_s[:].rearrange("p (f e) -> p f e", e=2), raw.rearrange("p (f e) -> p f e", e=2)[:, :, ::-1],
                        sin_sb[:].rearrange("p a h (f e) -> p (a h f) e", e=2), ALU.mult).then_inc(rope_parts, 1)
                if s.i is None and s.base == 0:
                    dve.wait_ge(hi_ready, 2)
                    nc.vector.tensor_tensor(wvo_lo, bank(4, 4), wvo_hi.bitcast(F32), ALU.subtract).then_inc(lo_ready, 1)
                    sequences_stats(rest)
                    variances(rest)
                if s.has(1):
                    dve.wait_ge(scored, s.count(0))
                    for a in range(2):
                        sc = bank(S_BANK + a).rearrange("p (h k) -> p h k", k=T)
                        nc.vector.tensor_tensor(sc, sc, mask_f.unsqueeze(1).broadcast_to([P, HB, T]), ALU.add)\
                            .then_inc(masked, 1)
                        dve.wait_ge(masked, s.count(-1) * 2 + a + 1)
                        nc.vector.tensor_reduce(negmax[:, a * HB:(a + 1) * HB],
                                                bank(S_BANK + a).rearrange("p (h k) -> p h k", k=T), AX_X,
                                                ALU.max, negate=True).then_inc(max_ready, 1)
                if s.parity == 0 and s.has(3):
                    dve.wait_ge(residual, s.count(-2))
                    sequence_stats(s.seq(3))
                if more:
                    dve.wait_ge(v_projected, s.count(1))
                    split_xnT(s.seq(0) + 1)
                if s.i is None and s.base == UNITS + 1:
                    layer_norm2(slice(0, B - G), 1)
                if s.has(2):
                    dve.wait_ge(x_biased, s.seq(2) + 1)
                    dve.wait_ge(projected, s.count(-1))
                    xb = xs[:, bass.ds(s.seq(2) * E, E)]
                    if s.at_least(-2):
                        dve.wait_ge(residual, s.count(-2))
                    nc.vector.tensor_tensor(xb, xb, bank(O_BANK)[:, 0:E], ALU.add).then_inc(residual, 1)
                if s.has(1):
                    normalise_probs(s, 1, 0)

            for_slots(dve, step)
            dve.wait_ge(residual, UNITS)
            sequence_stats(B - 1)

            layer_norm2(slice(B - G, B), 2)
            dve.wait_ge(x_consts, 16 * 8)
            N = DK

            def correlate(s):
                if s.has(3):
                    dve.wait_ge(crossed, s.count(-2))
                    xg = xs[:, s.tokens(3)]
                    nc.vector.tensor_tensor(xg, xg, bank(7), ALU.add).then_inc(residual2, 1)
                    dve.wait_ge(residual2, s.count(-2))
                    for n in range(G):
                        b = s.count(-3) * G + n
                        nc.vector.bn_stats(bn[:, bass.ds(b, 1), :].rearrange("p a s -> p (a s)"), xs[:, bass.ds(b * E, E)])\
                            .then_inc(stats3, 1)
                if s.i is None and s.base == GROUPS:
                    half_moments(0)
                if s.has(0):
                    dve.wait_ge(hats_made, s.count(1))
                    dve.wait_ge(khat_ready, s.count(1))
                    if s.at_least(0):
                        dve.wait_ge(spec_turned, s.count(0))
                    q3 = bank(2).rearrange("p (g f) -> p g f", g=G)
                    k3 = khat[:].rearrange("p (g f) -> p g f", g=G)
                    s3 = spec[:].rearrange("p (g f) -> p g f", g=G)
                    re, im = slice(1, N), slice(N + 1, 2 * N)
                    nc.vector.tensor_tensor(spec[:], bank(2), khat[:], ALU.mult).then_inc(spec_step, 1)
                    nc.vector.tensor_tensor(cross_a[:], q3[:, :, im], k3[:, :, re], ALU.mult).then_inc(spec_step, 1)
                    nc.vector.tensor_tensor(cross_b[:], q3[:, :, re], k3[:, :, im], ALU.mult).then_inc(spec_step, 1)
                    dve.wait_ge(spec_step, s.count(0) * 4 + 3)
                    nc.vector.tensor_tensor(s3[:, :, re], s3[:, :, re], s3[:, :, im], ALU.add).then_inc(spec_step, 1)
                    dve.wait_ge(spec_step, s.count(1) * 4)
                    nc.vector.tensor_tensor(s3[:, :, im], cross_a[:], cross_b[:], ALU.subtract).then_inc(spec_ready, 1)
                if s.has(1):
                    dve.wait_ge(corr_made, s.count(0))
                    nc.vector.memset(wait_pad[:], 0.0)
                    for n in range(G):
                        nc.vector.max(top_v[:, n, :], bank(5)[:, n * T:(n + 1) * T]).then_inc(tops, 1)
                    dve.wait_ge(tops, s.count(0) * (2 * G) - G)
                    nc.vector.memset(wait_pad[:], 0.0)
                    for n in range(G):
                        nc.vector.max_index(top_i[:, n, :], top_v[:, n, :], bank(5)[:, n * T:(n + 1) * T]).then_inc(tops, 1)
                    nc.vector.tensor_tensor(top_e[:], top_v[:, :, 0:TOP], top_v[:, :, 0:1].broadcast_to([P, G, TOP]),
                                            ALU.subtract).then_inc(shifted, 1)
                if s.has(1):
                    k = 8
                    dve.wait_ge(tops, s.count(0) * (2 * G))
                    nc.vector.tensor_scalar(lag_n[:], top_i[:, :, 0:TOP], -1.0, head_pos, ALU.mult, ALU.add).then_inc(mixed, 1)
                    dve.wait_ge(mixed, s.count(-1) * k + 1)
                    nc.vector.tensor_scalar(lag_m[:], lag_n[:], DH - 1, None, ALU.bitwise_and).then_inc(mixed, 1)
                    dve.wait_ge(top_exp, s.count(0))
                    nc.vector.tensor_reduce(top_s[:], top_e[:], AX_X, ALU.add).then_inc(mixed, 1)
                    dve.wait_ge(mixed, s.count(-1) * k + 3)
                    nc.vector.reciprocal(top_r[:], top_s[:]).then_inc(mixed, 1)
                    nc.vector.tensor_tensor(
                        onehot[:], lag_m[:].rearrange("p g l -> p (g l)").unsqueeze(2).broadcast_to([P, G * TOP, DH]),
                        iota8.unsqueeze(1).broadcast_to([P, G * TOP, DH]), ALU.is_equal).then_inc(mixed, 1)
                    dve.wait_ge(mixed, s.count(-1) * k + 5)
                    nc.vector.tensor_tensor(top_e[:], top_e[:], top_r[:].unsqueeze(2).broadcast_to([P, G, TOP]), ALU.mult)\
                        .then_inc(mixed, 1)
                    dve.wait_ge(mixed, s.count(-1) * k + 6)
                    nc.vector.tensor_tensor(
                        onehot[:], onehot[:],
                        top_e[:].rearrange("p g l -> p (g l)").unsqueeze(2).broadcast_to([P, G * TOP, DH]), ALU.mult)\
                        .then_inc(mixed, 1)
                    dve.wait_ge(mixed, s.count(-1) * k + 7)
                    nc.vector.tensor_reduce(mix_row[:], onehot[:].rearrange("p (g l) d -> p g d l", g=G), AX_X, ALU.add)\
                        .then_inc(mixed, 1)
                    dve.wait_ge(mixed, s.count(0) * k)
                    if s.at_least(-1):
                        dve.wait_ge(mix_turned, s.count(-1))
                    nc.vector.tensor_tensor(
                        mix[:], mix_row[:].unsqueeze(3).broadcast_to([P, G, DH, H]),
                        same_head[:].rearrange("p (d h) -> p d h", h=H).unsqueeze(1).broadcast_to([P, G, DH, H]), ALU.mult)\
                        .then_inc(mix_ready, 1)

            def half_moments(h):
                b = slice(h * HALF, (h + 1) * HALF)
                dve.wait_ge(stats3, (h + 1) * HALF)
                moments(b)
                then(nc.vector.tensor_scalar(var_e[:, b], tmp_v[:, b], LN_EPS, None, ALU.add))
                then(nc.vector.reciprocal(scale3[:, b], var_e[:, b]))
                then(nc.vector.tensor_tensor(rms[:, b], tmp_v[:, b], scale3[:, b], ALU.mult))
                nc.vector.tensor_scalar(rms[:, b], rms[:, b], RMS_EPS, None, ALU.add).then_inc(ms_ready, 1)
                nc.vector.tensor_copy(tmp_v[:, b], var_e[:, b]).then_inc(var3_ready, 1)

            def scale_tokens(h):
                b = slice(h * HALF, (h + 1) * HALF)
                dve.wait_ge(std3_ready, h + 1)
                dve.wait_ge(rms_ready, h + 1)
                then(nc.vector.tensor_tensor(tmp_v[:, b], tmp_v[:, b], rms[:, b], ALU.mult))
                then(nc.vector.reciprocal(scale3[:, b], tmp_v[:, b]))
                nc.vector.scalar_tensor_tensor(shift3[:, b], mean[:, b], -1.0, scale3[:, b], ALU.mult, ALU.mult)\
                    .then_inc(shift3_ready, 1)
                for g in range(h * HALF_GROUPS, (h + 1) * HALF_GROUPS, 2):
                    for n in range(g * G, (g + 1) * G):
                        nc.vector.tensor_scalar(xr[:, n * E:(n + 1) * E], xs[:, n * E:(n + 1) * E], mean[:, n:n + 1],
                                                scale3[:, n:n + 1], ALU.subtract, ALU.mult).then_inc(xr_even_ready, 1)

            def choose(h):
                b = slice(h * HALF, (h + 1) * HALF)
                wide = [P, HALF, ROUTED]
                g, top, total = gates[:, b], row_max[:, b], row_sum[:, b]
                dve.wait_ge(routed, (h + 1) * HALF)
                logits = bank(L_BANKS[h])[:, 0:HALF * RP].rearrange("p (b n) -> p b n", n=RP)[:, :, 0:ROUTED]
                then(nc.vector.tensor_tensor(g, logits, rms[:, b].unsqueeze(2).broadcast_to(wide), ALU.mult))
                then(nc.vector.tensor_reduce(top, g, AX_X, ALU.max))
                nc.vector.tensor_tensor(g, g, top.unsqueeze(2).broadcast_to(wide), ALU.subtract).then_inc(logits_shifted, 1)
                dve.wait_ge(gates_exp, h + 1)
                then(nc.vector.tensor_reduce(total, g, AX_X, ALU.add))
                then(nc.vector.reciprocal(top, total))
                then(nc.vector.tensor_tensor(g, g, top.unsqueeze(2).broadcast_to(wide), ALU.mult))
                for n in range(h * HALF, (h + 1) * HALF):
                    last = nc.vector.max(best_v[:, n, :], gates[:, n, :])
                then(last)
                for n in range(h * HALF, (h + 1) * HALF):
                    last = nc.vector.max_index(best_i[:, n, :], best_v[:, n, :], gates[:, n, :])
                then(last)
                then(nc.vector.tensor_tensor(total, best_v[:, b, 0], best_v[:, b, 1], ALU.add))
                then(nc.vector.tensor_scalar(total, total, GATE_EPS, None, ALU.add))
                then(nc.vector.reciprocal(top, total))
                then(nc.vector.tensor_tensor(best_n[:, b], best_v[:, b, 0:2], top.unsqueeze(2).broadcast_to([P, HALF, 2]),
                                             ALU.mult))
                for k in range(TOP_K):
                    then(nc.vector.tensor_tensor(picks[k][:, b], best_i[:, b, k:k + 1].broadcast_to(wide),
                                                 iota14.unsqueeze(1).broadcast_to(wide), ALU.is_equal))
                nc.vector.tensor_tensor(chosen[:, b], picks[0][:, b], picks[1][:, b], ALU.add).then_inc(chosen_ready, 1)

            def plan(h):
                b = slice(h * HALF, (h + 1) * HALF)
                dve.wait_ge(ranked, 2 * (h + 1))
                then(nc.vector.tensor_scalar(count_n[:], bank(6)[:, 0:ROUTED], float(P - 1), None, ALU.add))
                then(nc.vector.tensor_scalar(count_m[:], count_n[:], 0xFFFF - (P - 1), None, ALU.bitwise_and))
                then(nc.vector.tensor_tensor(spread_e, count_m[:].unsqueeze(1).broadcast_to([P, ROUTED, ROUTED]),
                                             before_e, ALU.mult))
                then(nc.vector.tensor_reduce(begin[:], spread_e, AX_X, ALU.add))
                then(nc.vector.tensor_tensor(
                    place[:, b], bank(7)[:, 0:HALF * ROUTED].rearrange("p (b e) -> p b e", e=ROUTED),
                    begin[:].unsqueeze(1).broadcast_to([P, HALF, ROUTED]), ALU.add))
                for k in range(TOP_K):
                    then(nc.vector.tensor_tensor(picks[k][:, b], picks[k][:, b], place[:, b], ALU.mult))
                    then(nc.vector.tensor_reduce(dest_f[:, k, b], picks[k][:, b], AX_X, ALU.add))
                nc.vector.tensor_copy(dest[:, :, b], dest_f[:, :, b]).then_inc(dest_ready, 1)
                then(nc.vector.tensor_tensor(end[:], begin[:], count_m[:], ALU.add))
                behind = past[0:1, 0:TILES * ROUTED].rearrange("p (j e) -> p j e", e=ROUTED)
                tiles = tile_e[:, h * TILES:(h + 1) * TILES]
                then(nc.vector.tensor_tensor(behind, end[0:1].unsqueeze(1).broadcast_to([1, TILES, ROUTED]),
                                             tile_start[0:1].unsqueeze(2).broadcast_to([1, TILES, ROUTED]), ALU.is_le))
                then(nc.vector.tensor_reduce(tiles, behind, AX_X, ALU.add))
                then(nc.vector.tensor_scalar(tiles, tiles, float(ROUTED - 1), float(HID), ALU.min, ALU.mult))
                nc.vector.tensor_copy(w_offset[:, LAG + h * TILES:LAG + (h + 1) * TILES], tiles).then_inc(plan_ready, 1)

            def add_shared(g, b):
                xg = xs[:, bass.ds(g * G * E, G * E)]
                dve.wait_ge(shared_made, g + 1)
                nc.vector.tensor_tensor(xg, xg, bank(b), ALU.add).then_inc(shared_added, 1)

            nc.vector.tensor_scalar(before_h[:], mask_f, 0.0, None, ALU.is_lt)
            nc.vector.memset(ones_h[:], 1.0)
            then(nc.vector.memset(w_offset[:], 0))
            for_groups(dve, correlate, {GROUPS + 1: lambda: scale_tokens(0)})
            choose(0)
            half_moments(1)
            add_shared(0, 4)
            plan(0)
            scale_tokens(1)
            add_shared(1, 5)
            choose(1)
            add_shared(2, 4)
            plan(1)
            add_shared(3, 5)

            def tile_slot(s):
                dve.wait_ge(tile_turned, s.count(1))
                src = bank(s.k % 3)
                if s.at_least(-2):
                    dve.wait_ge(tile_multiplied, s.count(-2))
                hi = x_tile_hi[:, s.k % 3, :]
                if s.has(0):
                    nc.vector.tensor_copy(hi, src[:, 0:P]).then_inc(tile_hi, 1)
                if s.has(3):
                    last = nc.vector.tensor_copy(h_tileT[:, s.k % 3, :], src[:, P:P + HID])
                if s.has(0):
                    dve.wait_ge(tile_hi, s.count(1))
                    last = nc.vector.tensor_tensor(x_tile_lo[:, s.k % 3, :], src[:, 0:P], hi.bitcast(F32), ALU.subtract)
                last.then_inc(tile_copied, 1)

            def combine(c, n, k, b, m):
                xb = xs[:, bass.ds(b * E, E)]
                if k == 1:
                    dve.wait_ge(combined, c - G + 1)
                nc.vector.scalar_tensor_tensor(xb, back[:, bass.ds(m * E, E)],
                                               best_n[:].rearrange("p b k -> p (b k)")[:, bass.ds(b * TOP_K + k, 1)],
                                               xb, ALU.mult, ALU.add).then_inc(combined, 1)

            dve.wait_ge(shared_added, EARLY)
            for k in range(TURN):
                tile_slot(Tile(k, 0))
            with dve.Fori(1, FIRST_B + 2) as i:
                for k in range(TURN):
                    tile_slot(Tile(k, i))
            with dve.Fori(FIRST_B + 2, 2 * TURNS) as i:
                c = i - (FIRST_B + 2)
                for k in range(TURN):
                    tile_slot(Tile(k, i))
                    if k < TOP_K * G:
                        if k == 0:
                            dve.wait_ge(gathered_a, 16 * TOP_K * G * (c + 1))
                        combine(c * TOP_K * G + k, k % G, k // G, c * G + k % G, c * TOP_K * G + k)
            for k in range(LAG - 1):
                tile_slot(Tile(k, 2 * TURNS))
            c = CHUNKS - 1
            dve.wait_ge(gathered_a, 16 * TOP_K * HALF)
            for k in range(TOP_K * G):
                combine(c * TOP_K * G + k, k % G, k // G, c * G + k % G, c * TOP_K * G + k)
            for c in range(CHUNKS):
                if c >= EARLY - HALF_GROUPS:
                    add_shared(HALF_GROUPS + c, 4 + c % 2)
                    dve.wait_ge(shared_added, HALF_GROUPS + c + 1)
                dve.wait_ge(gathered_b[c], 16 * TOP_K * G)
                for k in range(TOP_K * G):
                    combine((CHUNKS + c) * TOP_K * G + k, k % G, k // G, HALF + c * G + k % G, c * TOP_K * G + k)

        @block.tensor
        def _(pe):
            def turn(b):
                pe.wait_ge(xn_ready, b + 1)
                nc.tensor.transpose(bank(XN_BANK)[:, 0:T], xn[:], ident).then_inc(xn_turned, 1)

            pe.wait_ge(c_loaded, 16)
            turn(0)

            def fold_vo():
                pe.wait_ge(wv_ready, 1)
                for u in range(2):
                    for n in range(CU):
                        for a in range(2):
                            rows, c = slice(a * DK, (a + 1) * DK), u * CU + n
                            last = nc.tensor.matmul(bank(4 + 2 * u + a)[:, n * E:(n + 1) * E], wv_raw[rows, c, :],
                                                    wo_raw[rows, c, :], start=True, stop=True)
                last.then_inc(vo_folded, 1)

            def project(n, cols, hi, lo):
                nc.tensor.matmul(bank(n), xnT_hi[:], hi[:, cols], start=True, stop=False)
                nc.tensor.matmul(bank(n), xnT_hi[:], lo[:, cols], start=False, stop=False)
                return nc.tensor.matmul(bank(n), xnT_lo[:], hi[:, cols], start=False, stop=True)

            def step(s):
                if s.has(1):
                    pe.wait_ge(rope_done, s.count(0))
                    for n in range(2 * CU):
                        last = nc.tensor.transpose(bank(T_BANK, 2)[:, n * T:(n + 1) * T], qk[:, n * P:(n + 1) * P], ident)
                    last.then_inc(qk_turned, 1)
                if s.has(0):
                    pe.wait_ge(xnT_ready, s.seq(0) + 1)
                    if s.i is None and s.base == 0:
                        pe.wait_ge(lo_ready, 1)
                    if s.at_least(-2):
                        pe.wait_ge(residual, s.count(-2))
                    for a in range(2):
                        last = project(QK_BANK + a, slice(s.parity * FU, (s.parity + 1) * FU),
                                       wqk_hi[:, a], wqk_lo[:, a])
                    last.then_inc(qk_projected, 1)
                if s.i is None and s.base == 0:
                    fold_vo()
                if s.has(1):
                    pe.wait_ge(qkT_ready, s.count(0))
                    if s.at_least(-1):
                        pe.wait_ge(exp_done, s.count(-1) * HPU)
                    for c in range(CU):
                        for a in range(2):
                            rows = slice(a * DK, (a + 1) * DK)
                            last = nc.tensor.matmul(bank(S_BANK + a)[:, c * T:(c + 1) * T], qkT[rows, 0, c, :],
                                                    qkT[rows, 1, c, :], start=True, stop=True)
                    last.then_inc(scored, 1)
                if s.has(2):
                    if s.has(1):
                        pe.wait_ge(qkT_ready, s.count(0))
                    for h in range(HPU):
                        if h % HB == 0:
                            pe.wait_ge(probs_ready, s.count(-2) * 2 + h // HB + 1)
                        last = nc.tensor.transpose(bank(T_BANK, 2)[:, h * T:(h + 1) * T], probs[:, h, :], ident)
                    last.then_inc(probs_turned, 1)
                if s.parity == 1 and (s.i is not None or s.base < UNITS - 1):
                    pe.wait_ge(rope_parts, s.count(1))
                    turn(s.seq(0) + 1)
                if s.has(0):
                    if s.at_least(0):
                        pe.wait_ge(v_ready, s.count(0))
                    else:
                        pe.wait_ge(lo_ready, 2)
                    for a in range(2):
                        last = project(V_BANK + a, slice((2 * s.parity + a) * BANK, (2 * s.parity + a + 1) * BANK),
                                       wvo_hi, wvo_lo)
                    last.then_inc(v_projected, 1)
                if s.has(2):
                    pe.wait_ge(probsT_ready, s.count(-1))
                    pe.wait_ge(v_ready, s.count(-1))
                    if s.has(0):
                        pe.wait_ge(rope_parts, s.count(1))
                    elif s.at_least(-2):
                        pe.wait_ge(residual, s.count(-2))
                    for n in range(HPU):
                        last = nc.tensor.matmul(bank(O_BANK)[:, 0:E], probsT[:, n, :], v[:, s.parity, n * E:(n + 1) * E],
                                                start=(n == 0), stop=(n == HPU - 1))
                    last.then_inc(projected, 1)

            for_slots(pe, step)

            pe.wait_ge(x_consts, 16 * 8)
            pe.wait_ge(residual, UNITS)

            def correlate(s):
                if s.has(0):
                    pe.wait_ge(ctx_a_ready, s.count(1))
                    pe.wait_ge(xn4_ready, s.count(1) * G)
                    if s.at_least(0):
                        pe.wait_ge(freq_ready, s.count(0))
                    for a, src in enumerate((xn4, ctx_a)):
                        for n in range(G):
                            last = nc.tensor.matmul(bank(a)[:, n * T:(n + 1) * T], src[:, n * E:(n + 1) * E], dft_fwd,
                                                    start=True, stop=True)
                    last.then_inc(freq_made, 1)
                if s.has(3):
                    pe.wait_ge(val_o_ready, s.count(-2))
                    pe.wait_ge(mixT_ready, s.count(-2))
                    for n in range(G):
                        last = nc.tensor.matmul(bank(7)[:, n * E:(n + 1) * E], mixT[:, n * T:(n + 1) * T],
                                                val_o[:, n * E:(n + 1) * E], start=True, stop=True)
                    last.then_inc(crossed, 1)
                if s.has(1):
                    pe.wait_ge(spec_ready, s.count(0))
                    if s.has(3):
                        pe.wait_ge(mixT_ready, s.count(-2))
                    for n in range(G):
                        last = nc.tensor.transpose(bank(4)[:, n * T:(n + 1) * T], spec[:, n * T:(n + 1) * T], ident)
                    last.then_inc(spec_turned, 1)
                if s.has(2):
                    pe.wait_ge(ctx_b_ready, s.count(-1))
                    if s.at_least(-2):
                        pe.wait_ge(ctx_o_ready, s.count(-2))
                    for n in range(G):
                        last = nc.tensor.matmul(bank(6)[:, n * E:(n + 1) * E], ctx_b[:, n * E:(n + 1) * E],
                                                xw[:, 3, :], start=True, stop=True)
                    last.then_inc(ctx_o_made, 1)
                if s.has(0):
                    pe.wait_ge(freq_ready, s.count(1))
                    if s.at_least(0):
                        pe.wait_ge(spec_ready, s.count(0))
                    for a in range(2):
                        last = nc.tensor.matmul(bank(2 + a), xw[:, a, :], freq[:, a, :], start=True, stop=True)
                    last.then_inc(hats_made, 1)
                if s.has(2):
                    pe.wait_ge(ctx_o_ready, s.count(-1))
                    if s.at_least(-2):
                        pe.wait_ge(residual2, s.count(-2))
                    nc.tensor.matmul(bank(7), xw[:, 2, :], ctx_o[:], start=True, stop=True).then_inc(val_o_made, 1)
                if s.has(1):
                    pe.wait_ge(specT_ready, s.count(0))
                    if s.at_least(-1):
                        pe.wait_ge(tops, s.count(-1) * (2 * G))
                    for n in range(G):
                        last = nc.tensor.matmul(bank(5)[:, n * T:(n + 1) * T], specT[:, n * T:(n + 1) * T], dft_inv,
                                                start=True, stop=True)
                    last.then_inc(corr_made, 1)
                if s.has(2):
                    pe.wait_ge(mix_ready, s.count(-1))
                    pe.wait_ge(specT_ready, s.count(0) if s.has(1) else GROUPS)
                    for n in range(G):
                        last = nc.tensor.transpose(bank(4)[:, n * T:(n + 1) * T],
                                                   mix[:, n].rearrange("p d h -> p (d h)"), ident)
                    last.then_inc(mix_turned, 1)

            def turn_tokens(h):
                first, end = h * HALF_GROUPS, (h + 1) * HALF_GROUPS
                if h == 1:
                    pe.wait_ge(dest_ready, 1)
                else:
                    pe.wait_ge(tops, GROUPS * (2 * G))
                    pe.wait_ge(freq_ready, GROUPS)
                    pe.wait_ge(e_loaded, 16 * 4)
                for g in range(first, end + 1):
                    if g < end:
                        pe.wait_ge(xr_odd_ready if g % 2 else xr_even_ready, (g // 2 + 1) * G)
                        if g >= first + len(T_BANKS[h]):
                            pe.wait_ge(xrT_ready, g - len(T_BANKS[h]) + 1)
                        for n in range(G):
                            b = g * G + n
                            last = nc.tensor.transpose(bank(T_BANKS[h][g % len(T_BANKS[h])])[:, n * T:(n + 1) * T],
                                                       xr[:, b * E:(b + 1) * E], ident)
                        last.then_inc(xr_turned, 1)
                    if g > first:
                        pe.wait_ge(xrT_ready, g)
                        for b in range((g - 1) * G, g * G):
                            col = (b % HALF) * RP
                            nc.tensor.matmul(bank(L_BANKS[h])[:, col:col + ROUTED], xrT[:, b * T:(b + 1) * T], router_sb[:],
                                             start=True, stop=True).then_inc(routed, 1)

            def rank(h):
                pe.wait_ge(chosen_ready, h + 1)
                if h == 1:
                    pe.wait_ge(xrT_ready, GROUPS)
                rows = bank(7)[:, 0:HALF * ROUTED]
                half = chosen[:, h * HALF:(h + 1) * HALF].rearrange("p b n -> p (b n)")
                nc.tensor.matmul(rows, before_h[:], half, start=True, stop=True)
                for d in range(1, HALF):
                    last = nc.tensor.matmul(rows[:, d * ROUTED:], ones_h[:], half[:, 0:(HALF - d) * ROUTED],
                                            start=False, stop=True, skip_group_check=True)
                last.then_inc(ranked, 1)
                for b in range(HALF):
                    last = nc.tensor.matmul(bank(6)[:, 0:ROUTED], ones_h[:], half[:, b * ROUTED:(b + 1) * ROUTED],
                                            start=(b == 0), stop=(b == HALF - 1))
                last.then_inc(ranked, 1)

            for_groups(pe, correlate)
            turn_tokens(0)
            pe.wait_ge(w1_ready, 2)
            pe.wait_ge(residual2, GROUPS)

            def shared(g, b):
                for m in range(SHARED):
                    for c in range(CH):
                        nc.tensor.matmul(bank(2 * m + c), w1_sb[:, ROUTED + m, c * P:(c + 1) * P],
                                         xrT[:, bass.ds(g * GT, GT)], start=True, stop=True).then_inc(hidden_made, 1)
                for m in range(SHARED):
                    for c in range(CH):
                        pe.wait_ge(hidden_ready, g * (SHARED * CH) + m * CH + c + 1)
                    for t in range(G):
                        for c in range(CH):
                            last = nc.tensor.matmul(bank(b)[:, t * E:(t + 1) * E], hT[:, m, c, t * T:(t + 1) * T],
                                                    w2_sb[:, ROUTED + m, c, :], start=(m == 0 and t == 0 and c == 0),
                                                    stop=(c == CH - 1), skip_group_check=True)
                last.then_inc(shared_made, 1)

            shared(0, 4)
            rank(0)
            pe.wait_ge(logits_shifted, 1)
            shared(1, 5)
            turn_tokens(1)
            pe.wait_ge(shared_added, 1)
            shared(2, 4)
            rank(1)
            pe.wait_ge(shared_added, 2)
            shared(3, 5)

            w2_flat = w2_sb[:].rearrange("p n c e -> p (n c e)")
            registers = [pe.alloc_register(f"w_offset_{k}") for k in range(LAG + TURN - 1)]

            def experts_of(first, count):
                pe.reg_load(registers[0:count], w_offset[0:1, bass.ds(first, count)])
                return [pe.snap(r, min_val=0, max_val=(ROUTED - 1) * HID) for r in registers[0:count]]

            def tile_slot(s, offsets):
                if s.has(0) or s.has(3):
                    if s.at_least(-2):
                        pe.wait_ge(tile_copied, s.count(-2))
                    if s.has(0):
                        if s.k % BATCH == 0:
                            pe.wait_ge(tile_loaded[s.k // BATCH], 16 * (s.turn + 1))
                        last = nc.tensor.transpose(bank(s.k % 3)[:, 0:P], x_tile[:, s.k, :], ident)
                    if s.has(3):
                        pe.wait_ge(tile_activated, s.count(-2))
                        for c in range(CH):
                            last = nc.tensor.transpose(bank(s.k % 3)[:, P + c * P:P + (c + 1) * P],
                                                       h_tile[:, s.k % 3, c * P:(c + 1) * P], ident)
                    last.then_inc(tile_turned, 1)
                if s.at_least(0):
                    pe.wait_ge(tile_copied, s.count(0) if s.has(0) or s.has(1) or s.has(2) or s.has(3) else ALL_TILES + 3)
                    if s.at_least(-3):
                        pe.wait_ge(tile_activated, s.count(-3))
                    if s.has(1):
                        h, r = bank(3 + s.k % 3)[:, 0:HID], (s.k - 1) % 3
                        cols = bass.ds(offsets[s.k + LAG - 1], HID)
                        nc.tensor.matmul(h, x_tile_hi[:, r, :], w1_hi[:, cols], start=True, stop=False)
                        nc.tensor.matmul(h, x_tile_hi[:, r, :], w1_lo[:, cols], start=False, stop=False)
                        last = nc.tensor.matmul(h, x_tile_lo[:, r, :], w1_hi[:, cols], start=False, stop=True)
                    if s.has(LAG):
                        for c in range(CH):
                            last = nc.tensor.matmul(bank(3 + s.k % 3)[:, HID:HID + E],
                                                    h_tileT[:, (s.k - LAG) % 3, c * P:(c + 1) * P],
                                                    w2_flat[:, bass.ds(offsets[s.k] + c * E, E)],
                                                    start=(c == 0), stop=(c == CH - 1), skip_group_check=True)
                    last.then_inc(tile_multiplied, 1)

            pe.wait_ge(plan_ready, 2)
            pe.wait_ge(w1_split, 2)
            pe.wait_ge(shared_added, EARLY)
            offsets = experts_of(0, LAG + TURN - 1)
            for k in range(TURN):
                tile_slot(Tile(k, 0), offsets)
            with pe.Fori(1, 2 * TURNS) as i:
                offsets = experts_of(i * TURN, LAG + TURN - 1)
                for k in range(TURN):
                    tile_slot(Tile(k, i), offsets)
            offsets = experts_of(ALL_TILES, LAG)
            for k in range(LAG):
                tile_slot(Tile(k, 2 * TURNS), offsets)
            pe.wait_ge(tile_copied, ALL_TILES + LAG - 1)
            pe.wait_ge(tile_activated, ALL_TILES + LAG - 1)
            for g in range(EARLY, GROUPS):
                if g >= EARLY + 2:
                    pe.wait_ge(shared_added, g - 1)
                shared(g, 4 + g % 2)


def _tables(np):
    f = np.float32
    ident = np.eye(P, dtype=f)
    mask = np.triu(np.full((P, P), MASKED, dtype=f), k=1)
    theta = (f(10000.0) ** (np.arange(0, DK, 2, dtype=f) / f(DK))).astype(f)
    freqs = np.arange(T, dtype=f)[:, None] * (f(1.0) / theta)[None, :]
    emb = np.concatenate([freqs, freqs], axis=-1)
    cos, sin = np.cos(emb).astype(f), np.sin(emb).astype(f)
    sin[:, 0::2] = -sin[:, 0::2]
    q_scale = f(DK ** -0.5)
    t = np.arange(T)
    k_re, k_im = np.arange(T // 2 + 1), np.arange(1, T // 2)
    turn = 2.0 * np.pi / T
    fwd = np.concatenate([np.cos(turn * (np.outer(t, k_re) % T)), -np.sin(turn * (np.outer(t, k_im) % T))], axis=1)
    weight = np.full(T, 2.0 / T)
    weight[0] = weight[T // 2] = 1.0 / T
    inv = fwd.T * weight[:, None]
    row = np.arange(P)
    same = (row[:, None] % H == row[None, :] % H)
    pos = np.zeros((P, P))
    pos[:, 0] = row // H + T
    pos[:, 1:1 + DH] = np.arange(DH)
    pos[:, 1 + RP:1 + RP + ROUTED] = np.arange(ROUTED)
    plan = np.zeros((P, 2 * P))
    plan[:, 0:ROUTED * ROUTED] = np.tril(np.ones((ROUTED, ROUTED)), k=-1).reshape(-1)
    plan[:, ROUTED * ROUTED:ROUTED * ROUTED + TILES] = np.arange(TILES) * P
    return np.concatenate([ident, mask, cos * q_scale, cos, sin * q_scale, sin, fwd, inv, same, pos, plan],
                          axis=1).astype(f)


def kernel(**inputs):
    import numpy as np
    import concourse.bacc as bacc
    from concourse.bass_utils import run_bass_kernel_spmd

    layout = {k: np.ascontiguousarray(v) for k, v in inputs.items()}
    for k in ("L0_attn_wq", "L0_attn_wk", "L0_attn_wo"):
        layout[k] = np.ascontiguousarray(layout[k].T)
    for k in ("L0_xattn_wq", "L0_xattn_wk", "L0_xattn_wv"):
        layout[k] = np.ascontiguousarray(layout[k].reshape(E, H, DH).transpose(0, 2, 1).reshape(E, E))
    layout["consts"] = _tables(np)
    for name, routed, shared in (("rms", "L0_ffn_rms_w", "L0_ffn_rms_w_s"), ("w1", "L0_ffn_w1", "L0_ffn_w1_s"),
                                 ("w2", "L0_ffn_w2", "L0_ffn_w2_s")):
        layout[name] = np.concatenate([layout[routed], layout[shared]], axis=0)
    nc = bacc.Bacc("TRN2", target_bir_lowering=False, num_devices=1)
    names = ["x", "ctx_1024", "L0_attn_wq", "L0_attn_wk", "L0_attn_wv", "L0_attn_wo",
             "L0_attn_bq", "L0_attn_bk", "L0_attn_bv", "L0_attn_bo", "L0_xattn_wq", "L0_xattn_wk", "L0_xattn_wv", "L0_xattn_wo",
             "L0_ffn_router_w", "rms", "w1", "w2", "consts"]
    arrays, args = {}, []
    for name in names:
        a = layout[name]
        arrays[f"in_{name}"] = a
        args.append(nc.dram_tensor(f"in_{name}", a.shape, mybir.dt.from_np(a.dtype), kind="ExternalInput").ap())
    out = nc.dram_tensor("out_x", (B, T, E), F32, kind="ExternalOutput").ap()
    decoder_layer(nc, *args, out)
    r = run_bass_kernel_spmd(nc, [arrays], core_ids=[0])
    return r.results[0]["out_x"]
```
